# Optimizing a Trainium2 kernel written in Bass

```python
import numpy as np
import jax
import jax.numpy as jnp

def _softmax(x, axis=-1):
    return jax.nn.softmax(x, axis=axis)

def _gelu(x):
    return jax.nn.gelu(x, approximate=True)

def _silu(x):
    return jax.nn.silu(x)

def _sigmoid(x):
    return jax.nn.sigmoid(x)

def _layernorm(x, axis=-1, eps=1e-05):
    m = jnp.mean(x, axis=axis, keepdims=True)
    v = jnp.var(x, axis=axis, keepdims=True)
    return (x - m) / jnp.sqrt(v + eps)

def _scatter_add(tgt, idx, src, axis=0):
    return tgt.at[idx].add(src)

def _segment_sum(src, seg, n):
    return jax.ops.segment_sum(src, seg, n)
kernel_name = 'mk_recurrent_d2_jaxref_r4_83577a'

def setup_inputs(seed: int=0):
    np.random.seed(seed)
    _w = jnp.asarray

    def _L0_attn_setup():
        import jax, jax.numpy as jnp
        import numpy as np
        from jax import lax
        H = 4
        CHUNK = 64
        EPS = 1e-05

        def _rope(t, cos, sin):
            t1, t2 = jnp.split(t, 2, axis=-1)
            c = cos[None, :, None, :]
            s = sin[None, :, None, :]
            return jnp.concatenate([t1 * c - t2 * s, t2 * c + t1 * s], axis=-1)
        key = jax.random.key(seed)
        ks = jax.random.split(key, 8)
        B, T, D = (4, 1024, 256)
        s = lambda fan: 1.0 / np.sqrt(fan)
        return {'x': jax.random.normal(ks[0], (B, T, D), jnp.float32), 'ln_w': jnp.ones((D,), jnp.float32), 'ln_b': jnp.zeros((D,), jnp.float32), 'Wq': jax.random.normal(ks[1], (D, D), jnp.float32) * s(D), 'Wk': jax.random.normal(ks[2], (D, D), jnp.float32) * s(D), 'Wv': jax.random.normal(ks[3], (D, 2 * D), jnp.float32) * s(D), 'Wg': jax.random.normal(ks[4], (D, 2 * D), jnp.float32) * s(D), 'g_norm_w': jnp.ones((2 * D // H,), jnp.float32), 'Wo': jax.random.normal(ks[5], (2 * D, D), jnp.float32) * s(2 * D)}
    _L0_attn_in = _L0_attn_setup()

    def _L0_ffn_setup():
        import jax, jax.numpy as jnp
        import numpy as np
        DIM = 256
        DEPTH = 2
        HEADS = 8
        DIM_HEAD = 64
        WINDOW = 128
        INNER = HEADS * DIM_HEAD
        HID = int(DIM * 4 * 2 / 3)
        B, N = (2, 2048)
        QK_SCALE = 8.0

        def shift_token(t):
            t1, t2 = jnp.split(t, 2, axis=-1)
            t2 = jnp.pad(t2, ((0, 0), (1, 0), (0, 0)))[:, :-1]
            return jnp.concatenate([t1, t2], axis=-1)

        def l2norm(t):
            return t / jnp.clip(jnp.linalg.norm(t, axis=-1, keepdims=True), 1e-12)

        def rotate_half(x):
            x1, x2 = jnp.split(x, 2, axis=-1)
            return jnp.concatenate([-x2, x1], axis=-1)

        def rotary_xpos(q, k):
            n = q.shape[-2]
            half_idx = jnp.arange(0, DIM_HEAD, 2, dtype=jnp.float32)
            inv_freq = 1.0 / 10000.0 ** (half_idx / DIM_HEAD)
            t = jnp.arange(n, dtype=jnp.float32)
            freqs = t[:, None] * inv_freq[None, :]
            freqs = jnp.concatenate([freqs, freqs], axis=-1)
            base = (half_idx + 0.4 * DIM_HEAD) / (1.4 * DIM_HEAD)
            power = (t - n // 2) / float(WINDOW // 2)
            scale = base[None, :] ** power[:, None]
            scale = jnp.concatenate([scale, scale], axis=-1)
            cos, sin = (jnp.cos(freqs), jnp.sin(freqs))
            q = q * cos * scale + rotate_half(q) * sin * scale
            k = k * cos / scale + rotate_half(k) * sin / scale
            return (q, k)

        def local_attention(q, k, v):
            b, h, n, d = q.shape
            w = n // WINDOW
            bq = q.reshape(b, h, w, WINDOW, d) * QK_SCALE
            bk = k.reshape(b, h, w, WINDOW, d)
            bv = v.reshape(b, h, w, WINDOW, d)

            def look_around(t):
                p = jnp.pad(t, ((0, 0), (0, 0), (1, 0), (0, 0), (0, 0)))
                return jnp.concatenate([p[:, :, :w], p[:, :, 1:]], axis=3)
            bk, bv = (look_around(bk), look_around(bv))
            bt = jnp.arange(n).reshape(w, WINDOW)
            btp = jnp.pad(bt, ((1, 0), (0, 0)), constant_values=-1)
            btk = jnp.concatenate([btp[:w], btp[1:]], axis=1)
            sim = jnp.einsum('bhwid,bhwjd->bhwij', bq, bk)
            i = bt[:, :, None]
            j = btk[:, None, :]
            mask = (i < j) | (i > j + WINDOW) | (j == -1)
            sim = jnp.where(mask, -jnp.finfo(sim.dtype).max, sim)
            attn = jax.nn.softmax(sim, axis=-1)
            out = jnp.einsum('bhwij,bhwjd->bhwid', attn, bv)
            return out.reshape(b, h, n, d)

        def _layer(x, wqkv, qs, ksc, wo, lg, lb, w1, b1, w2, b2):
            b, n, _ = x.shape
            h = shift_token(x)
            qkv = h @ wqkv
            q, k, v = jnp.split(qkv, 3, axis=-1)
            to_heads = lambda t: t.reshape(b, n, HEADS, DIM_HEAD).transpose(0, 2, 1, 3)
            q, k, v = (to_heads(q), to_heads(k), to_heads(v))
            q = l2norm(q) * qs
            k = l2norm(k) * ksc
            q, k = rotary_xpos(q, k)
            o = local_attention(q, k, v)
            o = o.transpose(0, 2, 1, 3).reshape(b, n, INNER)
            x = x + o @ wo
            h = shift_token(x)
            mu = h.mean(-1, keepdims=True)
            var = h.var(-1, keepdims=True)
            h = (h - mu) / jnp.sqrt(var + 1e-05) * lg + lb
            h = h @ w1 + b1
            a, g = jnp.split(h, 2, axis=-1)
            h = a * jax.nn.gelu(g, approximate=False)
            x = x + h @ w2 + b2
            return x
        key = jax.random.key(seed)
        ks = jax.random.split(key, 6)
        return {'x': jax.random.normal(ks[0], (B, N, DIM), jnp.float32), 'wqkv': jax.random.normal(ks[1], (DEPTH, DIM, 3 * INNER), jnp.float32) * 0.02, 'q_scale': jnp.ones((DEPTH, DIM_HEAD), jnp.float32), 'k_scale': jnp.ones((DEPTH, DIM_HEAD), jnp.float32), 'wo': jax.random.normal(ks[2], (DEPTH, INNER, DIM), jnp.float32) * 0.02, 'ln_g': jnp.ones((DEPTH, DIM), jnp.float32), 'ln_b': jnp.zeros((DEPTH, DIM), jnp.float32), 'w1': jax.random.normal(ks[3], (DEPTH, DIM, 2 * HID), jnp.float32) * 0.02, 'b1': jnp.zeros((DEPTH, 2 * HID), jnp.float32), 'w2': jax.random.normal(ks[4], (DEPTH, HID, DIM), jnp.float32) * 0.02, 'b2': jnp.zeros((DEPTH, DIM), jnp.float32)}
    _L0_ffn_in = _L0_ffn_setup()

    def _L1_attn_setup():
        import jax, jax.numpy as jnp
        import numpy as np
        D_MODEL, N_HEADS = (256, 16)
        D_H = D_MODEL // N_HEADS
        D_HR = D_H // 2
        D_LATENT = 64
        THETA = 10000.0

        def rope(x, theta=THETA):
            S, d = (x.shape[-2], x.shape[-1])
            inv = theta ** (-jnp.arange(0, d, 2, dtype=jnp.float32) / d)
            ang = jnp.arange(S, dtype=jnp.float32)[:, None] * inv
            cos, sin = (jnp.cos(ang), jnp.sin(ang))
            x1, x2 = (x[..., 0::2], x[..., 1::2])
            r1 = x1 * cos - x2 * sin
            r2 = x1 * sin + x2 * cos
            return jnp.stack([r1, r2], axis=-1).reshape(x.shape)
        key = jax.random.key(seed)
        ks = jax.random.split(key, 9)
        s = lambda fan_in: 1.0 / np.sqrt(fan_in)
        return {'x': jax.random.normal(ks[0], (4, 512, D_MODEL), jnp.float32), 'W_DQ': jax.random.normal(ks[1], (D_MODEL, D_LATENT), jnp.float32) * s(D_MODEL), 'W_UQ': jax.random.normal(ks[2], (D_LATENT, N_HEADS * D_H), jnp.float32) * s(D_LATENT), 'W_QR': jax.random.normal(ks[3], (D_LATENT, N_HEADS * D_HR), jnp.float32) * s(D_LATENT), 'W_DKV': jax.random.normal(ks[4], (D_MODEL, D_LATENT), jnp.float32) * s(D_MODEL), 'W_UK': jax.random.normal(ks[5], (D_LATENT, N_HEADS * D_H), jnp.float32) * s(D_LATENT), 'W_UV': jax.random.normal(ks[6], (D_LATENT, N_HEADS * D_H), jnp.float32) * s(D_LATENT), 'W_KR': jax.random.normal(ks[7], (D_MODEL, D_HR), jnp.float32) * s(D_MODEL), 'W_O': jax.random.normal(ks[8], (N_HEADS * D_H, D_MODEL), jnp.float32) * s(N_HEADS * D_H)}
    _L1_attn_in = _L1_attn_setup()

    def _L1_ffn_setup():
        import jax, jax.numpy as jnp
        import numpy as np
        TOP_K = 2
        key = jax.random.key(seed)
        k0, k1, k2, k3 = jax.random.split(key, 4)
        B, T, C, E, F = (4, 512, 256, 8, 1024)
        x = jax.random.normal(k0, (B, T, C), dtype=jnp.float32)
        gate_w = jax.random.normal(k1, (C, E), dtype=jnp.float32) * 0.02
        w1 = jax.random.normal(k2, (E, C, F), dtype=jnp.float32) * 0.02
        w2 = jax.random.normal(k3, (E, F, C), dtype=jnp.float32) * 0.02
        return {'x': x, 'gate_w': gate_w, 'w1': w1, 'w2': w2}
    _L1_ffn_in = _L1_ffn_setup()
    _d = {'L0_attn_x': _L0_attn_in['x'], 'L0_attn_ln_w': _L0_attn_in['ln_w'], 'L0_attn_ln_b': _L0_attn_in['ln_b'], 'L0_attn_Wq': _L0_attn_in['Wq'], 'L0_attn_Wk': _L0_attn_in['Wk'], 'L0_attn_Wv': _L0_attn_in['Wv'], 'L0_attn_Wg': _L0_attn_in['Wg'], 'L0_attn_g_norm_w': _L0_attn_in['g_norm_w'], 'L0_attn_Wo': _L0_attn_in['Wo'], 'L0_ffn_wqkv': _L0_ffn_in['wqkv'], 'L0_ffn_q_scale': _L0_ffn_in['q_scale'], 'L0_ffn_k_scale': _L0_ffn_in['k_scale'], 'L0_ffn_wo': _L0_ffn_in['wo'], 'L0_ffn_ln_g': _L0_ffn_in['ln_g'], 'L0_ffn_ln_b': _L0_ffn_in['ln_b'], 'L0_ffn_w1': _L0_ffn_in['w1'], 'L0_ffn_b1': _L0_ffn_in['b1'], 'L0_ffn_w2': _L0_ffn_in['w2'], 'L0_ffn_b2': _L0_ffn_in['b2'], 'L1_attn_W_DQ': _L1_attn_in['W_DQ'], 'L1_attn_W_UQ': _L1_attn_in['W_UQ'], 'L1_attn_W_QR': _L1_attn_in['W_QR'], 'L1_attn_W_DKV': _L1_attn_in['W_DKV'], 'L1_attn_W_UK': _L1_attn_in['W_UK'], 'L1_attn_W_UV': _L1_attn_in['W_UV'], 'L1_attn_W_KR': _L1_attn_in['W_KR'], 'L1_attn_W_O': _L1_attn_in['W_O'], 'L1_ffn_gate_w': _L1_ffn_in['gate_w'], 'L1_ffn_w1': _L1_ffn_in['w1'], 'L1_ffn_w2': _L1_ffn_in['w2']}
    _x0 = _d['L0_attn_x']
    _d['L0_attn_x'] = jax.random.normal(jax.random.fold_in(jax.random.key(seed), 1), (8, 512, 256), dtype=_x0.dtype)
    del _x0
    return _d

def reference(L0_attn_x, L0_attn_ln_w, L0_attn_ln_b, L0_attn_Wq, L0_attn_Wk, L0_attn_Wv, L0_attn_Wg, L0_attn_g_norm_w, L0_attn_Wo, L0_ffn_wqkv, L0_ffn_q_scale, L0_ffn_k_scale, L0_ffn_wo, L0_ffn_ln_g, L0_ffn_ln_b, L0_ffn_w1, L0_ffn_b1, L0_ffn_w2, L0_ffn_b2, L1_attn_W_DQ, L1_attn_W_UQ, L1_attn_W_QR, L1_attn_W_DKV, L1_attn_W_UK, L1_attn_W_UV, L1_attn_W_KR, L1_attn_W_O, L1_ffn_gate_w, L1_ffn_w1, L1_ffn_w2):

    def _L0_attn_ref(x, ln_w, ln_b, Wq, Wk, Wv, Wg, g_norm_w, Wo):
        import jax, jax.numpy as jnp
        import numpy as np
        from jax import lax
        H = 4
        CHUNK = 64
        EPS = 1e-05

        def _rope(t, cos, sin):
            t1, t2 = jnp.split(t, 2, axis=-1)
            c = cos[None, :, None, :]
            s = sin[None, :, None, :]
            return jnp.concatenate([t1 * c - t2 * s, t2 * c + t1 * s], axis=-1)
        B, T, D = x.shape
        dk, dv = (D // H, 2 * D // H)
        C = CHUNK
        N = T // C
        mu = x.mean(-1, keepdims=True)
        var = ((x - mu) ** 2).mean(-1, keepdims=True)
        normed = (x - mu) * lax.rsqrt(var + EPS) * ln_w + ln_b
        q = (normed @ Wq).reshape(B, T, H, dk)
        k = (normed @ Wk).reshape(B, T, H, dk)
        v = (normed @ Wv).reshape(B, T, H, dv)
        g = (normed @ Wg).reshape(B, T, H, dv)
        inv_freq = 1.0 / 10000.0 ** (jnp.arange(0, dk, 2, dtype=jnp.float32) / dk)
        freqs = jnp.arange(T, dtype=jnp.float32)[:, None] * inv_freq[None, :]
        cos, sin = (jnp.cos(freqs), jnp.sin(freqs))
        q = _rope(q, cos, sin) * dk ** (-0.5)
        k = _rope(k, cos, sin)
        gamma = 1.0 - jnp.exp2(-5.0 - jnp.arange(H, dtype=jnp.float32))
        i = jnp.arange(C, dtype=jnp.float32)
        Dmask = jnp.where(i[:, None] >= i[None, :], gamma[:, None, None] ** (i[:, None] - i[None, :]), 0.0)
        cross = gamma[:, None] ** (i + 1.0)
        kdec = gamma[:, None] ** (C - 1.0 - i)
        gC = gamma ** C
        to_chunks = lambda t, d: t.reshape(B, N, C, H, d).transpose(1, 0, 3, 2, 4)
        qc, kc, vc = (to_chunks(q, dk), to_chunks(k, dk), to_chunks(v, dv))

        def step(S, inp):
            qn, kn, vn = inp
            attn = jnp.einsum('bhid,bhjd->bhij', qn, kn) * Dmask
            o = jnp.einsum('bhij,bhjv->bhiv', attn, vn) + jnp.einsum('bhid,bhdv->bhiv', qn * cross[None, :, :, None], S)
            S = S * gC[None, :, None, None] + jnp.einsum('bhid,bhiv->bhdv', kn * kdec[None, :, :, None], vn)
            return (S, o)
        S0 = jnp.zeros((B, H, dk, dv), x.dtype)
        _, o = lax.scan(step, S0, (qc, kc, vc))
        o = o.transpose(1, 0, 3, 2, 4).reshape(B, T, H, dv)
        o = o * lax.rsqrt((o ** 2).mean(-1, keepdims=True) + EPS) * g_norm_w
        o = o * (g * jax.nn.sigmoid(g))
        out = o.reshape(B, T, 2 * D) @ Wo
        return x + out

    def _L0_ffn_ref(x, wqkv, q_scale, k_scale, wo, ln_g, ln_b, w1, b1, w2, b2):
        import jax, jax.numpy as jnp
        import numpy as np
        DIM = 256
        DEPTH = 2
        HEADS = 8
        DIM_HEAD = 64
        WINDOW = 128
        INNER = HEADS * DIM_HEAD
        HID = int(DIM * 4 * 2 / 3)
        B, N = (2, 2048)
        QK_SCALE = 8.0

        def shift_token(t):
            t1, t2 = jnp.split(t, 2, axis=-1)
            t2 = jnp.pad(t2, ((0, 0), (1, 0), (0, 0)))[:, :-1]
            return jnp.concatenate([t1, t2], axis=-1)

        def l2norm(t):
            return t / jnp.clip(jnp.linalg.norm(t, axis=-1, keepdims=True), 1e-12)

        def rotate_half(x):
            x1, x2 = jnp.split(x, 2, axis=-1)
            return jnp.concatenate([-x2, x1], axis=-1)

        def rotary_xpos(q, k):
            n = q.shape[-2]
            half_idx = jnp.arange(0, DIM_HEAD, 2, dtype=jnp.float32)
            inv_freq = 1.0 / 10000.0 ** (half_idx / DIM_HEAD)
            t = jnp.arange(n, dtype=jnp.float32)
            freqs = t[:, None] * inv_freq[None, :]
            freqs = jnp.concatenate([freqs, freqs], axis=-1)
            base = (half_idx + 0.4 * DIM_HEAD) / (1.4 * DIM_HEAD)
            power = (t - n // 2) / float(WINDOW // 2)
            scale = base[None, :] ** power[:, None]
            scale = jnp.concatenate([scale, scale], axis=-1)
            cos, sin = (jnp.cos(freqs), jnp.sin(freqs))
            q = q * cos * scale + rotate_half(q) * sin * scale
            k = k * cos / scale + rotate_half(k) * sin / scale
            return (q, k)

        def local_attention(q, k, v):
            b, h, n, d = q.shape
            w = n // WINDOW
            bq = q.reshape(b, h, w, WINDOW, d) * QK_SCALE
            bk = k.reshape(b, h, w, WINDOW, d)
            bv = v.reshape(b, h, w, WINDOW, d)

            def look_around(t):
                p = jnp.pad(t, ((0, 0), (0, 0), (1, 0), (0, 0), (0, 0)))
                return jnp.concatenate([p[:, :, :w], p[:, :, 1:]], axis=3)
            bk, bv = (look_around(bk), look_around(bv))
            bt = jnp.arange(n).reshape(w, WINDOW)
            btp = jnp.pad(bt, ((1, 0), (0, 0)), constant_values=-1)
            btk = jnp.concatenate([btp[:w], btp[1:]], axis=1)
            sim = jnp.einsum('bhwid,bhwjd->bhwij', bq, bk)
            i = bt[:, :, None]
            j = btk[:, None, :]
            mask = (i < j) | (i > j + WINDOW) | (j == -1)
            sim = jnp.where(mask, -jnp.finfo(sim.dtype).max, sim)
            attn = jax.nn.softmax(sim, axis=-1)
            out = jnp.einsum('bhwij,bhwjd->bhwid', attn, bv)
            return out.reshape(b, h, n, d)

        def _layer(x, wqkv, qs, ksc, wo, lg, lb, w1, b1, w2, b2):
            b, n, _ = x.shape
            h = shift_token(x)
            qkv = h @ wqkv
            q, k, v = jnp.split(qkv, 3, axis=-1)
            to_heads = lambda t: t.reshape(b, n, HEADS, DIM_HEAD).transpose(0, 2, 1, 3)
            q, k, v = (to_heads(q), to_heads(k), to_heads(v))
            q = l2norm(q) * qs
            k = l2norm(k) * ksc
            q, k = rotary_xpos(q, k)
            o = local_attention(q, k, v)
            o = o.transpose(0, 2, 1, 3).reshape(b, n, INNER)
            x = x + o @ wo
            h = shift_token(x)
            mu = h.mean(-1, keepdims=True)
            var = h.var(-1, keepdims=True)
            h = (h - mu) / jnp.sqrt(var + 1e-05) * lg + lb
            h = h @ w1 + b1
            a, g = jnp.split(h, 2, axis=-1)
            h = a * jax.nn.gelu(g, approximate=False)
            x = x + h @ w2 + b2
            return x
        for l in range(DEPTH):
            x = _layer(x, wqkv[l], q_scale[l], k_scale[l], wo[l], ln_g[l], ln_b[l], w1[l], b1[l], w2[l], b2[l])
        return x

    def _L1_attn_ref(x, W_DQ, W_UQ, W_QR, W_DKV, W_UK, W_UV, W_KR, W_O):
        import jax, jax.numpy as jnp
        import numpy as np
        D_MODEL, N_HEADS = (256, 16)
        D_H = D_MODEL // N_HEADS
        D_HR = D_H // 2
        D_LATENT = 64
        THETA = 10000.0

        def rope(x, theta=THETA):
            S, d = (x.shape[-2], x.shape[-1])
            inv = theta ** (-jnp.arange(0, d, 2, dtype=jnp.float32) / d)
            ang = jnp.arange(S, dtype=jnp.float32)[:, None] * inv
            cos, sin = (jnp.cos(ang), jnp.sin(ang))
            x1, x2 = (x[..., 0::2], x[..., 1::2])
            r1 = x1 * cos - x2 * sin
            r2 = x1 * sin + x2 * cos
            return jnp.stack([r1, r2], axis=-1).reshape(x.shape)
        B, S, _ = x.shape
        d_qk = D_H + D_HR
        c_q = x @ W_DQ
        Qc = (c_q @ W_UQ).reshape(B, S, N_HEADS, D_H).transpose(0, 2, 1, 3)
        Qr = (c_q @ W_QR).reshape(B, S, N_HEADS, D_HR).transpose(0, 2, 1, 3)
        Qr = rope(Qr)
        c_kv = x @ W_DKV
        Kc = (c_kv @ W_UK).reshape(B, S, N_HEADS, D_H).transpose(0, 2, 1, 3)
        Kr = rope((x @ W_KR)[:, None, :, :])
        Kr = jnp.broadcast_to(Kr, (B, N_HEADS, S, D_HR))
        V = (c_kv @ W_UV).reshape(B, S, N_HEADS, D_H).transpose(0, 2, 1, 3)
        Q = jnp.concatenate([Qc, Qr], axis=-1)
        K = jnp.concatenate([Kc, Kr], axis=-1)
        scores = jnp.einsum('bhqd,bhkd->bhqk', Q, K)
        scores = jnp.clip(scores, -80.0, 80.0)
        causal = jnp.tril(jnp.ones((S, S), dtype=bool))
        scores = jnp.where(causal, scores, -jnp.inf)
        weights = jax.nn.softmax(scores / jnp.sqrt(jnp.float32(d_qk)), axis=-1)
        attn = jnp.einsum('bhqk,bhkd->bhqd', weights, V)
        attn = attn.transpose(0, 2, 1, 3).reshape(B, S, N_HEADS * D_H)
        return attn @ W_O

    def _L1_ffn_ref(x, gate_w, w1, w2):
        import jax, jax.numpy as jnp
        import numpy as np
        TOP_K = 2
        E = gate_w.shape[-1]
        probs = jax.nn.softmax(x @ gate_w, axis=-1)
        topw, topi = jax.lax.top_k(probs, TOP_K)
        topw = topw / topw.sum(axis=-1, keepdims=True)
        combine = (jax.nn.one_hot(topi, E, dtype=x.dtype) * topw[..., None]).sum(axis=-2)

        def body(acc, params):
            w1_i, w2_i, cw = params
            h = jax.nn.gelu(x @ w1_i, approximate=False)
            return (acc + cw[..., None] * (h @ w2_i), None)
        acc0 = jnp.zeros_like(x)
        out, _ = jax.lax.scan(body, acc0, (w1, w2, jnp.moveaxis(combine, -1, 0)))
        return out
    x = L0_attn_x
    xn = _layernorm(x, axis=-1)
    s = _L0_attn_ref(xn, L0_attn_ln_w, L0_attn_ln_b, L0_attn_Wq, L0_attn_Wk, L0_attn_Wv, L0_attn_Wg, L0_attn_g_norm_w, L0_attn_Wo)
    g = _silu(_L0_ffn_ref(xn, L0_ffn_wqkv, L0_ffn_q_scale, L0_ffn_k_scale, L0_ffn_wo, L0_ffn_ln_g, L0_ffn_ln_b, L0_ffn_w1, L0_ffn_b1, L0_ffn_w2, L0_ffn_b2))
    x = x + s * g
    xn = _layernorm(x, axis=-1)
    s = _L1_attn_ref(xn, L1_attn_W_DQ, L1_attn_W_UQ, L1_attn_W_QR, L1_attn_W_DKV, L1_attn_W_UK, L1_attn_W_UV, L1_attn_W_KR, L1_attn_W_O)
    g = _silu(_L1_ffn_ref(xn, L1_ffn_gate_w, L1_ffn_w1, L1_ffn_w2))
    x = x + s * g
    return x

_drawn_inputs = setup_inputs


def setup_inputs(seed=0):
    import zlib

    import numpy as np

    out = dict(_drawn_inputs(seed))
    spreads = {'L0_attn_ln_w': (1.0, 0.2),
     'L0_attn_ln_b': (0.0, 0.1),
     'L0_attn_g_norm_w': (1.0, 0.2),
     'L0_ffn_q_scale': (1.0, 0.6),
     'L0_ffn_k_scale': (1.0, 0.6),
     'L0_ffn_ln_g': (1.0, 0.6),
     'L0_ffn_ln_b': (0.0, 0.8),
     'L0_ffn_b1': (0.0, 0.8),
     'L0_ffn_b2': (0.0, 0.1)}
    factors = {'L0_ffn_wqkv': 3.435,
     'L0_ffn_wo': 3.377,
     'L1_attn_W_DQ': 8.0,
     'L1_attn_W_UQ': 8.0,
     'L1_attn_W_QR': 8.0,
     'L1_attn_W_DKV': 8.0,
     'L1_attn_W_UK': 8.0,
     'L1_attn_W_UV': 8.0,
     'L1_attn_W_KR': 8.0,
     'L1_attn_W_O': 8.0,
     'L1_ffn_gate_w': 8.0,
     'L1_ffn_w1': 8.0,
     'L1_ffn_w2': 8.0}
    for name, (base, spread) in spreads.items():
        noise = np.random.default_rng([zlib.crc32(name.encode()), seed]).standard_normal(out[name].shape)
        drawn = base * np.exp(spread * noise) if base else spread * noise
        out[name] = jnp.asarray(drawn.astype(out[name].dtype))
    for name, factor in factors.items():
        out[name] = (out[name] * factor).astype(out[name].dtype)
    return out
```

```python
import concourse.bass as bass
from concourse import mybir
from contextlib import ExitStack
import numpy as np

F32 = mybir.dt.float32
BF16 = mybir.dt.bfloat16
ALU = mybir.AluOpType
ACT = mybir.ActivationFunctionType
AX = mybir.AxisListType

P = 128
B, T, D = 8, 512, 256
NT = T // P
DC = D // P
EPS = 1e-5
RH, RDK, RDV = 4, 64, 128
RV = RH * RDV
DEPTH, HEADS, DH, WINDOW = 2, 8, 64, 128
INNER = HEADS * DH
HID = 682
HCH = 120
NHC = 6
HSZ = [min(HCH, HID - HCH * c) for c in range(NHC)]
LH, LDH, LDR, LAT = 16, 16, 8, 64
LG = 4
SQ24 = float(np.sqrt(np.float32(LDH + LDR)))
E, F = 8, 1024
FC = F // P


def act_jobs(l):
    if l == 0:
        j = [("xT", t) for t in range(NT)] + [("zaT", t) for t in range(NT)]
    else:
        j = [("curT", t) for t in range(NT)]
    j += [("v", t) for t in range(NT)]
    for t in range(NT):
        j += [("rv", t)] if l == 0 else []
        j += [("qkT", t)]
    if l == 0:
        j += [("rg", t) for t in range(NT)]
    j += [("S", u) for u in range(2 * NT)]
    if l == 0:
        j += [("rT", t) for t in range(NT)]
        j += [("roT", t) for t in range(NT)]
    j += [("zT", t) for t in range(NT)]
    j += [("g", c) for c in range(NHC)]
    if l == 1:
        j += [("x1T", t) for t in range(NT)]
        j += [("lv", t) for t in range(NT)]
        j += [("av", g) for g in range(LG)]
        j += [("attnT", t) for t in range(NT)]
    return j


def dve_jobs(l):
    j = [("qk", t) for t in range(NT)]
    if l == 0:
        j += [("rqk", t) for t in range(NT)]
    for u in range(1, 2 * NT + 2):
        if u <= 2 * NT:
            j += [("PT", u - 1)]
        if u >= 2:
            j += [("O", u - 2)]
    if l == 0:
        for t in range(NT):
            j += [("AT", t)] + ([("st", t)] if t < NT - 1 else []) + [("ro", t)]
    j += [("wo", t) for t in range(NT)]
    j += [("a", c) for c in range(NHC)]
    j += [("w2", t) for t in range(NT)]
    if l == 0:
        j += [("rout", t) for t in range(NT)]
    else:
        j += [("lat",), ("kr",)] + [("kc", g) for g in range(LG)] + [("lq", g) for g in range(LG)]
        for h in range(LH):
            j += [("s1", h), ("s2", h)]
        j += [("aTM", t) for t in range(NT)]
        j += [("lo", t) for t in range(NT)]
        j += [("rt",)]
    return j


def place(h):
    return 2 * (h % 2) + h // 2


def build(nc, I, O):
    x_d = I["x"].rearrange("b (t p) c -> b p t c", p=P)
    out_d = O.rearrange("b (t p) c -> (b t) p c", p=P)
    scratch = lambda n, s: nc.dram_tensor(n, s, F32, kind="Internal").ap()
    x1_s = scratch("x1_s", [B, P, NT, D])
    s2_s = scratch("s2_s", [B, P, NT, D])
    cw_s = scratch("cw_s", [B, P, NT, E])
    x1T_s = scratch("x1T_s", [B, P, NT, DC, P])
    moe_s = scratch("moe_s", [B * NT, P, D])

    cur_s = scratch("cur_s", [B, P, NT, D])
    s_s = scratch("s_s", [B, P, NT, D])
    block_layer(nc, I, 0, x_d, cur_s, s_s, x1_s, s2_s, cw_s, x1T_s)
    block_layer(nc, I, 1, x_d, cur_s, s_s, x1_s, s2_s, cw_s, x1T_s)
    block_moe(nc, I, x1T_s, cw_s, moe_s)
    block_out(nc, x1_s, s2_s, moe_s, out_d)


def block_layer(nc, I, l, x_d, cur_s, s_s, x1_s, s2_s, cw_s, x1T_s):
    AJ = {n: i for i, n in enumerate(act_jobs(l))}
    DJ = {n: i for i, n in enumerate(dve_jobs(l))}
    ctx = ExitStack()
    with ctx:
        def sb(name, shape, dt=F32):
            return ctx.enter_context(nc.sbuf_tensor(f"L{l}_{name}", shape, dt))

        def sem(name):
            return ctx.enter_context(nc.semaphore(f"L{l}_{name}"))

        W = {}
        first = (("rWqk", [P, DC, 512]), ("rWv", [P, DC, RV]), ("rWg", [P, DC, RV]), ("rWo", [P, RH, D]),
                 ("rln", [P, 2, DC]), ("rgn", [P, 1]), ("rC", [P, NT, 8, 32]), ("rS", [P, NT, 8, 2, 32]))
        second = (("lWd", [P, 2, DC, LAT]), ("lWq", [LAT, 2, LG, P]), ("lWk", [LAT, LG, P]),
                  ("lWkr", [P, 2, DC, P]), ("lWv", [LAT, LH * LDH]), ("lWo", [P, DC, D]),
                  ("lcos", [P, T]), ("lsin", [P, T]), ("gw", [P, DC, E]))
        layer = (("wqkv", [P, DC, 3 * INNER]), ("wo", [P, 4, D]), ("ln", [P, 2, DC]), ("w1", [P, DC, 2 * HID]),
                 ("b1", [HCH, 2, NHC]), ("w2", [HCH, NHC, D]), ("qks", [P, 2, 2, DH]))
        both = (("fC", [P, NT, 2, DH]), ("fS", [P, NT, 2, DH]))
        source = {}
        for n, shape in (second if l else first) + both + layer:
            W[n] = sb("w_" + n, shape)
            source[n] = I["w_" + n][:, l] if (n, shape) in layer else I["w_" + n]
        Ct = sb("Ct", [P, NT, 2, DH])
        St = sb("St", [P, NT, 2, DH])
        ident = sb("ident", [P, P])
        identb = sb("identb", [P, P], BF16)
        tri = sb("tri", [P, P])
        maskw = sb("maskw", [P, 2, P], BF16)
        half = sb("half", [P, 16])

        x_tm = sb("x_tm", [P, NT, D])
        xn = sb("xn", [P, NT, D])
        cur = sb("cur", [P, NT, D])
        curT = sb("curT", [P, DC, T + 1])
        hB = sb("hB", [P, NT, P])
        z = sb("z", [P, NT, D])
        zT = sb("zT", [P, DC, T])
        stat = sb("stat", [P, NT, 2, 6])
        mv = sb("mv", [P, NT, 2])
        ve = sb("ve", [P, NT])
        rs = sb("rs", [P, NT])
        s_tm = sb("s_tm", [P, NT, D])

        ARENA = 20480 + 2048
        arena = sb("arena", [P, ARENA])
        at = [0]

        def view(n):
            v = arena[:, at[0]:at[0] + n]
            at[0] += n
            assert at[0] <= ARENA, at[0]
            return v

        rqk = view(NT * 512).rearrange("p (t n) -> p t n", t=NT)
        rqkT = view(4 * T).rearrange("p (c n) -> p c n", c=4)
        rv = view(NT * RV).rearrange("p (t n) -> p t n", t=NT)
        gs = view(NT * RV).rearrange("p (t n) -> p t n", t=NT)
        mid = at[0]
        qk = view(NT * 1024).rearrange("p (t n) -> p t n", t=NT)
        qkT = view(8 * T).rearrange("p (c n) -> p c n", c=8)
        v_tm = view(NT * INNER).rearrange("p (t n) -> p t n", t=NT)
        sq = view(2 * 1024).rearrange("p (b n) -> p b n", b=2)
        rot = view(2 * 1024).rearrange("p (b n) -> p b n", b=2)
        prob = qk.rearrange("p t n -> p (t n)")[:, 0:2048].rearrange("p (b n) -> p b n", b=2)
        PT = qk.rearrange("p t n -> p (t n)")[:, 2048:4096].rearrange("p (b n) -> p b n", b=2)
        oT = sq.rearrange("p b n -> p (b n)").rearrange("p (c n) -> p c n", c=4)
        AT = rot.rearrange("p b n -> p (b n)")[:, 0:1024].rearrange("p (b n) -> p b n", b=2)
        o_sb = rot.rearrange("p b n -> p (b n)")[:, 1024:2048].rearrange("p (b n) -> p b n", b=2)
        osq = prob[:, 0, :].rearrange("p (b n) -> p b n", b=2)
        roT = gs.rearrange("p t n -> p (t n)").rearrange("p (c n) -> p c n", c=4)
        rst = sb("rst", [P, NT, 2, RDV])
        hT = qkT.rearrange("p c n -> p (c n)")[:, 0:NHC * T].rearrange("p (c n) -> p c n", c=NHC)
        gl = v_tm.rearrange("p t n -> p (t n)")[:, 0:2 * T].rearrange("p (b n) -> p b n", b=2)
        at[0] = 0
        Pl = view(2 * 4 * 1280).rearrange("p (b h n) -> p b h n", b=2, h=4)
        QT = view(LG * T).rearrange("p (g n) -> p g n", g=LG)
        KT = view(LG * T).rearrange("p (g n) -> p g n", g=LG)
        KrT = view(T)
        rm1 = view(2 * T).rearrange("p (b n) -> p b n", b=2)
        rm2 = view(2 * T).rearrange("p (b n) -> p b n", b=2)
        latT = view(2 * T).rearrange("p (b n) -> p b n", b=2)
        aT = view(LG * T).rearrange("p (g n) -> p g n", g=LG)
        if l:
            Vaug = sb("Vaug", [P, NT, LH, 32])
            iota8 = sb("iota8", [P, NT, E])
        attn = z
        attnT = zT
        s2 = s_tm
        ssq = sb("ssq", [P, NT, 16])
        rinv = sb("rinv", [P, NT, 16])
        mx = sb("mx", [P, 2 * NT, 4])
        rsum = sb("rsum", [P, 2 * NT, 4])
        rrec = sb("rrec", [P, 2 * NT, 4])
        rss = sb("rss", [P, NT, 4])
        rrs = sb("rrs", [P, NT, 4])
        rd = sb("rd", [P, NT, LH])
        rt = sb("rt", [P, 8, NT, E])
        rt1 = sb("rt1", [P, 8, NT])

        pA = [ctx.enter_context(nc.psum_tensor(f"L{l}_pA{i}", [P, 1024], F32)) for i in range(2)]
        pD = [ctx.enter_context(nc.psum_tensor(f"L{l}_pD{i}", [P, 1024], F32)) for i in range(2)]

        loaded = sem("loaded")
        const_p = sem("const_p")
        const_v = sem("const_v")
        per_batch = []

        def bsem(name):
            s = sem(name)
            per_batch.append(s)
            return s

        x_in = bsem("x_in")
        mmA = bsem("mmA")
        outA = bsem("outA")
        mmD = bsem("mmD")
        outD = bsem("outD")
        v_step = bsem("v_step")
        p_step = bsem("p_step")
        a_step = bsem("a_step")
        var_rdy = bsem("var_rdy")
        rstd = bsem("rstd")
        norm = bsem("norm")
        squares = bsem("squares")
        ssq_rdy = bsem("ssq_rdy")
        rinv_rdy = bsem("rinv_rdy")
        qk_rdy = bsem("qk_rdy")
        rqk_rdy = bsem("rqk_rdy")
        mx_rdy = bsem("mx_rdy")
        p_rdy = bsem("p_rdy")
        osq_rdy = bsem("osq_rdy")
        rss_rdy = bsem("rss_rdy")
        rrs_rdy = bsem("rrs_rdy")
        og_rdy = bsem("og_rdy")
        shifted = [bsem(f"shifted{t}") for t in range(NT)]
        fin_silu = bsem("fin_silu")
        x1_rdy = bsem("x1_rdy")
        stores = bsem("stores")
        lq_rdy = bsem("lq_rdy")
        lexp = bsem("lexp")
        masked = bsem("masked")
        cw_rdy = bsem("cw_rdy")
        arrive = bsem("arrive")
        p_const = sem("p_const")
        go = {e: sem("go_" + e) for e in ("pe", "act", "dve", "pool")}
        block = ctx.enter_context(nc.Block())

        names = list(W)

        @block.sync
        def _(sp):
            for n in names:
                sp.dma_start(W[n][:], source[n]).then_inc(loaded, 16)
            sp.wait_ge(const_v, 1)
            with sp.Fori(0, B) as b:
                sp.dma_start(x_tm[:], x_d[b]).then_inc(x_in, 16)
                if l:
                    sp.dma_start(cur[:], cur_s[b]).then_inc(x_in, 16)
                    sp.dma_start(s_tm[:], s_s[b]).then_inc(x_in, 16)
                for t in range(NT):
                    sp.wait_ge(outD, DJ["wo", t] + 1)
                    sp.dma_start(hB[1:P, t, :], cur[0:P - 1, t, P:D]).then_inc(shifted[t], 16)
                    if t == 0:
                        sp.dma_start(hB[0:1, 0, :], I["zrow"]).then_inc(shifted[t], 16)
                    else:
                        sp.dma_start(hB[0:1, t, :], cur[P - 1:P, t - 1, P:D]).then_inc(shifted[t], 16)
                if l == 0:
                    sp.wait_ge(outD, DJ["w2", NT - 1] + 1)
                    sp.dma_start(cur_s[b], cur[:]).then_inc(stores, 16)
                    sp.wait_ge(outD, DJ["rout", NT - 1] + 1)
                    sp.dma_start(s_s[b], s_tm[:]).then_inc(stores, 16)
                    sp.wait_ge(stores, 32)
                else:
                    sp.wait_ge(x1_rdy, NT)
                    sp.dma_start(x1_s[b], x_tm[:]).then_inc(stores, 16)
                    for t in range(NT):
                        sp.wait_ge(outA, AJ["x1T", t] + 1)
                        sp.dma_start(x1T_s[b][:, t], curT[:, :, 1 + P * t:1 + P * (t + 1)]).then_inc(stores, 16)
                    sp.wait_ge(outD, DJ["lo", NT - 1] + 1)
                    sp.dma_start(s2_s[b], s2[:]).then_inc(stores, 16)
                    sp.wait_ge(cw_rdy, 1)
                    sp.dma_start(cw_s[b], rt[:, 7]).then_inc(stores, 16)
                    sp.wait_ge(stores, 16 * (3 + NT))
                sp.wait_ge(arrive, 4)
                for s in per_batch:
                    sp.sem_clear(s)
                for g in go.values():
                    sp.sem_inc(g, 1)

        @block.tensor
        def _(pe):
            na, nd = [0], [0]

            def slotA(name):
                k = AJ[name]
                assert k == na[0], (name, k, na[0])
                na[0] += 1
                if k >= 2:
                    pe.wait_ge(outA, k - 1)
                return pA[k % 2]

            def slotD(name):
                k = DJ[name]
                assert k == nd[0], (name, k, nd[0])
                nd[0] += 1
                if k >= 2:
                    pe.wait_ge(outD, k - 1)
                return pD[k % 2]

            def transposes(name, src, chunks):
                ps = slotA(name)
                for c in range(chunks):
                    last = nc.tensor.transpose(ps[:, c * P:(c + 1) * P], src(c), ident[:])
                last.then_inc(mmA, 1)

            def project(out, lhs, rhs, n):
                for c in range(n):
                    last = nc.tensor.matmul(out, lhs(c), rhs(c), start=(c == 0), stop=(c == n - 1))
                return last

            def tile_cols(t):
                return slice(t * P, (t + 1) * P)

            def shifted_lhs(t):
                return lambda c: curT[:, c, t * P + (1 - c):(t + 1) * P + (1 - c)]

            def latent_attention():
                for t in range(NT):
                    pe.wait_ge(norm, 2 * NT + t - NT + 1)
                    transposes(("x1T", t), lambda c: xn[:, t, c * P:(c + 1) * P], DC)
                xT = lambda c: curT[:, c, 1:T + 1]
                pe.wait_ge(outA, AJ["x1T", NT - 1] + 1)
                ps = slotD(("lat",))
                for i in range(2):
                    last = project(ps[0:LAT, i * T:(i + 1) * T], lambda c: W["lWd"][:, i, c, :], xT, DC)
                last.then_inc(mmD, 1)
                ps = slotD(("kr",))
                for i in range(2):
                    last = project(ps[:, i * T:(i + 1) * T], lambda c: W["lWkr"][:, i, c, :], xT, DC)
                last.then_inc(mmD, 1)
                pe.wait_ge(outD, DJ["lat",] + 1)
                for t in range(NT):
                    ps = slotA(("lv", t))
                    nc.tensor.matmul(ps[:, 0:D], latT[0:LAT, 1, tile_cols(t)], W["lWv"][:], start=True, stop=True).then_inc(mmA, 1)
                for g in range(LG):
                    ps = slotD(("kc", g))
                    nc.tensor.matmul(ps[:, 0:T], W["lWk"][:, g, :], latT[0:LAT, 1, :], start=True, stop=True).then_inc(mmD, 1)
                for g in range(LG):
                    ps = slotD(("lq", g))
                    for i in range(2):
                        last = nc.tensor.matmul(ps[:, i * T:(i + 1) * T], W["lWq"][:, i, g, :], latT[0:LAT, 0, :], start=True, stop=True)
                    last.then_inc(mmD, 1)

                def values(g):
                    pe.wait_ge(masked, 4 * g + 4)
                    pe.wait_ge(outA, AJ["lv", NT - 1] + 1)
                    ps = slotA(("av", g))
                    for kt, off in ((0, 0), (1, 512), (2, 1024), (3, 896)):
                        for i in range(4):
                            last = nc.tensor.matmul(ps[32 * i:32 * i + 32, kt * P:T], Vaug[:, kt, 4 * g + i, :],
                                                    Pl[:, g % 2, i, off:off + T - kt * P], start=(kt == 0), stop=(kt == NT - 1))
                    last.then_inc(mmA, 1)

                for g in range(LG):
                    pe.wait_ge(lq_rdy, g + 1)
                    pe.wait_ge(outD, DJ["kc", g] + 1)
                    for i in range(4):
                        r = slice(32 * i, 32 * i + 32)

                        def score(out, kt):
                            return nc.tensor.matmul(out, KT[r, g, tile_cols(kt)], QT[r, g, kt * P:T], start=True, stop=True)
                        ps = slotD(("s1", 4 * g + i))
                        score(ps[:, 0:512], 0)
                        score(ps[:, 512:896], 1)
                        score(ps[:, 896:1024], 3).then_inc(mmD, 1)
                        ps = slotD(("s2", 4 * g + i))
                        score(ps[:, 0:256], 2).then_inc(mmD, 1)
                    if g > 0:
                        values(g - 1)
                values(LG - 1)
                pe.wait_ge(outA, AJ["av", LG - 1] + 1)
                for t in range(NT):
                    ps = slotD(("aTM", t))
                    for g in range(LG):
                        last = nc.tensor.transpose(ps[:, g * P:(g + 1) * P], aT[:, g, tile_cols(t)], ident[:])
                    last.then_inc(mmD, 1)
                for t in range(NT):
                    pe.wait_ge(outD, DJ["aTM", t] + 1)
                    transposes(("attnT", t), lambda c: attn[:, t, c * P:(c + 1) * P], DC)
                for t in range(NT):
                    pe.wait_ge(outA, AJ["attnT", t] + 1)
                    ps = slotD(("lo", t))
                    project(ps[:, 0:D], lambda c: attnT[:, c, tile_cols(t)], lambda c: W["lWo"][:, c, :], DC).then_inc(mmD, 1)
                ps = slotD(("rt",))
                for t in range(NT):
                    last = project(ps[:, t * E:(t + 1) * E], lambda c: curT[:, c, 1 + t * P:1 + (t + 1) * P], lambda c: W["gw"][:, c, :], DC)
                last.then_inc(mmD, 1)

            pe.wait_ge(loaded, 16 * len(names))
            pe.wait_ge(const_v, 1)
            with pe.Fori(0, B):
                for t in range(NT if l else 0):
                    if t == 0:
                        pe.wait_ge(x_in, 48)
                    transposes(("curT", t), lambda c: cur[:, t, c * P:(c + 1) * P], DC)
                for t in range(0 if l else NT):
                    pe.wait_ge(norm, t + 1)
                    transposes(("xT", t), lambda c: xn[:, t, c * P:(c + 1) * P], DC)
                for t in range(0 if l else NT):
                    pe.wait_ge(norm, NT + t + 1)
                    transposes(("zaT", t), lambda c: z[:, t, c * P:(c + 1) * P], DC)
                for t in range(NT):
                    pe.wait_ge(outA, AJ["curT" if l else "xT", t] + 1)
                    ps = slotD(("qk", t))
                    project(ps[:, 0:512], shifted_lhs(t), lambda c: W["wqkv"][:, c, 0:512], DC)
                    project(ps[:, 512:1024], shifted_lhs(t), lambda c: W["wqkv"][:, c, 512:1024], DC).then_inc(mmD, 1)
                    ps = slotA(("v", t))
                    project(ps[:, 0:512], shifted_lhs(t), lambda c: W["wqkv"][:, c, 1024:1536], DC).then_inc(mmA, 1)
                for t in range(NT):
                    if l == 0:
                        zl = lambda c: zT[:, c, tile_cols(t)]
                        pe.wait_ge(outA, AJ["zaT", t] + 1)
                        ps = slotD(("rqk", t))
                        project(ps[:, 0:512], zl, lambda c: W["rWqk"][:, c, :], DC).then_inc(mmD, 1)
                        ps = slotA(("rv", t))
                        project(ps[:, 0:RV], zl, lambda c: W["rWv"][:, c, :], DC).then_inc(mmA, 1)
                    pe.wait_ge(qk_rdy, t + 1)
                    transposes(("qkT", t), lambda c: qk[:, t, c * P:(c + 1) * P], 8)
                if l == 0:
                    for t in range(NT):
                        zl = lambda c: zT[:, c, tile_cols(t)]
                        ps = slotA(("rg", t))
                        project(ps[:, 0:RV], zl, lambda c: W["rWg"][:, c, :], DC).then_inc(mmA, 1)

                for u in range(2 * NT + 2):
                    if u < 2 * NT:
                        t, hh = u // 2, u % 2
                        pe.wait_ge(outA, AJ["qkT", t] + 1)
                        ps = slotA(("S", u))
                        lo = 0 if t else 1
                        for bank in range(2):
                            nc.tensor.matmul(ps[:, bank * 512:(bank + 1) * 512].rearrange("p (h k q) -> p h k q", h=2, k=2)[:, :, lo:2, :],
                                             identb[:], maskw[:, lo:2, :].unsqueeze(1).broadcast_to((P, 2, 2 - lo, P)), start=True, stop=False)
                        for i in range(4):
                            h = 4 * hh + i
                            r = slice(64 * (h % 2), 64 * (h % 2) + 64)
                            last = nc.tensor.matmul(ps[:, place(i) * 256 + lo * P:(place(i) + 1) * 256], qkT[r, h // 2, tile_cols(t)],
                                                    qkT[r, 4 + h // 2, (t - 1 + lo) * P:(t + 1) * P], start=False, stop=(i >= 2))
                        last.then_inc(mmA, 1)
                    if 1 <= u <= 2 * NT:
                        w = u - 1
                        pe.wait_ge(p_rdy, w + 1)
                        ps = slotD(("PT", w))
                        for i in range(4):
                            for k in range(0 if w // 2 else 1, 2):
                                last = nc.tensor.transpose(ps[:, (2 * i + k) * P:(2 * i + k + 1) * P],
                                                           prob[:, w % 2, i * 256 + k * P:i * 256 + (k + 1) * P], ident[:])
                        last.then_inc(mmD, 1)
                    if u >= 2:
                        w = u - 2
                        t, hh = w // 2, w % 2
                        pe.wait_ge(outD, DJ["PT", w] + 1)
                        ps = slotD(("O", w))
                        lo = 0 if t else 1
                        for pr in range(2):
                            for k in range(lo, 2):
                                for i in (2 * pr, 2 * pr + 1):
                                    h = 4 * hh + i
                                    last = nc.tensor.matmul(ps[64 * (i % 2):64 * (i % 2) + 64, pr * P:(pr + 1) * P],
                                                            v_tm[:, t - 1 + k, h * DH:(h + 1) * DH],
                                                            PT[:, w % 2, (2 * place(i) + k) * P:(2 * place(i) + k + 1) * P],
                                                            start=(k == lo), stop=(k == 1))
                        last.then_inc(mmD, 1)

                if l == 0:
                    for t in range(NT):
                        pe.wait_ge(rqk_rdy, t + 1)
                        transposes(("rT", t), lambda c: rqk[:, t, c * P:(c + 1) * P], 4)
                    for t in range(NT):
                        pe.wait_ge(outA, AJ["rT", t] + 1)
                        ps = slotD(("AT", t))
                        for h in range(RH):
                            r = slice(64 * (h % 2), 64 * (h % 2) + 64)
                            last = nc.tensor.matmul(ps[:, (h % 2) * 512 + (h // 2) * P:(h % 2) * 512 + (h // 2 + 1) * P], rqkT[r, 2 + h // 2, tile_cols(t)],
                                                    rqkT[r, h // 2, tile_cols(t)], start=True, stop=True)
                        last.then_inc(mmD, 1)
                        if t < NT - 1:
                            ps = slotD(("st", t))
                            for h in range(RH):
                                last = nc.tensor.matmul(ps[64 * (h % 2):64 * (h % 2) + 64, (h // 2) * RDV:(h // 2 + 1) * RDV],
                                                        rqk[:, t, 256 + h * RDK:256 + (h + 1) * RDK],
                                                        rv[:, t, h * RDV:(h + 1) * RDV], start=True, stop=True)
                            last.then_inc(mmD, 1)
                        pe.wait_ge(outD, DJ["AT", t] + 1)
                        ps = slotD(("ro", t))
                        for h in range(RH):
                            r = slice(64 * (h % 2), 64 * (h % 2) + 64)
                            out = ps[:, (h % 2) * 512 + (h // 2) * RDV:(h % 2) * 512 + (h // 2 + 1) * RDV]
                            last = nc.tensor.matmul(out, AT[:, t % 2, place(h) * P:(place(h) + 1) * P], rv[:, t, h * RDV:(h + 1) * RDV],
                                                    start=True, stop=(t == 0))
                            if t:
                                last = nc.tensor.matmul(out, rqkT[r, h // 2, tile_cols(t)], rst[r, t, h // 2, :],
                                                        start=False, stop=True)
                        last.then_inc(mmD, 1)
                    for t in range(NT):
                        pe.wait_ge(og_rdy, t + 1)
                        transposes(("roT", t), lambda c: rqk[:, t, c * P:(c + 1) * P], 4)

                for t in range(NT):
                    pe.wait_ge(outD, DJ["O", 2 * t + 1] + 1)
                    ps = slotD(("wo", t))
                    project(ps[:, 0:D], lambda c: oT[:, c, tile_cols(t)], lambda c: W["wo"][:, c, :], 4).then_inc(mmD, 1)
                for t in range(NT):
                    pe.wait_ge(norm, (0 if l else 2 * NT) + t + 1)
                    transposes(("zT", t), lambda c: z[:, t, c * P:(c + 1) * P], DC)
                for c in range(NHC):
                    n = HSZ[c]
                    if c == 0:
                        pe.wait_ge(outA, AJ["zT", NT - 1] + 1)
                    ps = slotA(("g", c))
                    project(ps[0:n, 0:T], lambda k: W["w1"][:, k, HID + c * HCH:HID + c * HCH + n], lambda k: zT[:, k, :], DC).then_inc(mmA, 1)
                    ps = slotD(("a", c))
                    project(ps[0:n, 0:T], lambda k: W["w1"][:, k, c * HCH:c * HCH + n], lambda k: zT[:, k, :], DC).then_inc(mmD, 1)
                for t in range(NT):
                    if t == 0:
                        pe.wait_ge(outD, DJ["a", NHC - 1] + 1)
                    ps = slotD(("w2", t))
                    rows = [min(HCH, HSZ[c] + (c == NHC - 1)) for c in range(NHC)]
                    project(ps[:, 0:D], lambda c: hT[0:rows[c], c, tile_cols(t)], lambda c: W["w2"][0:rows[c], c, :], NHC).then_inc(mmD, 1)
                if l == 0:
                    for t in range(NT):
                        pe.wait_ge(outA, AJ["roT", t] + 1)
                        ps = slotD(("rout", t))
                        project(ps[:, 0:D], lambda c: roT[:, c, tile_cols(t)], lambda c: W["rWo"][:, c, :], RH).then_inc(mmD, 1)
                if l:
                    latent_attention()
                pe.sem_inc(arrive, 1)
                pe.wait_ge(go["pe"], 1)
                pe.sem_clear(go["pe"])

        @block.scalar
        def _(act):
            na = [0]

            def take(name):
                k = AJ[name]
                assert k == na[0], (name, k, na[0])
                na[0] += 1
                act.wait_ge(mmA, k + 1)
                return pA[k % 2]

            def scaled(name, t, w):
                ps = take(name)
                for c in range(DC):
                    last = nc.scalar.activation(zT[:, c, t * P:(t + 1) * P], ps[:, c * P:(c + 1) * P], ACT.Identity,
                                                bias=w[:, 1, c:c + 1], scale=w[:, 0, c:c + 1])
                last.then_inc(outA, 1)

            def by_channel(name, t):
                ps = take(name)
                nc.scalar.copy(curT[:, :, 1 + t * P:1 + (t + 1) * P], ps[:, 0:D].rearrange("p (c n) -> p c n", c=DC)).then_inc(outA, 1)

            def latent_attention():
                for t in range(NT):
                    act.wait_ge(outD, DJ["w2", t] + 1)
                    nc.scalar.activation(z[:, t, :], cur[:, t, :], ACT.Silu).then_inc(fin_silu, 1)
                for t in range(NT):
                    by_channel(("x1T", t), t)
                for t in range(NT):
                    ps = take(("lv", t))
                    nc.scalar.copy(Vaug[:, t, :, 0:LDH], ps[:, 0:D].rearrange("p (h d) -> p h d", h=LH)).then_inc(outA, 1)

                def av(g):
                    ps = take(("av", g))
                    nc.scalar.copy(aT[:, g, :], ps[:, 0:T]).then_inc(outA, 1)

                for g in range(LG):
                    for i in range(4):
                        act.wait_ge(outD, DJ["s2", 4 * g + i] + 1)
                        ph = Pl[:, g % 2, i, :]
                        nc.scalar.activation(ph, ph, ACT.Exp, scale=1.0 / SQ24).then_inc(lexp, 1)
                    if g > 0:
                        av(g - 1)
                av(LG - 1)
                for t in range(NT):
                    ps = take(("attnT", t))
                    nc.scalar.copy(attnT[:, :, t * P:(t + 1) * P], ps[:, 0:D].rearrange("p (c n) -> p c n", c=DC)).then_inc(outA, 1)
                act.wait_ge(outD, DJ["rt",] + 1)
                nc.scalar.activation(rt[:, 1], rt[:, 0], ACT.Exp).then_inc(a_step, 1)
                act.wait_ge(a_step, 1)

            act.wait_ge(loaded, 16 * len(names))
            act.wait_ge(const_p, 1)
            with act.Fori(0, B):
                for t in range(NT):
                    by_channel(("curT" if l else "xT", t), t)
                for t in range(0 if l else NT):
                    scaled(("zaT", t), t, W["rln"])
                for t in range(NT):
                    act.wait_ge(mmD, DJ["qk", t] + 1)
                    if t >= 2:
                        act.wait_ge(outD, DJ["qk", t - 2] + 1)
                    nc.scalar.activation(sq[:, t % 2, :], pD[DJ["qk", t] % 2][:], ACT.Square).then_inc(squares, 1)
                    ps = take(("v", t))
                    nc.scalar.copy(v_tm[:, t, :], ps[:, 0:512]).then_inc(outA, 1)
                for t in range(NT):
                    if l == 0:
                        ps = take(("rv", t))
                        nc.scalar.copy(rv[:, t, :], ps[:, 0:512]).then_inc(outA, 1)
                    ps = take(("qkT", t))
                    nc.scalar.copy(qkT[:, :, t * P:(t + 1) * P], ps[:].rearrange("p (c n) -> p c n", c=8)).then_inc(outA, 1)
                if l == 0:
                    for t in range(NT):
                        ps = take(("rg", t))
                        nc.scalar.activation(gs[:, t, :], ps[:, 0:512], ACT.Silu).then_inc(outA, 1)
                for u in range(2 * NT):
                    act.wait_ge(mx_rdy, u + 1)
                    if u >= 2:
                        act.wait_ge(mmD, DJ["PT", u - 2] + 1)
                    ps = take(("S", u))
                    lo = 0 if u // 2 else P
                    for i in range(4):
                        last = nc.scalar.activation(prob[:, u % 2, i * 256 + lo:(i + 1) * 256], ps[:, i * 256 + lo:(i + 1) * 256], ACT.Exp,
                                                    bias=mx[:, u, i:i + 1], accum_out=rsum[:, u, i:i + 1])
                    last.then_inc(outA, 1)
                if l == 0:
                    for t in range(NT):
                        ps = take(("rT", t))
                        nc.scalar.copy(rqkT[:, :, t * P:(t + 1) * P], ps[:, 0:512].rearrange("p (c n) -> p c n", c=4)).then_inc(outA, 1)
                    for t in range(NT):
                        act.wait_ge(outD, DJ["ro", t] + 1)
                        if t >= 2:
                            act.wait_ge(rss_rdy, t - 1)
                        nc.scalar.activation(osq[:, t % 2, :], o_sb[:, t % 2, :], ACT.Square).then_inc(osq_rdy, 1)
                    for t in range(NT):
                        ps = take(("roT", t))
                        act.wait_ge(og_rdy, NT)
                        nc.scalar.copy(roT[:, :, t * P:(t + 1) * P], ps[:, 0:512].rearrange("p (c n) -> p c n", c=4)).then_inc(outA, 1)
                for t in range(NT):
                    scaled(("zT", t), t, W["ln"])
                for c in range(NHC):
                    n = HSZ[c]
                    if c >= 2:
                        act.wait_ge(outD, DJ["a", c - 2] + 1)
                    ps = take(("g", c))
                    nc.scalar.activation(gl[0:n, c % 2, :], ps[0:n, 0:T], ACT.Gelu, bias=W["b1"][0:n, 1, c:c + 1]).then_inc(outA, 1)
                if l:
                    latent_attention()
                act.sem_inc(arrive, 1)
                act.wait_ge(go["act"], 1)
                act.sem_clear(go["act"])

        @block.gpsimd
        def _(pool):
            n = [0]

            def step(ins):
                n[0] += 1
                ins.then_inc(p_const, 1)
                pool.wait_ge(p_const, n[0])

            step(nc.gpsimd.memset(ident[:], 0.0))
            step(nc.gpsimd.affine_select(out=ident[:], in_=ident[:], compare_op=ALU.not_equal, fill=1.0, base=0,
                                         pattern=[[-1, P]], channel_multiplier=1))
            step(nc.gpsimd.tensor_copy(identb[:], ident[:]))
            step(nc.gpsimd.memset(tri[:], 1.0))
            step(nc.gpsimd.affine_select(out=tri[:], in_=tri[:], compare_op=ALU.is_ge, fill=0.0, base=0,
                                         pattern=[[1, P]], channel_multiplier=-1))
            step(nc.gpsimd.memset(maskw[:], 0.0))
            step(nc.gpsimd.affine_select(out=maskw[:, 0, :], in_=maskw[:, 0, :], compare_op=ALU.is_ge, fill=-1e30, base=0,
                                         pattern=[[1, P]], channel_multiplier=-1))
            step(nc.gpsimd.affine_select(out=maskw[:, 1, :], in_=maskw[:, 1, :], compare_op=ALU.is_ge, fill=-1e30, base=0,
                                         pattern=[[-1, P]], channel_multiplier=1))
            step(nc.gpsimd.memset(half[:], -0.5))
            if l:
                for e in range(E):
                    step(nc.gpsimd.memset(iota8[:, :, e:e + 1], float(E - e)))
                step(nc.gpsimd.memset(Vaug[:], 0.0))
                step(nc.gpsimd.memset(Vaug[:, :, :, LDH:LDH + 1], 1.0))
            nc.gpsimd.memset(curT[:, :, 0:1], 0.0).then_inc(const_p, 1)

            def rsqrt_tile(k):
                pool.wait_ge(var_rdy, k + 1)
                t = k % NT
                nc.gpsimd.tensor_tensor(rs[:, t:t + 1], ve[:, t:t + 1], half[:, 0:1], ALU.pow).then_inc(rstd, 1)

            with pool.Fori(0, B):
                for k in range(0 if l else 2 * NT):
                    rsqrt_tile(k)
                for t in range(NT):
                    pool.wait_ge(ssq_rdy, t + 1)
                    nc.gpsimd.tensor_tensor(rinv[:, t, :], ssq[:, t, :], half[:], ALU.pow)
                    nc.gpsimd.tensor_tensor(qk[:, t, :], qk[:, t, :], rot[:, t % 2, :], ALU.add).then_inc(rinv_rdy, 1)
                if l == 0:
                    for t in range(NT):
                        pool.wait_ge(outD, DJ["rqk", t] + 1)
                        nc.gpsimd.tensor_tensor(rqk[:, t, :], rqk[:, t, :], rot[:, t % 2, 0:512], ALU.add).then_inc(rqk_rdy, 1)
                    for t in range(NT):
                        pool.wait_ge(rss_rdy, t + 1)
                        nc.gpsimd.tensor_tensor(rrs[:, t, :], rss[:, t, :], half[:, 0:4], ALU.pow).then_inc(rrs_rdy, 1)
                for t in range(NT):
                    rsqrt_tile((0 if l else 2) * NT + t)
                if l:
                    for t in range(NT):
                        rsqrt_tile(NT + t)
                    for g in range(LG):
                        pool.wait_ge(outD, DJ["lq", g] + 1)
                        nc.gpsimd.tensor_tensor(QT[:, g, :], rm1[:, g % 2, :], rm2[:, g % 2, :], ALU.add).then_inc(lq_rdy, 1)
                    for h in range(LH):
                        pool.wait_ge(lexp, h + 1)
                        ph = Pl[:, (h // 4) % 2, h % 4, :]
                        nc.gpsimd.tensor_tensor(ph[:, 0:P], ph[:, 0:P], tri[:], ALU.mult)
                        nc.gpsimd.tensor_tensor(ph[:, 512:640], ph[:, 512:640], tri[:], ALU.mult)
                        pair = ph[:, 896:1152].rearrange("p (a n) -> p a n", a=2)
                        nc.gpsimd.tensor_tensor(pair, pair, tri[:].unsqueeze(1).broadcast_to((P, 2, P)), ALU.mult).then_inc(masked, 1)
                pool.wait_ge(masked, LH) if l else pool.wait_ge(rstd, 3 * NT)
                pool.sem_inc(arrive, 1)
                pool.wait_ge(go["pool"], 1)
                pool.sem_clear(go["pool"])

        @block.vector
        def _(dve):
            nd, ns, nln = [0], [0], [0]

            def take(name):
                k = DJ[name]
                assert k == nd[0], (name, k, nd[0])
                nd[0] += 1
                dve.wait_ge(mmD, k + 1)
                return pD[k % 2]

            def step(ins):
                ns[0] += 1
                ins.then_inc(v_step, 1)
                dve.wait_ge(v_step, ns[0])

            def heads(ap, h):
                return ap.rearrange("p (h d) -> p h d", h=h)

            def per_head(ap, n):
                return ap.unsqueeze(2).broadcast_to((P, ap.shape[1], n))

            def ln_stats(t, parts):
                for i, ap in enumerate(parts):
                    last = nc.vector.bn_stats(stat[:, t, i, :], ap)
                step(last)
                step(nc.vector.bn_aggr(mv[:, t, :], stat[:, t, 0:len(parts), :]))
                nc.vector.tensor_scalar(ve[:, t:t + 1], mv[:, t, 1:2], EPS, None, ALU.add).then_inc(var_rdy, 1)

            def ln_apply(t, parts, out):
                dve.wait_ge(rstd, nln[0] + 1)
                nln[0] += 1
                for i, ap in enumerate(parts):
                    n = D // len(parts)
                    last = nc.vector.tensor_scalar(out[:, t, i * n:(i + 1) * n], ap, mv[:, t, 0:1], rs[:, t:t + 1], ALU.subtract, ALU.mult)
                last.then_inc(norm, 1)

            def latent_attention():
                for t in range(NT):
                    dve.wait_ge(fin_silu, t + 1)
                    step(nc.vector.tensor_tensor(z[:, t, :], z[:, t, :], s_tm[:, t, :], ALU.mult))
                    nc.vector.tensor_tensor(x_tm[:, t, :], x_tm[:, t, :], z[:, t, :], ALU.add).then_inc(x1_rdy, 1)
                    dve.wait_ge(x1_rdy, t + 1)
                    ln_stats(t, [x_tm[:, t, :]])
                for t in range(NT):
                    ln_apply(t, [x_tm[:, t, :]], xn)

                ps = take(("lat",))
                nc.vector.tensor_copy(latT[0:LAT], ps[0:LAT, :].rearrange("p (a n) -> p a n", a=2)).then_inc(outD, 1)
                ps = take(("kr",))
                nc.vector.tensor_tensor(rm1[:, 0, :], ps[:, 0:T], W["lcos"][:], ALU.mult)
                nc.vector.tensor_tensor(rm2[:, 0, :], ps[:, T:2 * T], W["lsin"][:], ALU.mult).then_inc(outD, 1)
                dve.wait_ge(outD, DJ["kr",] + 1)
                step(nc.vector.tensor_tensor(KrT, rm1[:, 0, :], rm2[:, 0, :], ALU.add))
                for g in range(LG):
                    ps = take(("kc", g))
                    nc.vector.tensor_tensor(KT[:, g, :], ps[:, 0:T], KrT, ALU.add).then_inc(outD, 1)
                for g in range(LG):
                    ps = take(("lq", g))
                    if g >= 2:
                        dve.wait_ge(lq_rdy, g - 1)
                    nc.vector.tensor_tensor(rm1[:, g % 2, :], ps[:, 0:T], W["lcos"][:], ALU.mult)
                    nc.vector.tensor_tensor(rm2[:, g % 2, :], ps[:, T:2 * T], W["lsin"][:], ALU.mult).then_inc(outD, 1)
                for h in range(LH):
                    g = h // 4
                    if g >= 2 and h % 4 == 0:
                        dve.wait_ge(mmA, AJ["av", g - 2] + 1)
                    ph = Pl[:, g % 2, h % 4, :]
                    ps = take(("s1", h))
                    nc.vector.tensor_scalar(ph[:, 0:1024], ps[:], 80.0, -80.0, ALU.min, ALU.max).then_inc(outD, 1)
                    ps = take(("s2", h))
                    nc.vector.tensor_scalar(ph[:, 1024:1280], ps[:, 0:256], 80.0, -80.0, ALU.min, ALU.max).then_inc(outD, 1)
                for t in range(NT):
                    ps = take(("aTM", t))
                    pv = ps[:, 0:512].rearrange("p (h d) -> p h d", h=LH)
                    step(nc.vector.reciprocal(rd[:, t, :], pv[:, :, LDH]))
                    nc.vector.tensor_tensor(heads(attn[:, t, :], LH), pv[:, :, 0:LDH], per_head(rd[:, t, :], LDH), ALU.mult).then_inc(outD, 1)
                for t in range(NT):
                    ps = take(("lo", t))
                    nc.vector.tensor_copy(s2[:, t, :], ps[:, 0:D]).then_inc(outD, 1)

                ps = take(("rt",))
                lg = ps[:, 0:NT * E].rearrange("p (t e) -> p t e", t=NT)
                wide = lambda ap: ap.unsqueeze(2).broadcast_to((P, NT, E))
                step(nc.vector.tensor_reduce(rt1[:, 0], lg, AX.X, ALU.max))
                nc.vector.tensor_tensor(rt[:, 0], lg, wide(rt1[:, 0]), ALU.subtract).then_inc(outD, 1)
                dve.wait_ge(a_step, 1)
                step(nc.vector.tensor_reduce(rt1[:, 1], rt[:, 1], AX.X, ALU.add))
                step(nc.vector.reciprocal(rt1[:, 2], rt1[:, 1]))
                step(nc.vector.tensor_tensor(rt[:, 2], rt[:, 1], wide(rt1[:, 2]), ALU.mult))
                for k in range(2):
                    step(nc.vector.tensor_reduce(rt1[:, 3], rt[:, 2], AX.X, ALU.max))
                    step(nc.vector.tensor_tensor(rt[:, 3], rt[:, 2], wide(rt1[:, 3]), ALU.is_equal))
                    step(nc.vector.tensor_tensor(rt[:, 4], rt[:, 3], iota8[:], ALU.mult))
                    step(nc.vector.tensor_reduce(rt1[:, 4], rt[:, 4], AX.X, ALU.max))
                    step(nc.vector.tensor_tensor(rt[:, 5 + k], iota8[:], wide(rt1[:, 4]), ALU.is_equal))
                    if k == 0:
                        step(nc.vector.tensor_tensor(rt[:, 7], rt[:, 5], wide(rt1[:, 3]), ALU.mult))
                        step(nc.vector.tensor_copy(rt1[:, 5], rt1[:, 3]))
                        step(nc.vector.scalar_tensor_tensor(out=rt[:, 2], in0=rt[:, 5], scalar=-4.0, in1=rt[:, 2], op0=ALU.mult, op1=ALU.add))
                step(nc.vector.tensor_tensor(rt[:, 6], rt[:, 6], wide(rt1[:, 3]), ALU.mult))
                step(nc.vector.tensor_tensor(rt[:, 7], rt[:, 7], rt[:, 6], ALU.add))
                step(nc.vector.tensor_tensor(rt1[:, 6], rt1[:, 5], rt1[:, 3], ALU.add))
                step(nc.vector.reciprocal(rt1[:, 7], rt1[:, 6]))
                nc.vector.tensor_tensor(rt[:, 7], rt[:, 7], wide(rt1[:, 7]), ALU.mult).then_inc(cw_rdy, 1)
                dve.wait_ge(cw_rdy, 1)

            dve.wait_ge(loaded, 16 * len(names))
            dve.wait_ge(const_p, 1)
            for t in range(NT):
                nc.vector.tensor_tensor(Ct[:, t], W["fC"][:, t], W["qks"][:, 0], ALU.mult)
                last = nc.vector.tensor_tensor(St[:, t], W["fS"][:, t], W["qks"][:, 1], ALU.mult)
            if l == 0:
                last = nc.vector.tensor_scalar(W["rWo"][:], W["rWo"][:], W["rgn"][:, 0:1], None, ALU.mult)
            last.then_inc(const_v, 1)
            dve.wait_ge(const_v, 1)

            with dve.Fori(0, B):
                dve.wait_ge(x_in, 48 if l else 16)
                for t in range(0 if l else NT):
                    ln_stats(t, [x_tm[:, t, :]])
                for t in range(0 if l else NT):
                    ln_apply(t, [x_tm[:, t, :]], xn)
                for t in range(0 if l else NT):
                    dve.wait_ge(norm, t + 1)
                    ln_stats(t, [xn[:, t, :]])
                for t in range(0 if l else NT):
                    ln_apply(t, [xn[:, t, :]], z)

                stream = xn if l == 0 else cur
                def scale_qk(t):
                    dve.wait_ge(rinv_rdy, t + 1)
                    nc.vector.tensor_tensor(heads(qk[:, t, :], 16), heads(qk[:, t, :], 16), per_head(rinv[:, t, :], DH), ALU.mult).then_inc(qk_rdy, 1)

                for t in range(NT):
                    ps = take(("qk", t))
                    pv = ps[:].rearrange("p (a h d) -> p a h d", a=2, h=8)
                    o1 = qk[:, t, :].rearrange("p (a h d) -> p a h d", a=2, h=8)
                    o2 = rot[:, t % 2, :].rearrange("p (a h d) -> p a h d", a=2, h=8)
                    if t >= 2:
                        dve.wait_ge(rinv_rdy, t - 1)
                    dve.wait_ge(squares, t + 1)
                    nc.vector.tensor_tensor(o1, pv, Ct[:, t].unsqueeze(2).broadcast_to((P, 2, 8, DH)), ALU.mult)
                    for s in range(2):
                        a, b = slice(32 * s, 32 * s + 32), slice(32 * (1 - s), 32 * (1 - s) + 32)
                        nc.vector.tensor_tensor(o2[:, :, :, a], pv[:, :, :, b], St[:, t, :, a].unsqueeze(2).broadcast_to((P, 2, 8, 32)), ALU.mult)
                    nc.vector.tensor_reduce(ssq[:, t, :], heads(sq[:, t % 2, :], 16), AX.X, ALU.add).then_inc(outD, 1)
                    dve.wait_ge(outD, DJ["qk", t] + 1)
                    nc.vector.tensor_scalar(ssq[:, t, :], ssq[:, t, :], 1e-24, None, ALU.max).then_inc(ssq_rdy, 1)
                    if t:
                        scale_qk(t - 1)
                scale_qk(NT - 1)
                if l == 0:
                    for t in range(NT):
                        ps = take(("rqk", t))
                        pv = ps[:, 0:512].rearrange("p (h a d) -> p h a d", h=8, a=2)
                        o1 = rqk[:, t, :].rearrange("p (h a d) -> p h a d", h=8, a=2)
                        o2 = rot[:, t % 2, 0:512].rearrange("p (h a d) -> p h a d", h=8, a=2)
                        if t >= 2:
                            dve.wait_ge(rqk_rdy, t - 1)
                        elif t == 0:
                            dve.wait_ge(rinv_rdy, NT)
                        nc.vector.tensor_tensor(o1, pv, W["rC"][:, t].unsqueeze(2).broadcast_to((P, 8, 2, 32)), ALU.mult)
                        nc.vector.tensor_tensor(o2[:, :, 0, :], pv[:, :, 1, :], W["rS"][:, t, :, 0, :], ALU.mult)
                        nc.vector.tensor_tensor(o2[:, :, 1, :], pv[:, :, 0, :], W["rS"][:, t, :, 1, :], ALU.mult).then_inc(outD, 1)

                for u in range(2 * NT + 2):
                    if u < 2 * NT:
                        dve.wait_ge(mmA, AJ["S", u] + 1)
                        lo = 0 if u // 2 else P
                        nc.vector.tensor_reduce(mx[:, u, :], heads(pA[AJ["S", u] % 2][:], 4)[:, :, lo:256], AX.X, ALU.max, negate=True).then_inc(mx_rdy, 1)
                    if 1 <= u <= 2 * NT:
                        w = u - 1
                        lo = 0 if w // 2 else P
                        dve.wait_ge(outA, AJ["S", w] + 1)
                        step(nc.vector.reciprocal(rrec[:, w, :], rsum[:, w, :]))
                        pv = heads(prob[:, w % 2, :], 4)[:, :, lo:256]
                        nc.vector.tensor_tensor(pv, pv, per_head(rrec[:, w, :], 256 - lo), ALU.mult).then_inc(p_rdy, 1)
                        ps = take(("PT", w))
                        k = lo // P
                        if w >= 2:
                            dve.wait_ge(mmD, DJ["O", w - 2] + 1)
                        nc.vector.tensor_copy(PT[:, w % 2, :].rearrange("p (h k q) -> p h k q", h=4, k=2)[:, :, k:2, :],
                                              ps[:].rearrange("p (h k q) -> p h k q", h=4, k=2)[:, :, k:2, :]).then_inc(outD, 1)
                    if u >= 2:
                        w = u - 2
                        t, hh = w // 2, w % 2
                        ps = take(("O", w))
                        nc.vector.tensor_copy(oT[:, 2 * hh:2 * hh + 2, t * P:(t + 1) * P], ps[:, 0:256].rearrange("p (c n) -> p c n", c=2)).then_inc(outD, 1)

                if l == 0:
                    def gate(t):
                        dve.wait_ge(rrs_rdy, t + 1)
                        o = heads(rqk[:, t, :], 4)
                        step(nc.vector.tensor_tensor(o, heads(o_sb[:, t % 2, :], 4), per_head(rrs[:, t, :], RDV), ALU.mult))
                        nc.vector.tensor_tensor(rqk[:, t, :], rqk[:, t, :], gs[:, t, :], ALU.mult).then_inc(og_rdy, 1)
                    for t in range(NT):
                        ps = take(("AT", t))
                        nc.vector.tensor_tensor(AT[:, t % 2, :].rearrange("p (b a n) -> p b a n", b=2, a=2),
                                                ps[:].rearrange("p (b n) -> p b n", b=2)[:, :, 0:2 * P].rearrange("p b (a n) -> p b a n", a=2),
                                                tri[:].unsqueeze(1).unsqueeze(1).broadcast_to((P, 2, 2, P)), ALU.mult).then_inc(outD, 1)
                        if t < NT - 1:
                            ps = take(("st", t))
                            pv = ps[:, 0:256].rearrange("p (a n) -> p a n", a=2)
                            if t == 0:
                                nc.vector.tensor_copy(rst[:, 1], pv).then_inc(outD, 1)
                            else:
                                nc.vector.tensor_tensor(rst[:, t + 1], pv, rst[:, t], ALU.add).then_inc(outD, 1)
                        ps = take(("ro", t))
                        if t >= 2:
                            dve.wait_ge(og_rdy, t - 1)
                        nc.vector.tensor_copy(o_sb[:, t % 2, :].rearrange("p (a b n) -> p b a n", a=2, b=2),
                                              ps[:].rearrange("p (b n) -> p b n", b=2)[:, :, 0:2 * P].rearrange("p b (a n) -> p b a n", a=2)).then_inc(outD, 1)
                        dve.wait_ge(osq_rdy, t + 1)
                        step(nc.vector.tensor_reduce(rss[:, t, :], heads(osq[:, t % 2, :], 4), AX.X, ALU.add))
                        nc.vector.tensor_scalar(rss[:, t, :], rss[:, t, :], 1.0 / RDV, EPS, ALU.mult, ALU.add).then_inc(rss_rdy, 1)
                        if t:
                            gate(t - 1)
                    gate(NT - 1)

                parts = lambda t: [cur[:, t, 0:P], hB[:, t, :]]
                for t in range(NT):
                    ps = take(("wo", t))
                    nc.vector.tensor_tensor(cur[:, t, :], ps[:, 0:D], stream[:, t, :], ALU.add).then_inc(outD, 1)
                for t in range(NT):
                    dve.wait_ge(shifted[t], 32)
                    ln_stats(t, parts(t))
                for t in range(NT):
                    ln_apply(t, parts(t), z)
                step(nc.vector.memset(hT[64:HCH, NHC - 1, :], 1.0))
                for c in range(NHC):
                    n = HSZ[c]
                    ps = take(("a", c))
                    dve.wait_ge(outA, AJ["g", c] + 1)
                    nc.vector.scalar_tensor_tensor(out=hT[0:n, c, :], in0=ps[0:n, 0:T], scalar=W["b1"][0:n, 0, c:c + 1], in1=gl[0:n, c % 2, :],
                                                   op0=ALU.add, op1=ALU.mult).then_inc(outD, 1)
                for t in range(NT):
                    ps = take(("w2", t))
                    nc.vector.tensor_tensor(cur[:, t, :], ps[:, 0:D], cur[:, t, :], ALU.add).then_inc(outD, 1)
                if l == 0:
                    for t in range(NT):
                        ps = take(("rout", t))
                        nc.vector.tensor_tensor(s_tm[:, t, :], ps[:, 0:D], xn[:, t, :], ALU.add).then_inc(outD, 1)
                if l:
                    latent_attention()
                dve.sem_inc(arrive, 1)
                dve.wait_ge(go["dve"], 1)
                dve.sem_clear(go["dve"])


def block_moe(nc, I, x1T_s, cw_s, moe_s):
    ctx = ExitStack()
    with ctx:
        def sb(name, shape, dt=F32):
            return ctx.enter_context(nc.sbuf_tensor(name, shape, dt))

        def sem(name):
            return ctx.enter_context(nc.semaphore(name))
        w1 = sb("m_w1", [P, E, DC, F])
        w2 = sb("m_w2", [P, E, FC, D])
        ident = sb("m_ident", [P, P])
        xT = sb("m_xT", [P, DC, P])
        cw = sb("m_cw", [P, E])
        h = sb("m_h", [P, 2, F])
        hT = sb("m_hT", [P, 2, F])
        acc = sb("m_acc", [P, 2, D])
        ph = [ctx.enter_context(nc.psum_tensor(f"mh{i}", [P, F], F32)) for i in range(2)]
        pt = ctx.enter_context(nc.psum_tensor("mt", [P, F], F32))
        py = [ctx.enter_context(nc.psum_tensor(f"my{i}", [P, 512], F32)) for i in range(2)]
        wl = sem("m_wl")
        idr = sem("m_idr")
        zero = sem("m_zero")
        per_tile = []

        def bsem(name):
            s = sem(name)
            per_tile.append(s)
            return s
        xin = bsem("m_xin")
        up = bsem("m_up")
        gel = bsem("m_gel")
        tr = bsem("m_tr")
        trc = bsem("m_trc")
        dn = bsem("m_dn")
        ac = bsem("m_ac")
        st = bsem("m_st")
        arrive = bsem("m_arrive")
        go = {e: sem("m_go_" + e) for e in ("pe", "act", "dve")}
        block = ctx.enter_context(nc.Block())
        NTILES = B * NT

        @block.gpsimd
        def _(pool):
            nc.gpsimd.memset(ident[:], 0.0).then_inc(zero, 1)
            pool.wait_ge(zero, 1)
            nc.gpsimd.affine_select(out=ident[:], in_=ident[:], compare_op=ALU.not_equal, fill=1.0, base=0,
                                    pattern=[[-1, P]], channel_multiplier=1).then_inc(idr, 1)

        @block.sync
        def _(sp):
            for e in range(E):
                sp.dma_start(w1[:, e], I["m_w1"][e]).then_inc(wl, 16)
                sp.dma_start(w2[:, e], I["m_w2"][e]).then_inc(wl, 16)
            with sp.Fori(0, B) as b:
                for t in range(NT):
                    sp.dma_start(xT[:], x1T_s[b][:, t]).then_inc(xin, 16)
                    sp.dma_start(cw[:], cw_s[b][:, t]).then_inc(xin, 16)
                    sp.wait_ge(ac, E)
                    sp.dma_start(moe_s[b * NT + t], acc[:, (E - 1) % 2, :]).then_inc(st, 16)
                    sp.wait_ge(st, 16)
                    sp.wait_ge(arrive, 3)
                    for s in per_tile:
                        sp.sem_clear(s)
                    for g in go.values():
                        sp.sem_inc(g, 1)

        @block.tensor
        def _(pe):
            pe.wait_ge(wl, 32 * E)
            pe.wait_ge(idr, 1)
            with pe.Fori(0, NTILES):
                pe.wait_ge(xin, 32)
                for u in range(E + 2):
                    if u < E:
                        if u >= 2:
                            pe.wait_ge(gel, u - 1)
                        for c in range(DC):
                            for n in range(2):
                                last = nc.tensor.matmul(ph[u % 2][:, n * 512:(n + 1) * 512], xT[:, c, :], w1[:, u, c, n * 512:(n + 1) * 512],
                                                        start=(c == 0), stop=(c == DC - 1))
                        last.then_inc(up, 1)
                    if 1 <= u <= E:
                        w = u - 1
                        pe.wait_ge(gel, w + 1)
                        if w >= 1:
                            pe.wait_ge(trc, w)
                        for c in range(FC):
                            last = nc.tensor.transpose(pt[:, c * P:(c + 1) * P], h[:, w % 2, c * P:(c + 1) * P], ident[:])
                        last.then_inc(tr, 1)
                    if u >= 2:
                        w = u - 2
                        pe.wait_ge(trc, w + 1)
                        if w >= 2:
                            pe.wait_ge(ac, w - 1)
                        for c in range(FC):
                            last = nc.tensor.matmul(py[w % 2][:, 0:D], hT[:, w % 2, c * P:(c + 1) * P], w2[:, w, c, :], start=(c == 0), stop=(c == FC - 1))
                        last.then_inc(dn, 1)
                pe.sem_inc(arrive, 1)
                pe.wait_ge(go["pe"], 1)
                pe.sem_clear(go["pe"])

        @block.scalar
        def _(act):
            with act.Fori(0, NTILES):
                for w in range(E):
                    act.wait_ge(up, w + 1)
                    if w >= 2:
                        act.wait_ge(tr, w - 1)
                    nc.scalar.activation(h[:, w % 2, :], ph[w % 2][:], ACT.Gelu).then_inc(gel, 1)
                act.wait_ge(gel, E)
                act.sem_inc(arrive, 1)
                act.wait_ge(go["act"], 1)
                act.sem_clear(go["act"])

        @block.vector
        def _(dve):
            with dve.Fori(0, NTILES):
                dve.wait_ge(xin, 32)
                for u in range(E + 1):
                    if u < E:
                        dve.wait_ge(tr, u + 1)
                        if u >= 2:
                            dve.wait_ge(dn, u - 1)
                        nc.vector.tensor_copy(hT[:, u % 2, :], pt[:]).then_inc(trc, 1)
                    if u >= 1:
                        w = u - 1
                        dve.wait_ge(dn, w + 1)
                        if w == 0:
                            nc.vector.tensor_scalar(acc[:, 0, :], py[0][:, 0:D], cw[:, 0:1], None, ALU.mult).then_inc(ac, 1)
                        else:
                            dve.wait_ge(ac, w)
                            nc.vector.scalar_tensor_tensor(out=acc[:, w % 2, :], in0=py[w % 2][:, 0:D], scalar=cw[:, w:w + 1], in1=acc[:, 1 - w % 2, :],
                                                           op0=ALU.mult, op1=ALU.add).then_inc(ac, 1)
                dve.sem_inc(arrive, 1)
                dve.wait_ge(go["dve"], 1)
                dve.sem_clear(go["dve"])


def block_out(nc, x1_s, s2_s, moe_s, out_d):
    ctx = ExitStack()
    with ctx:
        def sb(name, shape, dt=F32):
            return ctx.enter_context(nc.sbuf_tensor(name, shape, dt))

        def sem(name):
            return ctx.enter_context(nc.semaphore(name))
        y = [sb(f"o_y{b}", [P, NT, D]) for b in range(B)]
        s = [sb(f"o_s{b}", [P, NT, D]) for b in range(B)]
        x = [sb(f"o_x{b}", [P, NT, D]) for b in range(B)]
        fetched = [sem(f"o_in{b}") for b in range(B)]
        gate = sem("o_gate")
        prod = sem("o_prod")
        sums = sem("o_sum")
        stored = sem("o_st")
        block = ctx.enter_context(nc.Block())
        moe_v = moe_s.rearrange("(b t) p c -> b p t c", t=NT)
        out_v = out_d.rearrange("(b t) p c -> b p t c", t=NT)

        @block.sync
        def _(sp):
            for b in range(B):
                sp.dma_start(y[b][:], moe_v[b]).then_inc(fetched[b], 16)
                sp.dma_start(s[b][:], s2_s[b]).then_inc(fetched[b], 16)
                sp.dma_start(x[b][:], x1_s[b]).then_inc(fetched[b], 16)
            for b in range(B):
                sp.wait_ge(sums, b + 1)
                sp.dma_start(out_v[b], x[b][:]).then_inc(stored, 16)
            sp.wait_ge(stored, 16 * B)

        @block.scalar
        def _(act):
            for b in range(B):
                act.wait_ge(fetched[b], 48)
                nc.scalar.activation(y[b][:], y[b][:], ACT.Silu).then_inc(gate, 1)

        @block.vector
        def _(dve):
            for b in range(B):
                dve.wait_ge(gate, b + 1)
                nc.vector.tensor_tensor(y[b][:], y[b][:], s[b][:], ALU.mult).then_inc(prod, 1)
                dve.wait_ge(prod, b + 1)
                nc.vector.tensor_tensor(x[b][:], x[b][:], y[b][:], ALU.add).then_inc(sums, 1)


def tables():
    f = np.float32
    inv = 1.0 / 10000.0 ** (np.arange(0, RDK, 2, dtype=np.float64) / RDK)
    ang = (np.arange(T, dtype=f)[:, None] * inv.astype(f)).astype(np.float64)
    gamma = 1.0 - 2.0 ** (-5.0 - np.arange(RH))
    rC = np.zeros((T, 8, 32))
    rS = np.zeros((T, 8, 2, 32))
    for h in range(RH):
        dq = gamma[h] ** (np.arange(T) + 1.0)
        for u, fac in ((h, dq * RDK ** -0.5), (RH + h, 1.0 / dq)):
            rC[:, u] = np.cos(ang) * fac[:, None]
            rS[:, u, 0] = -np.sin(ang) * fac[:, None]
            rS[:, u, 1] = np.sin(ang) * fac[:, None]
    hi = np.arange(0, DH, 2, dtype=f)
    inv = (1.0 / 10000.0 ** (hi.astype(np.float64) / DH)).astype(f)
    fr = (np.arange(T, dtype=f)[:, None] * inv).astype(np.float64)
    base = (hi.astype(np.float64) + 0.4 * DH) / (1.4 * DH)
    power = (np.arange(T) - T // 2) / float(WINDOW // 2)
    sc = base[None, :] ** power[:, None]
    fC = np.zeros((T, 2, DH))
    fS = np.zeros((T, 2, DH))
    for i, s in ((0, sc * 8.0), (1, 1.0 / sc)):
        fC[:, i] = np.concatenate([np.cos(fr) * s] * 2, -1)
        fS[:, i] = np.concatenate([-np.sin(fr) * s, np.sin(fr) * s], -1)
    inv = (10000.0 ** (-np.arange(0, LDR, 2, dtype=np.float64) / LDR)).astype(f)
    an = (np.arange(T, dtype=f)[:, None] * inv).astype(np.float64)
    lc = np.zeros((32, T))
    ls = np.zeros((32, T))
    lc[0:LDH] = 1.0
    for j in range(LDR // 2):
        lc[LDH + 2 * j] = lc[LDH + 2 * j + 1] = np.cos(an[:, j])
        ls[LDH + 2 * j] = -np.sin(an[:, j])
        ls[LDH + 2 * j + 1] = np.sin(an[:, j])
    by_tile = lambda a: np.ascontiguousarray(a.reshape((NT, P) + a.shape[1:]).swapaxes(0, 1).astype(f))
    return {"w_rC": by_tile(rC), "w_rS": by_tile(rS), "w_fC": by_tile(fC), "w_fS": by_tile(fS),
            "w_lcos": np.tile(lc, (4, 1)).astype(f), "w_lsin": np.tile(ls, (4, 1)).astype(f),
            "zrow": np.zeros((1, P), f)}


def arrange(a):
    ch = lambda w: np.ascontiguousarray(w.reshape((-1, P) + w.shape[1:]).swapaxes(0, 1))
    per = lambda v: np.ascontiguousarray(v.reshape(-1, P).T)
    r = {"x": a["L0_attn_x"]}
    r["w_rWqk"] = ch(np.concatenate([a["L0_attn_Wq"], a["L0_attn_Wk"]], 1))
    r["w_rWv"] = ch(a["L0_attn_Wv"])
    r["w_rWg"] = ch(a["L0_attn_Wg"])
    r["w_rWo"] = ch(a["L0_attn_Wo"])
    r["w_rln"] = np.stack([per(a["L0_attn_ln_w"]), per(a["L0_attn_ln_b"])], 1)
    r["w_rgn"] = a["L0_attn_g_norm_w"].reshape(P, 1)
    r["w_wqkv"] = np.stack([ch(w) for w in a["L0_ffn_wqkv"]], 1)
    r["w_wo"] = np.stack([ch(w) for w in a["L0_ffn_wo"]], 1)
    r["w_ln"] = np.stack([np.stack([per(g), per(b)], 1) for g, b in zip(a["L0_ffn_ln_g"], a["L0_ffn_ln_b"])], 1)
    r["w_w1"] = np.stack([ch(w) for w in a["L0_ffn_w1"]], 1)
    b1 = np.zeros((HCH, DEPTH, 2, NHC), np.float32)
    w2 = np.zeros((HCH, DEPTH, NHC, D), np.float32)
    for l in range(DEPTH):
        for c in range(NHC):
            n = HSZ[c]
            for i in range(2):
                b1[0:n, l, i, c] = a["L0_ffn_b1"][l, i * HID + c * HCH:i * HID + c * HCH + n]
            w2[0:n, l, c] = a["L0_ffn_w2"][l, c * HCH:c * HCH + n]
        w2[HSZ[-1], l, NHC - 1] = a["L0_ffn_b2"][l]
    r["w_b1"], r["w_w2"] = b1, w2
    swap = np.concatenate([np.arange(32, 64), np.arange(0, 32)])
    qs = np.stack([np.stack([a["L0_ffn_q_scale"], a["L0_ffn_k_scale"]], 1),
                   np.stack([a["L0_ffn_q_scale"][:, swap], a["L0_ffn_k_scale"][:, swap]], 1)], 1)
    r["w_qks"] = np.broadcast_to(qs[None], (P,) + qs.shape)
    r["w_lWd"] = np.stack([ch(a["L1_attn_W_DQ"]), ch(a["L1_attn_W_DKV"])], 1)
    wq = np.zeros((LAT, 2, LG, 4, 32), np.float32)
    wk = np.zeros((LAT, LG, 4, 32), np.float32)
    wkr = np.zeros((D, 2, 4, 32), np.float32)
    partner = np.arange(LDR).reshape(-1, 2)[:, ::-1].reshape(-1)
    wq[:, 0, :, :, 0:LDH] = a["L1_attn_W_UQ"].reshape(LAT, LG, 4, LDH)
    qr = a["L1_attn_W_QR"].reshape(LAT, LG, 4, LDR)
    wq[:, 0, :, :, LDH:LDH + LDR] = qr
    wq[:, 1, :, :, LDH:LDH + LDR] = qr[..., partner]
    wk[..., 0:LDH] = a["L1_attn_W_UK"].reshape(LAT, LG, 4, LDH)
    kr = a["L1_attn_W_KR"]
    wkr[:, 0, :, LDH:LDH + LDR] = kr[:, None]
    wkr[:, 1, :, LDH:LDH + LDR] = kr[:, partner][:, None]
    r["w_lWq"] = wq.reshape(LAT, 2, LG, P)
    r["w_lWk"] = wk.reshape(LAT, LG, P)
    r["w_lWkr"] = wkr.reshape(DC, P, 2, P).transpose(1, 2, 0, 3)
    r["w_lWv"] = a["L1_attn_W_UV"]
    r["w_lWo"] = ch(a["L1_attn_W_O"])
    r["w_gw"] = ch(a["L1_ffn_gate_w"])
    r["m_w1"] = np.stack([ch(w) for w in a["L1_ffn_w1"]], 0)
    r["m_w2"] = np.stack([ch(w) for w in a["L1_ffn_w2"]], 0)
    return r


def kernel(**inputs):
    import numpy as _np
    import concourse.bacc as _bacc
    from concourse import mybir as _mybir
    from concourse.bass_utils import run_bass_kernel_spmd as _run

    nc = _bacc.Bacc("TRN2", target_bir_lowering=False, num_devices=1)
    arrays = {**arrange({k: _np.asarray(v) for k, v in inputs.items()}), **tables()}
    arrays = {k: _np.ascontiguousarray(v) for k, v in arrays.items()}
    ins = {k: nc.dram_tensor(f"in_{k}", v.shape, _mybir.dt.from_np(v.dtype), kind="ExternalInput").ap() for k, v in arrays.items()}
    out = nc.dram_tensor("out_0", (B, T, D), F32, kind="ExternalOutput").ap()
    build(nc, ins, out)
    r = _run(nc, [{f"in_{k}": v for k, v in arrays.items()}], core_ids=[0])
    return r.results[0]["out_0"]
```

```python
import concourse.bass as bass
from concourse import mybir
from contextlib import ExitStack
import numpy as np

F32 = mybir.dt.float32
BF16 = mybir.dt.bfloat16
I32 = mybir.dt.int32
ALU = mybir.AluOpType
ACT = mybir.ActivationFunctionType
AX = mybir.AxisListType

P = 128
B, T, D = 8, 512, 256
NT = T // P
DC = D // P
EPS = 1e-5
RH, RDK, RDV = 4, 64, 128
RV = RH * RDV
DEPTH, HEADS, DH, WINDOW = 2, 8, 64, 128
INNER = HEADS * DH
HID = 682
HCH = 120
NHC = 6
HSZ = [min(HCH, HID - HCH * c) for c in range(NHC)]
LH, LDH, LDR, LAT = 16, 16, 8, 64
LG = 4
SQ24 = float(np.sqrt(np.float32(LDH + LDR)))
E, F = 8, 1024
FC = F // P
TOPK = 2
REG = B * T + P
NTILES = (B * T * TOPK + E * (P - 1)) // P + 1
UNROLL = 12
assert NTILES % UNROLL == 0


def act_jobs(l):
    if l == 0:
        j = [("xT", t) for t in range(NT)] + [("zaT", t) for t in range(NT)]
    else:
        j = [("curT", t) for t in range(NT)]
    j += [("v", t) for t in range(NT)]
    for t in range(NT):
        j += [("rv", t)] if l == 0 else []
        j += [("qkT", t)]
    if l == 0:
        j += [("rg", t) for t in range(NT)]
    j += [("S", u) for u in range(2 * NT)]
    if l == 0:
        j += [("rT", t) for t in range(NT)]
        j += [("roT", t) for t in range(NT)]
    j += [("zT", t) for t in range(NT)]
    j += [("g", c) for c in range(NHC)]
    if l == 1:
        j += [("x1T", t) for t in range(NT)]
        j += [("lv", t) for t in range(NT)]
        j += [("av", g) for g in range(LG)]
        j += [("attnT", t) for t in range(NT)]
    return j


def dve_jobs(l):
    j = [("qk", t) for t in range(NT)]
    if l == 0:
        j += [("rqk", t) for t in range(NT)]
    for u in range(1, 2 * NT + 2):
        if u <= 2 * NT:
            j += [("PT", u - 1)]
        if u >= 2:
            j += [("O", u - 2)]
    if l == 0:
        for t in range(NT):
            j += [("AT", t)] + ([("st", t)] if t < NT - 1 else []) + [("ro", t)]
    j += [("wo", t) for t in range(NT)]
    j += [("a", c) for c in range(NHC)]
    j += [("w2", t) for t in range(NT)]
    if l == 0:
        j += [("rout", t) for t in range(NT)]
    else:
        j += [("lat",), ("kr",)] + [("kc", g) for g in range(LG)] + [("lq", g) for g in range(LG)]
        for h in range(LH):
            j += [("s1", h), ("s2", h)]
        j += [("aTM", t) for t in range(NT)]
        j += [("lo", t) for t in range(NT)]
        j += [("rt",), ("rank",)]
    return j


def place(h):
    return 2 * (h % 2) + h // 2


def build(nc, I, O):
    x_d = I["x"].rearrange("b (t p) c -> b p t c", p=P)
    out_d = O.rearrange("b (t p) c -> (b t) p c", p=P)
    scratch = lambda n, s, dt=F32: nc.dram_tensor(n, s, dt, kind="Internal").ap()
    S = {
        "cur": scratch("cur_s", [B, P, NT, D]),
        "s": scratch("s_s", [B, P, NT, D]),
        "x1": scratch("x1_s", [B, P, NT, D]),
        "s2": scratch("s2_s", [B, P, NT, D]),
        "route": scratch("route_s", [B, P, 4, NT]),
        "count": scratch("count_s", [P, E]),
        "rows": scratch("rows_s", [E * REG + P, D]),
        "tile": scratch("tile_s", [P, 3, E]),
        "y": scratch("y_s", [NTILES * P, D]),
    }
    block_layer(nc, I, 0, x_d, S)
    block_layer(nc, I, 1, x_d, S)
    block_moe(nc, I, S)
    block_out(nc, S, out_d)


def block_layer(nc, I, l, x_d, S):
    AJ = {n: i for i, n in enumerate(act_jobs(l))}
    DJ = {n: i for i, n in enumerate(dve_jobs(l))}
    ctx = ExitStack()
    with ctx:
        def sb(name, shape, dt=F32):
            return ctx.enter_context(nc.sbuf_tensor(f"L{l}_{name}", shape, dt))

        def sem(name):
            return ctx.enter_context(nc.semaphore(f"L{l}_{name}"))

        W = {}
        first = (("rWqk", [P, DC, 512]), ("rWv", [P, DC, RV]), ("rWg", [P, DC, RV]), ("rWo", [P, RH, D]),
                 ("rln", [P, 2, DC]), ("rgn", [P, 1]), ("rC", [P, NT, 8, 32]), ("rS", [P, NT, 8, 2, 32]))
        second = (("lWd", [P, 2, DC, LAT]), ("lWq", [LAT, 2, LG, P]), ("lWk", [LAT, LG, P]),
                  ("lWkr", [P, 2, DC, P]), ("lWv", [LAT, LH * LDH]), ("lWo", [P, DC, D]),
                  ("lcos", [P, T]), ("lsin", [P, T]), ("gw", [P, DC, E]))
        layer = (("wqkv", [P, DC, 3 * INNER]), ("wo", [P, 4, D]), ("ln", [P, 2, DC]), ("w1", [P, DC, 2 * HID]),
                 ("b1", [HCH, 2, NHC]), ("w2", [HCH, NHC, D]), ("qks", [P, 2, 2, DH]))
        both = (("fC", [P, NT, 2, DH]), ("fS", [P, NT, 2, DH]))
        source = {}
        for n, shape in (second if l else first) + both + layer:
            W[n] = sb("w_" + n, shape)
            source[n] = I["w_" + n][:, l] if (n, shape) in layer else I["w_" + n]
        Ct = sb("Ct", [P, NT, 2, DH])
        St = sb("St", [P, NT, 2, DH])
        ident = sb("ident", [P, P])
        identb = sb("identb", [P, P], BF16)
        tri = sb("tri", [P, P])
        maskw = sb("maskw", [P, 2, P], BF16)
        half = sb("half", [P, 16])

        x_tm = sb("x_tm", [P, NT, D])
        xn = sb("xn", [P, NT, D])
        cur = sb("cur", [P, NT, D])
        curT = sb("curT", [P, DC, T + 1])
        hB = sb("hB", [P, NT, P])
        z = sb("z", [P, NT, D])
        zT = sb("zT", [P, DC, T])
        stat = sb("stat", [P, NT, 2, 6])
        mv = sb("mv", [P, NT, 2])
        ve = sb("ve", [P, NT])
        rs = sb("rs", [P, NT])
        s_tm = sb("s_tm", [P, NT, D])

        ARENA = 20480 + 2048
        arena = sb("arena", [P, ARENA])
        at = [0]

        def view(n):
            v = arena[:, at[0]:at[0] + n]
            at[0] += n
            assert at[0] <= ARENA, at[0]
            return v

        rqk = view(NT * 512).rearrange("p (t n) -> p t n", t=NT)
        rqkT = view(4 * T).rearrange("p (c n) -> p c n", c=4)
        rv = view(NT * RV).rearrange("p (t n) -> p t n", t=NT)
        gs = view(NT * RV).rearrange("p (t n) -> p t n", t=NT)
        mid = at[0]
        qk = view(NT * 1024).rearrange("p (t n) -> p t n", t=NT)
        qkT = view(8 * T).rearrange("p (c n) -> p c n", c=8)
        v_tm = view(NT * INNER).rearrange("p (t n) -> p t n", t=NT)
        sq = view(2 * 1024).rearrange("p (b n) -> p b n", b=2)
        rot = view(2 * 1024).rearrange("p (b n) -> p b n", b=2)
        prob = qk.rearrange("p t n -> p (t n)")[:, 0:2048].rearrange("p (b n) -> p b n", b=2)
        PT = qk.rearrange("p t n -> p (t n)")[:, 2048:4096].rearrange("p (b n) -> p b n", b=2)
        oT = sq.rearrange("p b n -> p (b n)").rearrange("p (c n) -> p c n", c=4)
        AT = rot.rearrange("p b n -> p (b n)")[:, 0:1024].rearrange("p (b n) -> p b n", b=2)
        o_sb = rot.rearrange("p b n -> p (b n)")[:, 1024:2048].rearrange("p (b n) -> p b n", b=2)
        osq = prob[:, 0, :].rearrange("p (b n) -> p b n", b=2)
        roT = gs.rearrange("p t n -> p (t n)").rearrange("p (c n) -> p c n", c=4)
        rst = sb("rst", [P, NT, 2, RDV])
        hT = qkT.rearrange("p c n -> p (c n)")[:, 0:NHC * T].rearrange("p (c n) -> p c n", c=NHC)
        gl = v_tm.rearrange("p t n -> p (t n)")[:, 0:2 * T].rearrange("p (b n) -> p b n", b=2)
        at[0] = 0
        Pl = view(2 * 4 * 1280).rearrange("p (b h n) -> p b h n", b=2, h=4)
        QT = view(LG * T).rearrange("p (g n) -> p g n", g=LG)
        KT = view(LG * T).rearrange("p (g n) -> p g n", g=LG)
        KrT = view(T)
        rm1 = view(2 * T).rearrange("p (b n) -> p b n", b=2)
        rm2 = view(2 * T).rearrange("p (b n) -> p b n", b=2)
        latT = view(2 * T).rearrange("p (b n) -> p b n", b=2)
        aT = view(LG * T).rearrange("p (g n) -> p g n", g=LG)
        if l:
            Vaug = sb("Vaug", [P, NT, LH, 32])
            iota8 = sb("iota8", [P, NT, E])
            region = sb("region", [P, NT, E])
            before = sb("before", [P, P])
            ones = sb("ones", [P, P])
            zrows = sb("zrows", [P, D])
            counts = sb("counts", [P, NT + 1, E])
            counts_i = sb("counts_i", [P, E], I32)
            route = sb("route", [P, 4, NT])
            rows_i = sb("rows_i", [P, 2 * NT], I32)
            zero_in = sem("zero_in")
        attn = z
        attnT = zT
        s2 = s_tm
        ssq = sb("ssq", [P, NT, 16])
        rinv = sb("rinv", [P, NT, 16])
        mx = sb("mx", [P, 2 * NT, 4])
        rsum = sb("rsum", [P, 2 * NT, 4])
        rrec = sb("rrec", [P, 2 * NT, 4])
        rss = sb("rss", [P, NT, 4])
        rrs = sb("rrs", [P, NT, 4])
        rd = sb("rd", [P, NT, LH])
        rt = sb("rt", [P, 8, NT, E])
        rt1 = sb("rt1", [P, 8, NT])

        pA = [ctx.enter_context(nc.psum_tensor(f"L{l}_pA{i}", [P, 1024], F32)) for i in range(2)]
        pD = [ctx.enter_context(nc.psum_tensor(f"L{l}_pD{i}", [P, 1024], F32)) for i in range(2)]

        loaded = sem("loaded")
        const_p = sem("const_p")
        const_v = sem("const_v")
        per_batch = []

        def bsem(name):
            s = sem(name)
            per_batch.append(s)
            return s

        x_in = bsem("x_in")
        mmA = bsem("mmA")
        outA = bsem("outA")
        mmD = bsem("mmD")
        outD = bsem("outD")
        v_step = bsem("v_step")
        p_step = bsem("p_step")
        a_step = bsem("a_step")
        var_rdy = bsem("var_rdy")
        rstd = bsem("rstd")
        norm = bsem("norm")
        squares = bsem("squares")
        ssq_rdy = bsem("ssq_rdy")
        rinv_rdy = bsem("rinv_rdy")
        qk_rdy = bsem("qk_rdy")
        rqk_rdy = bsem("rqk_rdy")
        mx_rdy = bsem("mx_rdy")
        p_rdy = bsem("p_rdy")
        osq_rdy = bsem("osq_rdy")
        rss_rdy = bsem("rss_rdy")
        rrs_rdy = bsem("rrs_rdy")
        og_rdy = bsem("og_rdy")
        shifted = [bsem(f"shifted{t}") for t in range(NT)]
        fin_silu = bsem("fin_silu")
        x1_rdy = bsem("x1_rdy")
        stores = bsem("stores")
        lq_rdy = bsem("lq_rdy")
        lexp = bsem("lexp")
        masked = bsem("masked")
        chosen = bsem("chosen")
        rows_rdy = bsem("rows_rdy")
        scattered = sem("scattered")
        arrive = bsem("arrive")
        p_const = sem("p_const")
        go = {e: sem("go_" + e) for e in ("pe", "act", "dve", "pool")}
        block = ctx.enter_context(nc.Block())

        names = list(W)

        @block.sync
        def _(sp):
            for n in names:
                sp.dma_start(W[n][:], source[n]).then_inc(loaded, 16)
            sp.wait_ge(const_v, 1)
            if l:
                sp.dma_start(S["rows"][E * REG:E * REG + P, :], zrows[:]).then_inc(zero_in, 16)
            with sp.Fori(0, B) as b:
                sp.dma_start(x_tm[:], x_d[b]).then_inc(x_in, 16)
                if l:
                    sp.dma_start(cur[:], S["cur"][b]).then_inc(x_in, 16)
                    sp.dma_start(s_tm[:], S["s"][b]).then_inc(x_in, 16)
                for t in range(NT):
                    sp.wait_ge(outD, DJ["wo", t] + 1)
                    sp.dma_start(hB[1:P, t, :], cur[0:P - 1, t, P:D]).then_inc(shifted[t], 16)
                    if t == 0:
                        sp.dma_start(hB[0:1, 0, :], I["zrow"]).then_inc(shifted[t], 16)
                    else:
                        sp.dma_start(hB[0:1, t, :], cur[P - 1:P, t - 1, P:D]).then_inc(shifted[t], 16)
                if l == 0:
                    sp.wait_ge(outD, DJ["w2", NT - 1] + 1)
                    sp.dma_start(S["cur"][b], cur[:]).then_inc(stores, 16)
                    sp.wait_ge(outD, DJ["rout", NT - 1] + 1)
                    sp.dma_start(S["s"][b], s_tm[:]).then_inc(stores, 16)
                    sp.wait_ge(stores, 32)
                else:
                    sp.wait_ge(x1_rdy, NT)
                    sp.dma_start(S["x1"][b], x_tm[:]).then_inc(stores, 16)
                    sp.wait_ge(outD, DJ["lo", NT - 1] + 1)
                    sp.dma_start(S["s2"][b], s2[:]).then_inc(stores, 16)
                    sp.wait_ge(outD, DJ["rank",] + 1)
                    sp.dma_start(S["route"][b], route[:]).then_inc(stores, 16)
                    sp.wait_ge(stores, 16 * 3)
                sp.wait_ge(arrive, 4)
                for s in per_batch:
                    sp.sem_clear(s)
                for g in go.values():
                    sp.sem_inc(g, 1)
            if l:
                sp.dma_start(S["count"], counts[:, 0, :]).then_inc(zero_in, 16)
                for e in range(E):
                    end = sp.value_load(counts_i[0:1, e:e + 1], min_val=0, max_val=B * T)
                    sp.dma_start(S["rows"][bass.ds(end + e * REG, P), :], zrows[:]).then_inc(zero_in, 16)
                sp.wait_ge(zero_in, 16 * (E + 2))

        @block.tensor
        def _(pe):
            na, nd = [0], [0]

            def slotA(name):
                k = AJ[name]
                assert k == na[0], (name, k, na[0])
                na[0] += 1
                if k >= 2:
                    pe.wait_ge(outA, k - 1)
                return pA[k % 2]

            def slotD(name):
                k = DJ[name]
                assert k == nd[0], (name, k, nd[0])
                nd[0] += 1
                if k >= 2:
                    pe.wait_ge(outD, k - 1)
                return pD[k % 2]

            def transposes(name, src, chunks):
                ps = slotA(name)
                for c in range(chunks):
                    last = nc.tensor.transpose(ps[:, c * P:(c + 1) * P], src(c), ident[:])
                last.then_inc(mmA, 1)

            def project(out, lhs, rhs, n):
                for c in range(n):
                    last = nc.tensor.matmul(out, lhs(c), rhs(c), start=(c == 0), stop=(c == n - 1))
                return last

            def tile_cols(t):
                return slice(t * P, (t + 1) * P)

            def shifted_lhs(t):
                return lambda c: curT[:, c, t * P + (1 - c):(t + 1) * P + (1 - c)]

            def latent_attention():
                for t in range(NT):
                    pe.wait_ge(norm, 2 * NT + t - NT + 1)
                    transposes(("x1T", t), lambda c: xn[:, t, c * P:(c + 1) * P], DC)
                xT = lambda c: curT[:, c, 1:T + 1]
                pe.wait_ge(outA, AJ["x1T", NT - 1] + 1)
                ps = slotD(("lat",))
                for i in range(2):
                    last = project(ps[0:LAT, i * T:(i + 1) * T], lambda c: W["lWd"][:, i, c, :], xT, DC)
                last.then_inc(mmD, 1)
                ps = slotD(("kr",))
                for i in range(2):
                    last = project(ps[:, i * T:(i + 1) * T], lambda c: W["lWkr"][:, i, c, :], xT, DC)
                last.then_inc(mmD, 1)
                pe.wait_ge(outD, DJ["lat",] + 1)
                for t in range(NT):
                    ps = slotA(("lv", t))
                    nc.tensor.matmul(ps[:, 0:D], latT[0:LAT, 1, tile_cols(t)], W["lWv"][:], start=True, stop=True).then_inc(mmA, 1)
                for g in range(LG):
                    ps = slotD(("kc", g))
                    nc.tensor.matmul(ps[:, 0:T], W["lWk"][:, g, :], latT[0:LAT, 1, :], start=True, stop=True).then_inc(mmD, 1)
                for g in range(LG):
                    ps = slotD(("lq", g))
                    for i in range(2):
                        last = nc.tensor.matmul(ps[:, i * T:(i + 1) * T], W["lWq"][:, i, g, :], latT[0:LAT, 0, :], start=True, stop=True)
                    last.then_inc(mmD, 1)

                def values(g):
                    pe.wait_ge(masked, 4 * g + 4)
                    pe.wait_ge(outA, AJ["lv", NT - 1] + 1)
                    ps = slotA(("av", g))
                    for kt, off in ((0, 0), (1, 512), (2, 1024), (3, 896)):
                        for i in range(4):
                            last = nc.tensor.matmul(ps[32 * i:32 * i + 32, kt * P:T], Vaug[:, kt, 4 * g + i, :],
                                                    Pl[:, g % 2, i, off:off + T - kt * P], start=(kt == 0), stop=(kt == NT - 1))
                    last.then_inc(mmA, 1)

                for g in range(LG):
                    pe.wait_ge(lq_rdy, g + 1)
                    pe.wait_ge(outD, DJ["kc", g] + 1)
                    for i in range(4):
                        r = slice(32 * i, 32 * i + 32)

                        def score(out, kt):
                            return nc.tensor.matmul(out, KT[r, g, tile_cols(kt)], QT[r, g, kt * P:T], start=True, stop=True)
                        ps = slotD(("s1", 4 * g + i))
                        score(ps[:, 0:512], 0)
                        score(ps[:, 512:896], 1)
                        score(ps[:, 896:1024], 3).then_inc(mmD, 1)
                        ps = slotD(("s2", 4 * g + i))
                        score(ps[:, 0:256], 2).then_inc(mmD, 1)
                    if g > 0:
                        values(g - 1)
                values(LG - 1)
                pe.wait_ge(outA, AJ["av", LG - 1] + 1)
                for t in range(NT):
                    ps = slotD(("aTM", t))
                    for g in range(LG):
                        last = nc.tensor.transpose(ps[:, g * P:(g + 1) * P], aT[:, g, tile_cols(t)], ident[:])
                    last.then_inc(mmD, 1)
                for t in range(NT):
                    pe.wait_ge(outD, DJ["aTM", t] + 1)
                    transposes(("attnT", t), lambda c: attn[:, t, c * P:(c + 1) * P], DC)
                for t in range(NT):
                    pe.wait_ge(outA, AJ["attnT", t] + 1)
                    ps = slotD(("lo", t))
                    project(ps[:, 0:D], lambda c: attnT[:, c, tile_cols(t)], lambda c: W["lWo"][:, c, :], DC).then_inc(mmD, 1)
                ps = slotD(("rt",))
                for t in range(NT):
                    last = project(ps[:, t * E:(t + 1) * E], lambda c: curT[:, c, 1 + t * P:1 + (t + 1) * P], lambda c: W["gw"][:, c, :], DC)
                last.then_inc(mmD, 1)
                pe.wait_ge(chosen, 1)
                ps = slotD(("rank",))
                for i, m in enumerate((before, ones)):
                    last = nc.tensor.matmul(ps[:, i * NT * E:(i + 1) * NT * E], m[:], rt[:, 3].rearrange("p t e -> p (t e)"), start=True, stop=True)
                last.then_inc(mmD, 1)

            pe.wait_ge(loaded, 16 * len(names))
            pe.wait_ge(const_v, 1)
            with pe.Fori(0, B):
                for t in range(NT if l else 0):
                    if t == 0:
                        pe.wait_ge(x_in, 48)
                    transposes(("curT", t), lambda c: cur[:, t, c * P:(c + 1) * P], DC)
                for t in range(0 if l else NT):
                    pe.wait_ge(norm, t + 1)
                    transposes(("xT", t), lambda c: xn[:, t, c * P:(c + 1) * P], DC)
                for t in range(0 if l else NT):
                    pe.wait_ge(norm, NT + t + 1)
                    transposes(("zaT", t), lambda c: z[:, t, c * P:(c + 1) * P], DC)
                for t in range(NT):
                    pe.wait_ge(outA, AJ["curT" if l else "xT", t] + 1)
                    ps = slotD(("qk", t))
                    project(ps[:, 0:512], shifted_lhs(t), lambda c: W["wqkv"][:, c, 0:512], DC)
                    project(ps[:, 512:1024], shifted_lhs(t), lambda c: W["wqkv"][:, c, 512:1024], DC).then_inc(mmD, 1)
                    ps = slotA(("v", t))
                    project(ps[:, 0:512], shifted_lhs(t), lambda c: W["wqkv"][:, c, 1024:1536], DC).then_inc(mmA, 1)
                for t in range(NT):
                    if l == 0:
                        zl = lambda c: zT[:, c, tile_cols(t)]
                        pe.wait_ge(outA, AJ["zaT", t] + 1)
                        ps = slotD(("rqk", t))
                        project(ps[:, 0:512], zl, lambda c: W["rWqk"][:, c, :], DC).then_inc(mmD, 1)
                        ps = slotA(("rv", t))
                        project(ps[:, 0:RV], zl, lambda c: W["rWv"][:, c, :], DC).then_inc(mmA, 1)
                    pe.wait_ge(qk_rdy, t + 1)
                    transposes(("qkT", t), lambda c: qk[:, t, c * P:(c + 1) * P], 8)
                if l == 0:
                    for t in range(NT):
                        zl = lambda c: zT[:, c, tile_cols(t)]
                        ps = slotA(("rg", t))
                        project(ps[:, 0:RV], zl, lambda c: W["rWg"][:, c, :], DC).then_inc(mmA, 1)

                for u in range(2 * NT + 2):
                    if u < 2 * NT:
                        t, hh = u // 2, u % 2
                        pe.wait_ge(outA, AJ["qkT", t] + 1)
                        ps = slotA(("S", u))
                        lo = 0 if t else 1
                        for bank in range(2):
                            nc.tensor.matmul(ps[:, bank * 512:(bank + 1) * 512].rearrange("p (h k q) -> p h k q", h=2, k=2)[:, :, lo:2, :],
                                             identb[:], maskw[:, lo:2, :].unsqueeze(1).broadcast_to((P, 2, 2 - lo, P)), start=True, stop=False)
                        for i in range(4):
                            h = 4 * hh + i
                            r = slice(64 * (h % 2), 64 * (h % 2) + 64)
                            last = nc.tensor.matmul(ps[:, place(i) * 256 + lo * P:(place(i) + 1) * 256], qkT[r, h // 2, tile_cols(t)],
                                                    qkT[r, 4 + h // 2, (t - 1 + lo) * P:(t + 1) * P], start=False, stop=(i >= 2))
                        last.then_inc(mmA, 1)
                    if 1 <= u <= 2 * NT:
                        w = u - 1
                        pe.wait_ge(p_rdy, w + 1)
                        ps = slotD(("PT", w))
                        for i in range(4):
                            for k in range(0 if w // 2 else 1, 2):
                                last = nc.tensor.transpose(ps[:, (2 * i + k) * P:(2 * i + k + 1) * P],
                                                           prob[:, w % 2, i * 256 + k * P:i * 256 + (k + 1) * P], ident[:])
                        last.then_inc(mmD, 1)
                    if u >= 2:
                        w = u - 2
                        t, hh = w // 2, w % 2
                        pe.wait_ge(outD, DJ["PT", w] + 1)
                        ps = slotD(("O", w))
                        lo = 0 if t else 1
                        for pr in range(2):
                            for k in range(lo, 2):
                                for i in (2 * pr, 2 * pr + 1):
                                    h = 4 * hh + i
                                    last = nc.tensor.matmul(ps[64 * (i % 2):64 * (i % 2) + 64, pr * P:(pr + 1) * P],
                                                            v_tm[:, t - 1 + k, h * DH:(h + 1) * DH],
                                                            PT[:, w % 2, (2 * place(i) + k) * P:(2 * place(i) + k + 1) * P],
                                                            start=(k == lo), stop=(k == 1))
                        last.then_inc(mmD, 1)

                if l == 0:
                    for t in range(NT):
                        pe.wait_ge(rqk_rdy, t + 1)
                        transposes(("rT", t), lambda c: rqk[:, t, c * P:(c + 1) * P], 4)
                    for t in range(NT):
                        pe.wait_ge(outA, AJ["rT", t] + 1)
                        ps = slotD(("AT", t))
                        for h in range(RH):
                            r = slice(64 * (h % 2), 64 * (h % 2) + 64)
                            last = nc.tensor.matmul(ps[:, (h % 2) * 512 + (h // 2) * P:(h % 2) * 512 + (h // 2 + 1) * P], rqkT[r, 2 + h // 2, tile_cols(t)],
                                                    rqkT[r, h // 2, tile_cols(t)], start=True, stop=True)
                        last.then_inc(mmD, 1)
                        if t < NT - 1:
                            ps = slotD(("st", t))
                            for h in range(RH):
                                last = nc.tensor.matmul(ps[64 * (h % 2):64 * (h % 2) + 64, (h // 2) * RDV:(h // 2 + 1) * RDV],
                                                        rqk[:, t, 256 + h * RDK:256 + (h + 1) * RDK],
                                                        rv[:, t, h * RDV:(h + 1) * RDV], start=True, stop=True)
                            last.then_inc(mmD, 1)
                        pe.wait_ge(outD, DJ["AT", t] + 1)
                        ps = slotD(("ro", t))
                        for h in range(RH):
                            r = slice(64 * (h % 2), 64 * (h % 2) + 64)
                            out = ps[:, (h % 2) * 512 + (h // 2) * RDV:(h % 2) * 512 + (h // 2 + 1) * RDV]
                            last = nc.tensor.matmul(out, AT[:, t % 2, place(h) * P:(place(h) + 1) * P], rv[:, t, h * RDV:(h + 1) * RDV],
                                                    start=True, stop=(t == 0))
                            if t:
                                last = nc.tensor.matmul(out, rqkT[r, h // 2, tile_cols(t)], rst[r, t, h // 2, :],
                                                        start=False, stop=True)
                        last.then_inc(mmD, 1)
                    for t in range(NT):
                        pe.wait_ge(og_rdy, t + 1)
                        transposes(("roT", t), lambda c: rqk[:, t, c * P:(c + 1) * P], 4)

                for t in range(NT):
                    pe.wait_ge(outD, DJ["O", 2 * t + 1] + 1)
                    ps = slotD(("wo", t))
                    project(ps[:, 0:D], lambda c: oT[:, c, tile_cols(t)], lambda c: W["wo"][:, c, :], 4).then_inc(mmD, 1)
                for t in range(NT):
                    pe.wait_ge(norm, (0 if l else 2 * NT) + t + 1)
                    transposes(("zT", t), lambda c: z[:, t, c * P:(c + 1) * P], DC)
                for c in range(NHC):
                    n = HSZ[c]
                    if c == 0:
                        pe.wait_ge(outA, AJ["zT", NT - 1] + 1)
                    ps = slotA(("g", c))
                    project(ps[0:n, 0:T], lambda k: W["w1"][:, k, HID + c * HCH:HID + c * HCH + n], lambda k: zT[:, k, :], DC).then_inc(mmA, 1)
                    ps = slotD(("a", c))
                    project(ps[0:n, 0:T], lambda k: W["w1"][:, k, c * HCH:c * HCH + n], lambda k: zT[:, k, :], DC).then_inc(mmD, 1)
                for t in range(NT):
                    if t == 0:
                        pe.wait_ge(outD, DJ["a", NHC - 1] + 1)
                    ps = slotD(("w2", t))
                    rows = [min(HCH, HSZ[c] + (c == NHC - 1)) for c in range(NHC)]
                    project(ps[:, 0:D], lambda c: hT[0:rows[c], c, tile_cols(t)], lambda c: W["w2"][0:rows[c], c, :], NHC).then_inc(mmD, 1)
                if l == 0:
                    for t in range(NT):
                        pe.wait_ge(outA, AJ["roT", t] + 1)
                        ps = slotD(("rout", t))
                        project(ps[:, 0:D], lambda c: roT[:, c, tile_cols(t)], lambda c: W["rWo"][:, c, :], RH).then_inc(mmD, 1)
                if l:
                    latent_attention()
                pe.sem_inc(arrive, 1)
                pe.wait_ge(go["pe"], 1)
                pe.sem_clear(go["pe"])

        @block.scalar
        def _(act):
            na = [0]

            def take(name):
                k = AJ[name]
                assert k == na[0], (name, k, na[0])
                na[0] += 1
                act.wait_ge(mmA, k + 1)
                return pA[k % 2]

            def scaled(name, t, w):
                ps = take(name)
                for c in range(DC):
                    last = nc.scalar.activation(zT[:, c, t * P:(t + 1) * P], ps[:, c * P:(c + 1) * P], ACT.Identity,
                                                bias=w[:, 1, c:c + 1], scale=w[:, 0, c:c + 1])
                last.then_inc(outA, 1)

            def by_channel(name, t):
                ps = take(name)
                nc.scalar.copy(curT[:, :, 1 + t * P:1 + (t + 1) * P], ps[:, 0:D].rearrange("p (c n) -> p c n", c=DC)).then_inc(outA, 1)

            def latent_attention():
                for t in range(NT):
                    act.wait_ge(outD, DJ["w2", t] + 1)
                    nc.scalar.activation(z[:, t, :], cur[:, t, :], ACT.Silu).then_inc(fin_silu, 1)
                for t in range(NT):
                    by_channel(("x1T", t), t)
                for t in range(NT):
                    ps = take(("lv", t))
                    nc.scalar.copy(Vaug[:, t, :, 0:LDH], ps[:, 0:D].rearrange("p (h d) -> p h d", h=LH)).then_inc(outA, 1)

                def av(g):
                    ps = take(("av", g))
                    nc.scalar.copy(aT[:, g, :], ps[:, 0:T]).then_inc(outA, 1)

                for g in range(LG):
                    for i in range(4):
                        act.wait_ge(outD, DJ["s2", 4 * g + i] + 1)
                        ph = Pl[:, g % 2, i, :]
                        nc.scalar.activation(ph, ph, ACT.Exp, scale=1.0 / SQ24).then_inc(lexp, 1)
                    if g > 0:
                        av(g - 1)
                av(LG - 1)
                for t in range(NT):
                    ps = take(("attnT", t))
                    nc.scalar.copy(attnT[:, :, t * P:(t + 1) * P], ps[:, 0:D].rearrange("p (c n) -> p c n", c=DC)).then_inc(outA, 1)
                act.wait_ge(outD, DJ["rt",] + 1)
                nc.scalar.activation(rt[:, 1], rt[:, 0], ACT.Exp).then_inc(a_step, 1)
                act.wait_ge(a_step, 1)

            act.wait_ge(loaded, 16 * len(names))
            act.wait_ge(const_p, 1)
            with act.Fori(0, B):
                for t in range(NT):
                    by_channel(("curT" if l else "xT", t), t)
                for t in range(0 if l else NT):
                    scaled(("zaT", t), t, W["rln"])
                for t in range(NT):
                    act.wait_ge(mmD, DJ["qk", t] + 1)
                    if t >= 2:
                        act.wait_ge(outD, DJ["qk", t - 2] + 1)
                    nc.scalar.activation(sq[:, t % 2, :], pD[DJ["qk", t] % 2][:], ACT.Square).then_inc(squares, 1)
                    ps = take(("v", t))
                    nc.scalar.copy(v_tm[:, t, :], ps[:, 0:512]).then_inc(outA, 1)
                for t in range(NT):
                    if l == 0:
                        ps = take(("rv", t))
                        nc.scalar.copy(rv[:, t, :], ps[:, 0:512]).then_inc(outA, 1)
                    ps = take(("qkT", t))
                    nc.scalar.copy(qkT[:, :, t * P:(t + 1) * P], ps[:].rearrange("p (c n) -> p c n", c=8)).then_inc(outA, 1)
                if l == 0:
                    for t in range(NT):
                        ps = take(("rg", t))
                        nc.scalar.activation(gs[:, t, :], ps[:, 0:512], ACT.Silu).then_inc(outA, 1)
                for u in range(2 * NT):
                    act.wait_ge(mx_rdy, u + 1)
                    if u >= 2:
                        act.wait_ge(mmD, DJ["PT", u - 2] + 1)
                    ps = take(("S", u))
                    lo = 0 if u // 2 else P
                    for i in range(4):
                        last = nc.scalar.activation(prob[:, u % 2, i * 256 + lo:(i + 1) * 256], ps[:, i * 256 + lo:(i + 1) * 256], ACT.Exp,
                                                    bias=mx[:, u, i:i + 1], accum_out=rsum[:, u, i:i + 1])
                    last.then_inc(outA, 1)
                if l == 0:
                    for t in range(NT):
                        ps = take(("rT", t))
                        nc.scalar.copy(rqkT[:, :, t * P:(t + 1) * P], ps[:, 0:512].rearrange("p (c n) -> p c n", c=4)).then_inc(outA, 1)
                    for t in range(NT):
                        act.wait_ge(outD, DJ["ro", t] + 1)
                        if t >= 2:
                            act.wait_ge(rss_rdy, t - 1)
                        nc.scalar.activation(osq[:, t % 2, :], o_sb[:, t % 2, :], ACT.Square).then_inc(osq_rdy, 1)
                    for t in range(NT):
                        ps = take(("roT", t))
                        act.wait_ge(og_rdy, NT)
                        nc.scalar.copy(roT[:, :, t * P:(t + 1) * P], ps[:, 0:512].rearrange("p (c n) -> p c n", c=4)).then_inc(outA, 1)
                for t in range(NT):
                    scaled(("zT", t), t, W["ln"])
                for c in range(NHC):
                    n = HSZ[c]
                    if c >= 2:
                        act.wait_ge(outD, DJ["a", c - 2] + 1)
                    ps = take(("g", c))
                    nc.scalar.activation(gl[0:n, c % 2, :], ps[0:n, 0:T], ACT.Gelu, bias=W["b1"][0:n, 1, c:c + 1]).then_inc(outA, 1)
                if l:
                    latent_attention()
                act.sem_inc(arrive, 1)
                act.wait_ge(go["act"], 1)
                act.sem_clear(go["act"])

        @block.gpsimd
        def _(pool):
            n = [0]

            def step(ins):
                n[0] += 1
                ins.then_inc(p_const, 1)
                pool.wait_ge(p_const, n[0])

            step(nc.gpsimd.memset(ident[:], 0.0))
            step(nc.gpsimd.affine_select(out=ident[:], in_=ident[:], compare_op=ALU.not_equal, fill=1.0, base=0,
                                         pattern=[[-1, P]], channel_multiplier=1))
            step(nc.gpsimd.tensor_copy(identb[:], ident[:]))
            step(nc.gpsimd.memset(tri[:], 1.0))
            step(nc.gpsimd.affine_select(out=tri[:], in_=tri[:], compare_op=ALU.is_ge, fill=0.0, base=0,
                                         pattern=[[1, P]], channel_multiplier=-1))
            step(nc.gpsimd.memset(maskw[:], 0.0))
            step(nc.gpsimd.affine_select(out=maskw[:, 0, :], in_=maskw[:, 0, :], compare_op=ALU.is_ge, fill=-1e30, base=0,
                                         pattern=[[1, P]], channel_multiplier=-1))
            step(nc.gpsimd.affine_select(out=maskw[:, 1, :], in_=maskw[:, 1, :], compare_op=ALU.is_ge, fill=-1e30, base=0,
                                         pattern=[[-1, P]], channel_multiplier=1))
            step(nc.gpsimd.memset(half[:], -0.5))
            if l:
                for e in range(E):
                    step(nc.gpsimd.memset(iota8[:, :, e:e + 1], float(E - e)))
                    step(nc.gpsimd.memset(region[:, :, e:e + 1], float(e * REG)))
                step(nc.gpsimd.memset(ones[:], 1.0))
                step(nc.gpsimd.memset(zrows[:], 0.0))
                step(nc.gpsimd.memset(counts[:], 0.0))
                step(nc.gpsimd.affine_select(out=before[:], in_=ones[:], compare_op=ALU.is_ge, fill=0.0, base=-1,
                                             pattern=[[1, P]], channel_multiplier=-1))
                step(nc.gpsimd.memset(Vaug[:], 0.0))
                step(nc.gpsimd.memset(Vaug[:, :, :, LDH:LDH + 1], 1.0))
            nc.gpsimd.memset(curT[:, :, 0:1], 0.0).then_inc(const_p, 1)

            def rsqrt_tile(k):
                pool.wait_ge(var_rdy, k + 1)
                t = k % NT
                nc.gpsimd.tensor_tensor(rs[:, t:t + 1], ve[:, t:t + 1], half[:, 0:1], ALU.pow).then_inc(rstd, 1)

            with pool.Fori(0, B) as b:
                for k in range(0 if l else 2 * NT):
                    rsqrt_tile(k)
                for t in range(NT):
                    pool.wait_ge(ssq_rdy, t + 1)
                    nc.gpsimd.tensor_tensor(rinv[:, t, :], ssq[:, t, :], half[:], ALU.pow)
                    nc.gpsimd.tensor_tensor(qk[:, t, :], qk[:, t, :], rot[:, t % 2, :], ALU.add).then_inc(rinv_rdy, 1)
                if l == 0:
                    for t in range(NT):
                        pool.wait_ge(outD, DJ["rqk", t] + 1)
                        nc.gpsimd.tensor_tensor(rqk[:, t, :], rqk[:, t, :], rot[:, t % 2, 0:512], ALU.add).then_inc(rqk_rdy, 1)
                    for t in range(NT):
                        pool.wait_ge(rss_rdy, t + 1)
                        nc.gpsimd.tensor_tensor(rrs[:, t, :], rss[:, t, :], half[:, 0:4], ALU.pow).then_inc(rrs_rdy, 1)
                for t in range(NT):
                    rsqrt_tile((0 if l else 2) * NT + t)
                if l:
                    for t in range(NT):
                        rsqrt_tile(NT + t)
                    for g in range(LG):
                        pool.wait_ge(outD, DJ["lq", g] + 1)
                        nc.gpsimd.tensor_tensor(QT[:, g, :], rm1[:, g % 2, :], rm2[:, g % 2, :], ALU.add).then_inc(lq_rdy, 1)
                    for h in range(LH):
                        pool.wait_ge(lexp, h + 1)
                        ph = Pl[:, (h // 4) % 2, h % 4, :]
                        nc.gpsimd.tensor_tensor(ph[:, 0:P], ph[:, 0:P], tri[:], ALU.mult)
                        nc.gpsimd.tensor_tensor(ph[:, 512:640], ph[:, 512:640], tri[:], ALU.mult)
                        pair = ph[:, 896:1152].rearrange("p (a n) -> p a n", a=2)
                        nc.gpsimd.tensor_tensor(pair, pair, tri[:].unsqueeze(1).broadcast_to((P, 2, P)), ALU.mult).then_inc(masked, 1)
                if l:
                    pool.wait_ge(rows_rdy, 1)
                    for k in range(TOPK):
                        for t in range(NT):
                            nc.gpsimd.indirect_dma_start(out=S["rows"], out_offset=bass.IndirectOffsetOnAxis(ap=rows_i[:, k * NT + t:k * NT + t + 1], axis=0),
                                                         in_=xn[:, t, :], in_offset=None).then_inc(scattered, 16)
                    pool.wait_ge(masked, LH)
                    pool.wait_ge(scattered, b * (16 * TOPK * NT) + 16 * TOPK * NT)
                else:
                    pool.wait_ge(rstd, 3 * NT)
                pool.sem_inc(arrive, 1)
                pool.wait_ge(go["pool"], 1)
                pool.sem_clear(go["pool"])

        @block.vector
        def _(dve):
            nd, ns, nln = [0], [0], [0]

            def take(name):
                k = DJ[name]
                assert k == nd[0], (name, k, nd[0])
                nd[0] += 1
                dve.wait_ge(mmD, k + 1)
                return pD[k % 2]

            def step(ins):
                ns[0] += 1
                ins.then_inc(v_step, 1)
                dve.wait_ge(v_step, ns[0])

            def heads(ap, h):
                return ap.rearrange("p (h d) -> p h d", h=h)

            def per_head(ap, n):
                return ap.unsqueeze(2).broadcast_to((P, ap.shape[1], n))

            def ln_stats(t, parts):
                for i, ap in enumerate(parts):
                    last = nc.vector.bn_stats(stat[:, t, i, :], ap)
                step(last)
                step(nc.vector.bn_aggr(mv[:, t, :], stat[:, t, 0:len(parts), :]))
                nc.vector.tensor_scalar(ve[:, t:t + 1], mv[:, t, 1:2], EPS, None, ALU.add).then_inc(var_rdy, 1)

            def ln_apply(t, parts, out):
                dve.wait_ge(rstd, nln[0] + 1)
                nln[0] += 1
                for i, ap in enumerate(parts):
                    n = D // len(parts)
                    last = nc.vector.tensor_scalar(out[:, t, i * n:(i + 1) * n], ap, mv[:, t, 0:1], rs[:, t:t + 1], ALU.subtract, ALU.mult)
                last.then_inc(norm, 1)

            def latent_attention():
                for t in range(NT):
                    dve.wait_ge(fin_silu, t + 1)
                    step(nc.vector.tensor_tensor(z[:, t, :], z[:, t, :], s_tm[:, t, :], ALU.mult))
                    nc.vector.tensor_tensor(x_tm[:, t, :], x_tm[:, t, :], z[:, t, :], ALU.add).then_inc(x1_rdy, 1)
                    dve.wait_ge(x1_rdy, t + 1)
                    ln_stats(t, [x_tm[:, t, :]])
                for t in range(NT):
                    ln_apply(t, [x_tm[:, t, :]], xn)

                ps = take(("lat",))
                nc.vector.tensor_copy(latT[0:LAT], ps[0:LAT, :].rearrange("p (a n) -> p a n", a=2)).then_inc(outD, 1)
                ps = take(("kr",))
                nc.vector.tensor_tensor(rm1[:, 0, :], ps[:, 0:T], W["lcos"][:], ALU.mult)
                nc.vector.tensor_tensor(rm2[:, 0, :], ps[:, T:2 * T], W["lsin"][:], ALU.mult).then_inc(outD, 1)
                dve.wait_ge(outD, DJ["kr",] + 1)
                step(nc.vector.tensor_tensor(KrT, rm1[:, 0, :], rm2[:, 0, :], ALU.add))
                for g in range(LG):
                    ps = take(("kc", g))
                    nc.vector.tensor_tensor(KT[:, g, :], ps[:, 0:T], KrT, ALU.add).then_inc(outD, 1)
                for g in range(LG):
                    ps = take(("lq", g))
                    if g >= 2:
                        dve.wait_ge(lq_rdy, g - 1)
                    nc.vector.tensor_tensor(rm1[:, g % 2, :], ps[:, 0:T], W["lcos"][:], ALU.mult)
                    nc.vector.tensor_tensor(rm2[:, g % 2, :], ps[:, T:2 * T], W["lsin"][:], ALU.mult).then_inc(outD, 1)
                for h in range(LH):
                    g = h // 4
                    if g >= 2 and h % 4 == 0:
                        dve.wait_ge(mmA, AJ["av", g - 2] + 1)
                    ph = Pl[:, g % 2, h % 4, :]
                    ps = take(("s1", h))
                    nc.vector.tensor_scalar(ph[:, 0:1024], ps[:], 80.0, -80.0, ALU.min, ALU.max).then_inc(outD, 1)
                    ps = take(("s2", h))
                    nc.vector.tensor_scalar(ph[:, 1024:1280], ps[:, 0:256], 80.0, -80.0, ALU.min, ALU.max).then_inc(outD, 1)
                for t in range(NT):
                    ps = take(("aTM", t))
                    pv = ps[:, 0:512].rearrange("p (h d) -> p h d", h=LH)
                    step(nc.vector.reciprocal(rd[:, t, :], pv[:, :, LDH]))
                    nc.vector.tensor_tensor(heads(attn[:, t, :], LH), pv[:, :, 0:LDH], per_head(rd[:, t, :], LDH), ALU.mult).then_inc(outD, 1)
                for t in range(NT):
                    ps = take(("lo", t))
                    nc.vector.tensor_copy(s2[:, t, :], ps[:, 0:D]).then_inc(outD, 1)

                ps = take(("rt",))
                lg = ps[:, 0:NT * E].rearrange("p (t e) -> p t e", t=NT)
                wide = lambda ap: ap.unsqueeze(2).broadcast_to((P, NT, E))
                step(nc.vector.tensor_reduce(rt1[:, 0], lg, AX.X, ALU.max))
                nc.vector.tensor_tensor(rt[:, 0], lg, wide(rt1[:, 0]), ALU.subtract).then_inc(outD, 1)
                dve.wait_ge(a_step, 1)
                step(nc.vector.tensor_reduce(rt1[:, 1], rt[:, 1], AX.X, ALU.add))
                step(nc.vector.reciprocal(rt1[:, 2], rt1[:, 1]))
                step(nc.vector.tensor_tensor(rt[:, 2], rt[:, 1], wide(rt1[:, 2]), ALU.mult))
                for k in range(TOPK):
                    best = rt1[:, 3 + k]
                    step(nc.vector.tensor_reduce(best, rt[:, 2], AX.X, ALU.max))
                    step(nc.vector.tensor_tensor(rt[:, 3], rt[:, 2], wide(best), ALU.is_equal))
                    step(nc.vector.tensor_tensor(rt[:, 4], rt[:, 3], iota8[:], ALU.mult))
                    step(nc.vector.tensor_reduce(rt1[:, 5], rt[:, 4], AX.X, ALU.max))
                    step(nc.vector.tensor_tensor(rt[:, 5 + k], iota8[:], wide(rt1[:, 5]), ALU.is_equal))
                    if k == 0:
                        step(nc.vector.scalar_tensor_tensor(out=rt[:, 2], in0=rt[:, 5], scalar=-4.0, in1=rt[:, 2], op0=ALU.mult, op1=ALU.add))
                nc.vector.tensor_tensor(rt[:, 3], rt[:, 5], rt[:, 6], ALU.add).then_inc(chosen, 1)
                step(nc.vector.tensor_tensor(rt1[:, 6], rt1[:, 3], rt1[:, 4], ALU.add))
                step(nc.vector.reciprocal(rt1[:, 7], rt1[:, 6]))
                step(nc.vector.tensor_tensor(route[:, 2:4, :], rt1[:, 3:5], rt1[:, 7:8].broadcast_to((P, 2, NT)), ALU.mult))
                ps = take(("rank",))
                rank = ps[:, 0:NT * E].rearrange("p (t e) -> p t e", t=NT)
                total = ps[:, NT * E:2 * NT * E].rearrange("p (t e) -> p t e", t=NT)
                for t in range(NT):
                    step(nc.vector.tensor_tensor(counts[:, t + 1], total[:, t], counts[:, t], ALU.add))
                step(nc.vector.tensor_tensor(rt[:, 1], rank, counts[:, 0:NT], ALU.add))
                step(nc.vector.tensor_tensor(rt[:, 2], rt[:, 1], region[:], ALU.add))
                for k in range(TOPK):
                    step(nc.vector.tensor_tensor(rt[:, 4], rt[:, 2], rt[:, 5 + k], ALU.mult))
                    step(nc.vector.tensor_reduce(route[:, k, :], rt[:, 4], AX.X, ALU.add))
                nc.vector.tensor_copy(rows_i[:], route[:, 0:2, :].rearrange("p k t -> p (k t)")).then_inc(rows_rdy, 1)
                step(nc.vector.tensor_copy(counts[:, 0], counts[:, NT]))
                nc.vector.tensor_copy(counts_i[:], counts[:, 0]).then_inc(outD, 1)
                dve.wait_ge(outD, DJ["rank",] + 1)

            dve.wait_ge(loaded, 16 * len(names))
            dve.wait_ge(const_p, 1)
            for t in range(NT):
                nc.vector.tensor_tensor(Ct[:, t], W["fC"][:, t], W["qks"][:, 0], ALU.mult)
                last = nc.vector.tensor_tensor(St[:, t], W["fS"][:, t], W["qks"][:, 1], ALU.mult)
            if l == 0:
                last = nc.vector.tensor_scalar(W["rWo"][:], W["rWo"][:], W["rgn"][:, 0:1], None, ALU.mult)
            last.then_inc(const_v, 1)
            dve.wait_ge(const_v, 1)

            with dve.Fori(0, B):
                dve.wait_ge(x_in, 48 if l else 16)
                for t in range(0 if l else NT):
                    ln_stats(t, [x_tm[:, t, :]])
                for t in range(0 if l else NT):
                    ln_apply(t, [x_tm[:, t, :]], xn)
                for t in range(0 if l else NT):
                    dve.wait_ge(norm, t + 1)
                    ln_stats(t, [xn[:, t, :]])
                for t in range(0 if l else NT):
                    ln_apply(t, [xn[:, t, :]], z)

                stream = xn if l == 0 else cur
                def scale_qk(t):
                    dve.wait_ge(rinv_rdy, t + 1)
                    nc.vector.tensor_tensor(heads(qk[:, t, :], 16), heads(qk[:, t, :], 16), per_head(rinv[:, t, :], DH), ALU.mult).then_inc(qk_rdy, 1)

                for t in range(NT):
                    ps = take(("qk", t))
                    pv = ps[:].rearrange("p (a h d) -> p a h d", a=2, h=8)
                    o1 = qk[:, t, :].rearrange("p (a h d) -> p a h d", a=2, h=8)
                    o2 = rot[:, t % 2, :].rearrange("p (a h d) -> p a h d", a=2, h=8)
                    if t >= 2:
                        dve.wait_ge(rinv_rdy, t - 1)
                    dve.wait_ge(squares, t + 1)
                    nc.vector.tensor_tensor(o1, pv, Ct[:, t].unsqueeze(2).broadcast_to((P, 2, 8, DH)), ALU.mult)
                    for s in range(2):
                        a, b = slice(32 * s, 32 * s + 32), slice(32 * (1 - s), 32 * (1 - s) + 32)
                        nc.vector.tensor_tensor(o2[:, :, :, a], pv[:, :, :, b], St[:, t, :, a].unsqueeze(2).broadcast_to((P, 2, 8, 32)), ALU.mult)
                    nc.vector.tensor_reduce(ssq[:, t, :], heads(sq[:, t % 2, :], 16), AX.X, ALU.add).then_inc(outD, 1)
                    dve.wait_ge(outD, DJ["qk", t] + 1)
                    nc.vector.tensor_scalar(ssq[:, t, :], ssq[:, t, :], 1e-24, None, ALU.max).then_inc(ssq_rdy, 1)
                    if t:
                        scale_qk(t - 1)
                scale_qk(NT - 1)
                if l == 0:
                    for t in range(NT):
                        ps = take(("rqk", t))
                        pv = ps[:, 0:512].rearrange("p (h a d) -> p h a d", h=8, a=2)
                        o1 = rqk[:, t, :].rearrange("p (h a d) -> p h a d", h=8, a=2)
                        o2 = rot[:, t % 2, 0:512].rearrange("p (h a d) -> p h a d", h=8, a=2)
                        if t >= 2:
                            dve.wait_ge(rqk_rdy, t - 1)
                        elif t == 0:
                            dve.wait_ge(rinv_rdy, NT)
                        nc.vector.tensor_tensor(o1, pv, W["rC"][:, t].unsqueeze(2).broadcast_to((P, 8, 2, 32)), ALU.mult)
                        nc.vector.tensor_tensor(o2[:, :, 0, :], pv[:, :, 1, :], W["rS"][:, t, :, 0, :], ALU.mult)
                        nc.vector.tensor_tensor(o2[:, :, 1, :], pv[:, :, 0, :], W["rS"][:, t, :, 1, :], ALU.mult).then_inc(outD, 1)

                for u in range(2 * NT + 2):
                    if u < 2 * NT:
                        dve.wait_ge(mmA, AJ["S", u] + 1)
                        lo = 0 if u // 2 else P
                        nc.vector.tensor_reduce(mx[:, u, :], heads(pA[AJ["S", u] % 2][:], 4)[:, :, lo:256], AX.X, ALU.max, negate=True).then_inc(mx_rdy, 1)
                    if 1 <= u <= 2 * NT:
                        w = u - 1
                        lo = 0 if w // 2 else P
                        dve.wait_ge(outA, AJ["S", w] + 1)
                        step(nc.vector.reciprocal(rrec[:, w, :], rsum[:, w, :]))
                        pv = heads(prob[:, w % 2, :], 4)[:, :, lo:256]
                        nc.vector.tensor_tensor(pv, pv, per_head(rrec[:, w, :], 256 - lo), ALU.mult).then_inc(p_rdy, 1)
                        ps = take(("PT", w))
                        k = lo // P
                        if w >= 2:
                            dve.wait_ge(mmD, DJ["O", w - 2] + 1)
                        nc.vector.tensor_copy(PT[:, w % 2, :].rearrange("p (h k q) -> p h k q", h=4, k=2)[:, :, k:2, :],
                                              ps[:].rearrange("p (h k q) -> p h k q", h=4, k=2)[:, :, k:2, :]).then_inc(outD, 1)
                    if u >= 2:
                        w = u - 2
                        t, hh = w // 2, w % 2
                        ps = take(("O", w))
                        nc.vector.tensor_copy(oT[:, 2 * hh:2 * hh + 2, t * P:(t + 1) * P], ps[:, 0:256].rearrange("p (c n) -> p c n", c=2)).then_inc(outD, 1)

                if l == 0:
                    def gate(t):
                        dve.wait_ge(rrs_rdy, t + 1)
                        o = heads(rqk[:, t, :], 4)
                        step(nc.vector.tensor_tensor(o, heads(o_sb[:, t % 2, :], 4), per_head(rrs[:, t, :], RDV), ALU.mult))
                        nc.vector.tensor_tensor(rqk[:, t, :], rqk[:, t, :], gs[:, t, :], ALU.mult).then_inc(og_rdy, 1)
                    for t in range(NT):
                        ps = take(("AT", t))
                        nc.vector.tensor_tensor(AT[:, t % 2, :].rearrange("p (b a n) -> p b a n", b=2, a=2),
                                                ps[:].rearrange("p (b n) -> p b n", b=2)[:, :, 0:2 * P].rearrange("p b (a n) -> p b a n", a=2),
                                                tri[:].unsqueeze(1).unsqueeze(1).broadcast_to((P, 2, 2, P)), ALU.mult).then_inc(outD, 1)
                        if t < NT - 1:
                            ps = take(("st", t))
                            pv = ps[:, 0:256].rearrange("p (a n) -> p a n", a=2)
                            if t == 0:
                                nc.vector.tensor_copy(rst[:, 1], pv).then_inc(outD, 1)
                            else:
                                nc.vector.tensor_tensor(rst[:, t + 1], pv, rst[:, t], ALU.add).then_inc(outD, 1)
                        ps = take(("ro", t))
                        if t >= 2:
                            dve.wait_ge(og_rdy, t - 1)
                        nc.vector.tensor_copy(o_sb[:, t % 2, :].rearrange("p (a b n) -> p b a n", a=2, b=2),
                                              ps[:].rearrange("p (b n) -> p b n", b=2)[:, :, 0:2 * P].rearrange("p b (a n) -> p b a n", a=2)).then_inc(outD, 1)
                        dve.wait_ge(osq_rdy, t + 1)
                        step(nc.vector.tensor_reduce(rss[:, t, :], heads(osq[:, t % 2, :], 4), AX.X, ALU.add))
                        nc.vector.tensor_scalar(rss[:, t, :], rss[:, t, :], 1.0 / RDV, EPS, ALU.mult, ALU.add).then_inc(rss_rdy, 1)
                        if t:
                            gate(t - 1)
                    gate(NT - 1)

                parts = lambda t: [cur[:, t, 0:P], hB[:, t, :]]
                for t in range(NT):
                    ps = take(("wo", t))
                    nc.vector.tensor_tensor(cur[:, t, :], ps[:, 0:D], stream[:, t, :], ALU.add).then_inc(outD, 1)
                for t in range(NT):
                    dve.wait_ge(shifted[t], 32)
                    ln_stats(t, parts(t))
                for t in range(NT):
                    ln_apply(t, parts(t), z)
                step(nc.vector.memset(hT[64:HCH, NHC - 1, :], 1.0))
                for c in range(NHC):
                    n = HSZ[c]
                    ps = take(("a", c))
                    dve.wait_ge(outA, AJ["g", c] + 1)
                    nc.vector.scalar_tensor_tensor(out=hT[0:n, c, :], in0=ps[0:n, 0:T], scalar=W["b1"][0:n, 0, c:c + 1], in1=gl[0:n, c % 2, :],
                                                   op0=ALU.add, op1=ALU.mult).then_inc(outD, 1)
                for t in range(NT):
                    ps = take(("w2", t))
                    nc.vector.tensor_tensor(cur[:, t, :], ps[:, 0:D], cur[:, t, :], ALU.add).then_inc(outD, 1)
                if l == 0:
                    for t in range(NT):
                        ps = take(("rout", t))
                        nc.vector.tensor_tensor(s_tm[:, t, :], ps[:, 0:D], xn[:, t, :], ALU.add).then_inc(outD, 1)
                if l:
                    latent_attention()
                dve.sem_inc(arrive, 1)
                dve.wait_ge(go["dve"], 1)
                dve.sem_clear(go["dve"])


def block_moe(nc, I, S):
    ctx = ExitStack()
    with ctx:
        def sb(name, shape, dt=F32):
            return ctx.enter_context(nc.sbuf_tensor("m_" + name, shape, dt))

        def sem(name):
            return ctx.enter_context(nc.semaphore("m_" + name))
        w1 = sb("w1", [P, E, DC, F])
        w2 = sb("w2", [P, E, FC, D])
        ident = sb("ident", [P, P])
        xin = sb("xin", [P, UNROLL, D])
        xT = sb("xT", [P, 2, DC, P])
        h = sb("h", [P, 2, F])
        hT = sb("hT", [P, 2, F])
        y = sb("y", [P, 2, D])
        cnt = sb("cnt", [P, E])
        k128 = sb("k128", [P, B * T // P])
        full = sb("full", [P, E, B * T // P])
        tl = sb("tl", [P, E])
        end = sb("end", [P, E + 1])
        jot = sb("jot", [P, NTILES])
        past = sb("past", [P, NTILES, E])
        tmp = sb("tmp", [P, NTILES, E])
        ex = sb("ex", [P, NTILES])
        start = sb("start", [P, NTILES])
        row = sb("row", [P, 2, NTILES])
        ex_i = sb("ex_i", [P, NTILES], I32)
        row_i = sb("row_i", [P, NTILES], I32)
        shift = sb("shift", [P, 3, E])
        ph = [ctx.enter_context(nc.psum_tensor(f"m_ph{i}", [P, F], F32)) for i in range(2)]
        pt = ctx.enter_context(nc.psum_tensor("m_pt", [P, F], F32))
        px = ctx.enter_context(nc.psum_tensor("m_px", [P, 512], F32))
        py = ctx.enter_context(nc.psum_tensor("m_py", [P, 512], F32))
        wl = sem("wl")
        cl = sem("cl")
        const = sem("const")
        p_const = sem("p_const")
        v_step = sem("v_step")
        table = sem("table")
        t_out = sem("t_out")
        per_loop = []

        def bsem(name):
            s = sem(name)
            per_loop.append(s)
            return s
        xl = [bsem(f"xl{u}") for u in range(UNROLL)]
        xt = bsem("xt")
        xtc = bsem("xtc")
        up = bsem("up")
        gel = bsem("gel")
        tr = bsem("tr")
        trc = bsem("trc")
        dn = bsem("dn")
        yc = bsem("yc")
        st = [bsem(f"st{i}") for i in range(2)]
        arrive = bsem("arrive")
        go = {e: sem("go_" + e) for e in ("pe", "act", "dve")}
        block = ctx.enter_context(nc.Block())
        NK = B * T // P

        @block.gpsimd
        def _(pool):
            n = [0]

            def step(ins):
                n[0] += 1
                ins.then_inc(p_const, 1)
                pool.wait_ge(p_const, n[0])
            step(nc.gpsimd.memset(ident[:], 0.0))
            step(nc.gpsimd.affine_select(out=ident[:], in_=ident[:], compare_op=ALU.not_equal, fill=1.0, base=0,
                                         pattern=[[-1, P]], channel_multiplier=1))
            step(nc.gpsimd.iota(k128[:], [[P, NK]], base=0, channel_multiplier=0, allow_small_or_imprecise_dtypes=True))
            step(nc.gpsimd.iota(shift[:, 1], [[REG, E]], base=0, channel_multiplier=0, allow_small_or_imprecise_dtypes=True))
            nc.gpsimd.iota(jot[:], [[1, NTILES]], base=0, channel_multiplier=0, allow_small_or_imprecise_dtypes=True).then_inc(const, 1)

        @block.sync
        def _(sp):
            sp.dma_start(cnt[:], S["count"]).then_inc(cl, 16)
            for e in range(E):
                sp.dma_start(w1[:, e], I["m_w1"][e]).then_inc(wl, 16)
                sp.dma_start(w2[:, e], I["m_w2"][e]).then_inc(wl, 16)
            sp.wait_ge(table, 1)
            sp.dma_start(S["tile"], shift[:]).then_inc(t_out, 16)
            with sp.Fori(0, NTILES // UNROLL) as it:
                for u in range(UNROLL):
                    r = sp.value_load(row_i[0:1, bass.ds(it * UNROLL + u, 1)], min_val=0, max_val=E * REG)
                    sp.dma_start(xin[:, u, :], S["rows"][bass.ds(r, P), :]).then_inc(xl[u], 16)
                for u in range(UNROLL):
                    sp.wait_ge(yc, u + 1)
                    sp.dma_start(S["y"][bass.ds((it * UNROLL + u) * P, P), :], y[:, u % 2, :]).then_inc(st[u % 2], 16)
                for i in range(2):
                    sp.wait_ge(st[i], 16 * UNROLL // 2)
                sp.wait_ge(arrive, 3)
                for s in per_loop:
                    sp.sem_clear(s)
                for g in go.values():
                    sp.sem_inc(g, 1)
            sp.wait_ge(t_out, 16)

        @block.tensor
        def _(pe):
            pe.wait_ge(wl, 32 * E)
            pe.wait_ge(const, 1)
            pe.wait_ge(table, 1)
            with pe.Fori(0, NTILES // UNROLL) as it:
                e = [None] * UNROLL

                def transpose_x(u):
                    pe.wait_ge(xl[u], 16)
                    if u >= 1:
                        pe.wait_ge(xtc, u)
                    for c in range(DC):
                        last = nc.tensor.transpose(px[:, c * P:(c + 1) * P], xin[:, u, c * P:(c + 1) * P], ident[:])
                    last.then_inc(xt, 1)
                transpose_x(0)
                for u in range(UNROLL + 2):
                    if u < UNROLL:
                        e[u] = pe.value_load(ex_i[0:1, bass.ds(it * UNROLL + u, 1)], min_val=0, max_val=E - 1)
                        pe.wait_ge(xtc, u + 1)
                        if u >= 2:
                            pe.wait_ge(gel, u - 1)
                        for c in range(DC):
                            for n in range(2):
                                last = nc.tensor.matmul(ph[u % 2][:, n * 512:(n + 1) * 512], xT[:, u % 2, c, :],
                                                        w1[:, bass.ds(e[u], 1), c, n * 512:(n + 1) * 512],
                                                        start=(c == 0), stop=(c == DC - 1))
                        last.then_inc(up, 1)
                    if u + 1 < UNROLL:
                        transpose_x(u + 1)
                    if 1 <= u <= UNROLL:
                        w = u - 1
                        pe.wait_ge(gel, w + 1)
                        if w >= 1:
                            pe.wait_ge(trc, w)
                        for c in range(FC):
                            last = nc.tensor.transpose(pt[:, c * P:(c + 1) * P], h[:, w % 2, c * P:(c + 1) * P], ident[:])
                        last.then_inc(tr, 1)
                    if u >= 2:
                        w = u - 2
                        pe.wait_ge(trc, w + 1)
                        if w >= 1:
                            pe.wait_ge(yc, w)
                        for c in range(FC):
                            last = nc.tensor.matmul(py[:, 0:D], hT[:, w % 2, c * P:(c + 1) * P], w2[:, bass.ds(e[w], 1), c, :],
                                                    start=(c == 0), stop=(c == FC - 1))
                        last.then_inc(dn, 1)
                pe.sem_inc(arrive, 1)
                pe.wait_ge(go["pe"], 1)
                pe.sem_clear(go["pe"])

        @block.scalar
        def _(act):
            with act.Fori(0, NTILES // UNROLL):
                for u in range(UNROLL + 2):
                    if u < UNROLL:
                        act.wait_ge(up, u + 1)
                        if u >= 2:
                            act.wait_ge(tr, u - 1)
                        nc.scalar.activation(h[:, u % 2, :], ph[u % 2][:], ACT.Gelu).then_inc(gel, 1)
                    if u >= 2:
                        w = u - 2
                        act.wait_ge(dn, w + 1)
                        if w >= 2:
                            act.wait_ge(st[w % 2], 16 * (w // 2))
                        nc.scalar.copy(y[:, w % 2, :], py[:, 0:D]).then_inc(yc, 1)
                act.wait_ge(yc, UNROLL)
                act.sem_inc(arrive, 1)
                act.wait_ge(go["act"], 1)
                act.sem_clear(go["act"])

        @block.vector
        def _(dve):
            n = [0]

            def step(ins):
                n[0] += 1
                ins.then_inc(v_step, 1)
                dve.wait_ge(v_step, n[0])
            by_expert = lambda ap: ap.unsqueeze(1).broadcast_to((P, NTILES, E))
            dve.wait_ge(const, 1)
            dve.wait_ge(cl, 16)
            step(nc.vector.tensor_tensor(full[:], cnt[:].unsqueeze(2).broadcast_to((P, E, NK)), k128[:].unsqueeze(1).broadcast_to((P, E, NK)), ALU.is_gt))
            step(nc.vector.tensor_reduce(tl[:], full[:], AX.X, ALU.add))
            step(nc.vector.memset(end[:, 0:1], 0.0))
            for e in range(E):
                step(nc.vector.tensor_tensor(end[:, e + 1:e + 2], end[:, e:e + 1], tl[:, e:e + 1], ALU.add))
            step(nc.vector.tensor_tensor(past[:], jot[:].unsqueeze(2).broadcast_to((P, NTILES, E)), by_expert(end[:, 1:E + 1]), ALU.is_ge))
            step(nc.vector.tensor_reduce(ex[:], past[:], AX.X, ALU.add))
            step(nc.vector.tensor_tensor(tmp[:], past[:], by_expert(tl[:]), ALU.mult))
            step(nc.vector.tensor_reduce(start[:], tmp[:], AX.X, ALU.add))
            step(nc.vector.tensor_tensor(start[:], jot[:], start[:], ALU.subtract))
            step(nc.vector.tensor_scalar(row[:, 0], ex[:], float(REG), None, ALU.mult))
            step(nc.vector.scalar_tensor_tensor(out=row[:, 1], in0=start[:], scalar=float(P), in1=row[:, 0], op0=ALU.mult, op1=ALU.add))
            step(nc.vector.tensor_scalar(row_i[:], row[:, 1], float(E * REG), None, ALU.min))
            step(nc.vector.tensor_scalar(ex_i[:], ex[:], float(E - 1), None, ALU.min))
            step(nc.vector.tensor_scalar(shift[:, 2], end[:, 0:E], float(P), None, ALU.mult))
            nc.vector.tensor_tensor(shift[:, 0], shift[:, 2], shift[:, 1], ALU.subtract).then_inc(table, 1)
            with dve.Fori(0, NTILES // UNROLL):
                for u in range(UNROLL + 1):
                    if u < UNROLL:
                        dve.wait_ge(xt, u + 1)
                        if u >= 2:
                            dve.wait_ge(up, u - 1)
                        nc.vector.tensor_copy(xT[:, u % 2, :, :].rearrange("p c n -> p (c n)"), px[:, 0:D]).then_inc(xtc, 1)
                    if u >= 1:
                        w = u - 1
                        dve.wait_ge(tr, w + 1)
                        if w >= 2:
                            dve.wait_ge(dn, w - 1)
                        nc.vector.tensor_copy(hT[:, w % 2, :], pt[:]).then_inc(trc, 1)
                dve.wait_ge(trc, UNROLL)
                dve.sem_inc(arrive, 1)
                dve.wait_ge(go["dve"], 1)
                dve.sem_clear(go["dve"])


def block_out(nc, S, out_d):
    ctx = ExitStack()
    with ctx:
        def sb(name, shape, dt=F32):
            return ctx.enter_context(nc.sbuf_tensor("o_" + name, shape, dt))

        def sem(name):
            return ctx.enter_context(nc.semaphore("o_" + name))
        NB = 2
        yk = [sb(f"y{b}", [P, TOPK, NT, D]) for b in range(B)]
        s = [sb(f"s{i}", [P, NT, D]) for i in range(NB)]
        x = [sb(f"x{i}", [P, NT, D]) for i in range(NB)]
        gated = [sb(f"g{i}", [P, NT, D]) for i in range(NB)]
        shift = sb("shift", [P, 3, E])
        route = sb("route", [P, B, 4, NT])
        rows = sb("rows", [P, B, 2 * NT])
        over = sb("over", [P, B, 2 * NT])
        step_e = sb("step_e", [P, E])
        rows_i = sb("rows_i", [P, B, 2 * NT], I32)
        fetched = [sem(f"in{b}") for b in range(B)]
        gathered = [sem(f"gath{b}") for b in range(B)]
        tables_in = sem("tables_in")
        v_step = sem("v_step")
        rows_rdy = sem("rows_rdy")
        mixed = sem("mixed")
        gate = sem("gate")
        sums = sem("sum")
        stored = [sem(f"st{i}") for i in range(NB)]
        block = ctx.enter_context(nc.Block())
        out_v = out_d.rearrange("(b t) p c -> b p t c", t=NT)

        @block.sync
        def _(sp):
            sp.dma_start(shift[:], S["tile"]).then_inc(tables_in, 16)
            sp.dma_start(route[:], S["route"].rearrange("b p k t -> p b k t")).then_inc(tables_in, 16)
            for b in range(B + NB):
                if b >= NB:
                    sp.wait_ge(sums, b - NB + 1)
                    sp.dma_start(out_v[b - NB], x[b % NB][:]).then_inc(stored[b % NB], 16)
                if b < B:
                    if b >= NB:
                        sp.wait_ge(stored[b % NB], 16 * (b // NB))
                    sp.dma_start(s[b % NB][:], S["s2"][b]).then_inc(fetched[b], 16)
                    sp.dma_start(x[b % NB][:], S["x1"][b]).then_inc(fetched[b], 16)
            for i in range(NB):
                sp.wait_ge(stored[i], 16 * B // NB)

        @block.gpsimd
        def _(pool):
            pool.wait_ge(rows_rdy, 1)
            for b in range(B):
                for k in range(TOPK):
                    for t in range(NT):
                        nc.gpsimd.indirect_dma_start(out=yk[b][:, k, t, :], out_offset=None, in_=S["y"],
                                                     in_offset=bass.IndirectOffsetOnAxis(ap=rows_i[:, b, k * NT + t:k * NT + t + 1], axis=0))\
                            .then_inc(gathered[b], 16)

        @block.scalar
        def _(act):
            for b in range(B):
                act.wait_ge(mixed, b + 1)
                nc.scalar.activation(gated[b % NB][:], yk[b][:, 0], ACT.Silu).then_inc(gate, 1)

        @block.vector
        def _(dve):
            n = [0]

            def step(ins):
                n[0] += 1
                ins.then_inc(v_step, 1)
                dve.wait_ge(v_step, n[0])
            dve.wait_ge(tables_in, 32)
            step(nc.vector.tensor_tensor(step_e[:, 1:E], shift[:, 0, 1:E], shift[:, 0, 0:E - 1], ALU.subtract))
            step(nc.vector.tensor_scalar(rows[:], route[:, :, 0:2, :].rearrange("p b k t -> p b (k t)"), shift[:, 0, 0:1], None, ALU.add))
            for e in range(1, E):
                step(nc.vector.tensor_scalar(over[:], route[:, :, 0:2, :].rearrange("p b k t -> p b (k t)"), float(e * REG), step_e[:, e:e + 1], ALU.is_ge, ALU.mult))
                step(nc.vector.tensor_tensor(rows[:], rows[:], over[:], ALU.add))
            nc.vector.tensor_copy(rows_i[:], rows[:]).then_inc(rows_rdy, 1)

            def mix(b):
                dve.wait_ge(gathered[b], 16 * TOPK * NT)
                for t in range(NT):
                    step(nc.vector.tensor_scalar(yk[b][:, 0, t, :], yk[b][:, 0, t, :], route[:, b, 2, t:t + 1], None, ALU.mult))
                for t in range(NT):
                    last = nc.vector.scalar_tensor_tensor(out=yk[b][:, 0, t, :], in0=yk[b][:, 1, t, :], scalar=route[:, b, 3, t:t + 1], in1=yk[b][:, 0, t, :],
                                                          op0=ALU.mult, op1=ALU.add)
                last.then_inc(mixed, 1)
            mix(0)
            for b in range(B):
                if b + 1 < B:
                    mix(b + 1)
                dve.wait_ge(gate, b + 1)
                dve.wait_ge(fetched[b], 32)
                step(nc.vector.tensor_tensor(gated[b % NB][:], gated[b % NB][:], s[b % NB][:], ALU.mult))
                nc.vector.tensor_tensor(x[b % NB][:], x[b % NB][:], gated[b % NB][:], ALU.add).then_inc(sums, 1)


def tables():
    f = np.float32
    inv = 1.0 / 10000.0 ** (np.arange(0, RDK, 2, dtype=np.float64) / RDK)
    ang = (np.arange(T, dtype=f)[:, None] * inv.astype(f)).astype(np.float64)
    gamma = 1.0 - 2.0 ** (-5.0 - np.arange(RH))
    rC = np.zeros((T, 8, 32))
    rS = np.zeros((T, 8, 2, 32))
    for h in range(RH):
        dq = gamma[h] ** (np.arange(T) + 1.0)
        for u, fac in ((h, dq * RDK ** -0.5), (RH + h, 1.0 / dq)):
            rC[:, u] = np.cos(ang) * fac[:, None]
            rS[:, u, 0] = -np.sin(ang) * fac[:, None]
            rS[:, u, 1] = np.sin(ang) * fac[:, None]
    hi = np.arange(0, DH, 2, dtype=f)
    inv = (1.0 / 10000.0 ** (hi.astype(np.float64) / DH)).astype(f)
    fr = (np.arange(T, dtype=f)[:, None] * inv).astype(np.float64)
    base = (hi.astype(np.float64) + 0.4 * DH) / (1.4 * DH)
    power = (np.arange(T) - T // 2) / float(WINDOW // 2)
    sc = base[None, :] ** power[:, None]
    fC = np.zeros((T, 2, DH))
    fS = np.zeros((T, 2, DH))
    for i, s in ((0, sc * 8.0), (1, 1.0 / sc)):
        fC[:, i] = np.concatenate([np.cos(fr) * s] * 2, -1)
        fS[:, i] = np.concatenate([-np.sin(fr) * s, np.sin(fr) * s], -1)
    inv = (10000.0 ** (-np.arange(0, LDR, 2, dtype=np.float64) / LDR)).astype(f)
    an = (np.arange(T, dtype=f)[:, None] * inv).astype(np.float64)
    lc = np.zeros((32, T))
    ls = np.zeros((32, T))
    lc[0:LDH] = 1.0
    for j in range(LDR // 2):
        lc[LDH + 2 * j] = lc[LDH + 2 * j + 1] = np.cos(an[:, j])
        ls[LDH + 2 * j] = -np.sin(an[:, j])
        ls[LDH + 2 * j + 1] = np.sin(an[:, j])
    by_tile = lambda a: np.ascontiguousarray(a.reshape((NT, P) + a.shape[1:]).swapaxes(0, 1).astype(f))
    return {"w_rC": by_tile(rC), "w_rS": by_tile(rS), "w_fC": by_tile(fC), "w_fS": by_tile(fS),
            "w_lcos": np.tile(lc, (4, 1)).astype(f), "w_lsin": np.tile(ls, (4, 1)).astype(f),
            "zrow": np.zeros((1, P), f)}


def arrange(a):
    ch = lambda w: np.ascontiguousarray(w.reshape((-1, P) + w.shape[1:]).swapaxes(0, 1))
    per = lambda v: np.ascontiguousarray(v.reshape(-1, P).T)
    r = {"x": a["L0_attn_x"]}
    r["w_rWqk"] = ch(np.concatenate([a["L0_attn_Wq"], a["L0_attn_Wk"]], 1))
    r["w_rWv"] = ch(a["L0_attn_Wv"])
    r["w_rWg"] = ch(a["L0_attn_Wg"])
    r["w_rWo"] = ch(a["L0_attn_Wo"])
    r["w_rln"] = np.stack([per(a["L0_attn_ln_w"]), per(a["L0_attn_ln_b"])], 1)
    r["w_rgn"] = a["L0_attn_g_norm_w"].reshape(P, 1)
    r["w_wqkv"] = np.stack([ch(w) for w in a["L0_ffn_wqkv"]], 1)
    r["w_wo"] = np.stack([ch(w) for w in a["L0_ffn_wo"]], 1)
    r["w_ln"] = np.stack([np.stack([per(g), per(b)], 1) for g, b in zip(a["L0_ffn_ln_g"], a["L0_ffn_ln_b"])], 1)
    r["w_w1"] = np.stack([ch(w) for w in a["L0_ffn_w1"]], 1)
    b1 = np.zeros((HCH, DEPTH, 2, NHC), np.float32)
    w2 = np.zeros((HCH, DEPTH, NHC, D), np.float32)
    for l in range(DEPTH):
        for c in range(NHC):
            n = HSZ[c]
            for i in range(2):
                b1[0:n, l, i, c] = a["L0_ffn_b1"][l, i * HID + c * HCH:i * HID + c * HCH + n]
            w2[0:n, l, c] = a["L0_ffn_w2"][l, c * HCH:c * HCH + n]
        w2[HSZ[-1], l, NHC - 1] = a["L0_ffn_b2"][l]
    r["w_b1"], r["w_w2"] = b1, w2
    swap = np.concatenate([np.arange(32, 64), np.arange(0, 32)])
    qs = np.stack([np.stack([a["L0_ffn_q_scale"], a["L0_ffn_k_scale"]], 1),
                   np.stack([a["L0_ffn_q_scale"][:, swap], a["L0_ffn_k_scale"][:, swap]], 1)], 1)
    r["w_qks"] = np.broadcast_to(qs[None], (P,) + qs.shape)
    r["w_lWd"] = np.stack([ch(a["L1_attn_W_DQ"]), ch(a["L1_attn_W_DKV"])], 1)
    wq = np.zeros((LAT, 2, LG, 4, 32), np.float32)
    wk = np.zeros((LAT, LG, 4, 32), np.float32)
    wkr = np.zeros((D, 2, 4, 32), np.float32)
    partner = np.arange(LDR).reshape(-1, 2)[:, ::-1].reshape(-1)
    wq[:, 0, :, :, 0:LDH] = a["L1_attn_W_UQ"].reshape(LAT, LG, 4, LDH)
    qr = a["L1_attn_W_QR"].reshape(LAT, LG, 4, LDR)
    wq[:, 0, :, :, LDH:LDH + LDR] = qr
    wq[:, 1, :, :, LDH:LDH + LDR] = qr[..., partner]
    wk[..., 0:LDH] = a["L1_attn_W_UK"].reshape(LAT, LG, 4, LDH)
    kr = a["L1_attn_W_KR"]
    wkr[:, 0, :, LDH:LDH + LDR] = kr[:, None]
    wkr[:, 1, :, LDH:LDH + LDR] = kr[:, partner][:, None]
    r["w_lWq"] = wq.reshape(LAT, 2, LG, P)
    r["w_lWk"] = wk.reshape(LAT, LG, P)
    r["w_lWkr"] = wkr.reshape(DC, P, 2, P).transpose(1, 2, 0, 3)
    r["w_lWv"] = a["L1_attn_W_UV"]
    r["w_lWo"] = ch(a["L1_attn_W_O"])
    r["w_gw"] = ch(a["L1_ffn_gate_w"])
    r["m_w1"] = np.stack([ch(w) for w in a["L1_ffn_w1"]], 0)
    r["m_w2"] = np.stack([ch(w) for w in a["L1_ffn_w2"]], 0)
    return r


def kernel(**inputs):
    import numpy as _np
    import concourse.bacc as _bacc
    from concourse import mybir as _mybir
    from concourse.bass_utils import run_bass_kernel_spmd as _run

    nc = _bacc.Bacc("TRN2", target_bir_lowering=False, num_devices=1)
    arrays = {**arrange({k: _np.asarray(v) for k, v in inputs.items()}), **tables()}
    arrays = {k: _np.ascontiguousarray(v) for k, v in arrays.items()}
    ins = {k: nc.dram_tensor(f"in_{k}", v.shape, _mybir.dt.from_np(v.dtype), kind="ExternalInput").ap() for k, v in arrays.items()}
    out = nc.dram_tensor("out_0", (B, T, D), F32, kind="ExternalOutput").ap()
    build(nc, ins, out)
    r = _run(nc, [{f"in_{k}": v for k, v in arrays.items()}], core_ids=[0])
    return r.results[0]["out_0"]
```

```python
import concourse.bass as bass
from concourse import mybir
from contextlib import ExitStack
import numpy as np

F32 = mybir.dt.float32
BF16 = mybir.dt.bfloat16
I32 = mybir.dt.int32
ALU = mybir.AluOpType
ACT = mybir.ActivationFunctionType
AX = mybir.AxisListType

P = 128
B, T, D = 8, 512, 256
NT = T // P
DC = D // P
EPS = 1e-5
RH, RDK, RDV = 4, 64, 128
RV = RH * RDV
DEPTH, HEADS, DH, WINDOW = 2, 8, 64, 128
INNER = HEADS * DH
HID = 682
HCH = 120
NHC = 6
HSZ = [min(HCH, HID - HCH * c) for c in range(NHC)]
LH, LDH, LDR, LAT = 16, 16, 8, 64
KEYS = (0, 512, 1024, 896)
LG = 4
SQ24 = float(np.sqrt(np.float32(LDH + LDR)))
E, F = 8, 1024
FC = F // P
TOPK = 2
REG = B * T + P
NTILES = (B * T * TOPK + E * (P - 1)) // P + 1
UNROLL = 18
assert NTILES % UNROLL == 0


def act_jobs(l):
    if l == 0:
        j = [("xT", 0)]
        for t in range(NT):
            j += ([("xT", t + 1)] if t + 1 < NT else []) + [("v", t)]
        j += [("zaT", t) for t in range(NT)]
    else:
        j = [("curT", t) for t in range(NT)]
    for t in range(NT):
        j += [("rv" if l == 0 else "v", t)]
        j += [("qkT", t)]
    j += [("S", u) for u in range(2 * NT)]
    if l == 0:
        j += [("rT", t) for t in range(NT)]
        j += [("rg", t) for t in range(NT)]
    j += [("zT", t) for t in range(NT)]
    j += [("g", c) for c in range(NHC)]
    if l == 0:
        j += [("roT", t) for t in range(NT)]
    if l == 1:
        j += [("x1T", t) for t in range(NT)]
        j += [("lv", t) for t in range(NT)]
        j += [("av", g) for g in range(LG)]
        j += [("attnT", t) for t in range(NT)]
    return j


def dve_jobs(l):
    j = [("qk", t) for t in range(NT)]
    if l == 0:
        j += [("rqk", t) for t in range(NT)]
    for u in range(2, 2 * NT + 3):
        if u - 2 < 2 * NT:
            j += [("PT", u - 2)]
        if u >= 3:
            j += [("O", u - 3)]
    j += [("wo", t) for t in range(NT)]
    if l == 0:
        for t in range(NT):
            j += [("AT", t)] + ([("st", t)] if t < NT - 1 else []) + [("ro", t)]
    j += [("a", c) for c in range(NHC)]
    j += [("w2", t) for t in range(NT)]
    if l == 0:
        j += [("rout", t) for t in range(NT)]
    else:
        j += [("lat",), ("kr",), ("rt",)] + [("kc", g) for g in range(LG)] + [("lq", g) for g in range(LG)]
        for g in range(LG):
            for h in range(4 * g, 4 * g + 4):
                j += [("sa", h), ("sb", h), ("sc", h)]
            if g == 1:
                j += [("rank",)]
            if g >= 2:
                j += [("aTM", g - 2)]
        j += [("aTM", LG - 2), ("aTM", LG - 1)]
        j += [("lo", t) for t in range(NT)]
    return j


TWO_BANKS = ("qkT", "S", "qk", "PT", "AT", "ro", "lat", "kr", "lq")
BANKS = 4


def ring(jobs):
    at, cols, firsts, before = 0, [], [], []
    for name in jobs:
        n = 2 if name[0] in TWO_BANKS else 1
        at += at % n
        cols.append(slice(at % BANKS * 512, (at % BANKS + n) * 512))
        before.append(sum(f <= at + n - 1 - BANKS for f in firsts))
        firsts.append(at)
        at += n
    return cols, before


def place(h):
    return 2 * (h % 2) + h // 2


def build(nc, I, O):
    x_d = I["x"].rearrange("b (t p) c -> b p t c", p=P)
    out_d = O.rearrange("b (t p) c -> (b t) p c", p=P)
    scratch = lambda n, s, dt=F32: nc.dram_tensor(n, s, dt, kind="Internal").ap()
    S = {
        "cur": scratch("cur_s", [B, P, NT, D]),
        "s": scratch("s_s", [B, P, NT, D]),
        "x1": scratch("x1_s", [B, P, NT, D]),
        "s2": scratch("s2_s", [B, P, NT, D]),
        "route": scratch("route_s", [B, P, 4, NT]),
        "count": scratch("count_s", [P, E]),
        "rows": scratch("rows_s", [E * REG + P, D]),
        "tile": scratch("tile_s", [P, 3, E]),
        "y": scratch("y_s", [NTILES * P, D]),
    }
    block_layer(nc, I, 0, x_d, S)
    block_layer(nc, I, 1, x_d, S)
    block_moe(nc, I, S)
    block_out(nc, S, out_d)


def block_layer(nc, I, l, x_d, S):
    AJ = {n: i for i, n in enumerate(act_jobs(l))}
    DJ = {n: i for i, n in enumerate(dve_jobs(l))}
    colsA, beforeA = ring(act_jobs(l))
    colsD, beforeD = ring(dve_jobs(l))
    ctx = ExitStack()
    with ctx:
        def sb(name, shape, dt=F32):
            return ctx.enter_context(nc.sbuf_tensor(f"L{l}_{name}", shape, dt))

        def sem(name):
            return ctx.enter_context(nc.semaphore(f"L{l}_{name}"))

        W = {}
        first = (("rWqk", [P, DC, 512]), ("rWv", [P, DC, RV]), ("rWg", [P, DC, RV]), ("rWo", [P, RH, D]),
                 ("rln", [P, 2, DC]), ("rgn", [P, 1]), ("rC", [P, NT, 8, 32]), ("rS", [P, NT, 8, 2, 32]))
        second = (("lWd", [P, 2, DC, LAT]), ("lWq", [LAT, 2, LG, P]), ("lWk", [LAT, LG, P]),
                  ("lWkr", [P, 2, DC, P]), ("lWv", [LAT, LH * LDH]), ("lWo", [P, DC, D]),
                  ("lcos", [P, T]), ("lsin", [P, T]), ("gw", [P, DC, E]))
        layer = (("wqkv", [P, DC, 3 * INNER]), ("wo", [P, 4, D]), ("ln", [P, 2, DC]), ("w1", [P, DC, 2 * HID]),
                 ("b1", [HCH, 2, NHC]), ("w2", [HCH, NHC, D]), ("qks", [P, 2, 2, DH]))
        both = (("fC", [P, NT, 2, DH]), ("fS", [P, NT, 2, DH]))
        source = {}
        for n, shape in (second if l else first) + both + layer:
            W[n] = sb("w_" + n, shape)
            source[n] = I["w_" + n][:, l] if (n, shape) in layer else I["w_" + n]
        Ct = sb("Ct", [P, NT, 2, DH])
        St = sb("St", [P, NT, 2, DH])
        ident = sb("ident", [P, P])
        identb = sb("identb", [P, P], BF16)
        tri = sb("tri", [P, P])
        maskw = sb("maskw", [P, 2, P], BF16)
        half = sb("half", [P, 16])

        x_tm = sb("x_tm", [P, NT, D])
        xn = sb("xn", [P, NT, D])
        cur = sb("cur", [P, NT, D])
        curT = sb("curT", [P, DC, T + 1])
        hB = sb("hB", [P, NT, P])
        z = sb("z", [P, NT, D])
        zT = sb("zT", [P, DC, T])
        stat = sb("stat", [P, NT, 2, 6])
        mv = sb("mv", [P, NT, 2])
        ve = sb("ve", [P, NT])
        rs = sb("rs", [P, NT])
        s_tm = sb("s_tm", [P, NT, D])
        if l:
            cin = sb("cin", [P, NT, D])

        ARENA = 20480 + 2048
        arena = sb("arena", [P, ARENA])
        at = [0]

        def view(n):
            v = arena[:, at[0]:at[0] + n]
            at[0] += n
            assert at[0] <= ARENA, at[0]
            return v

        rqk = view(NT * 512).rearrange("p (t n) -> p t n", t=NT)
        rqkT = view(4 * T).rearrange("p (c n) -> p c n", c=4)
        rv = view(NT * RV).rearrange("p (t n) -> p t n", t=NT)
        gs = view(NT * RV).rearrange("p (t n) -> p t n", t=NT)
        mid = at[0]
        qk = view(NT * 1024).rearrange("p (t n) -> p t n", t=NT)
        qkT = view(8 * T).rearrange("p (c n) -> p c n", c=8)
        v_tm = view(NT * INNER).rearrange("p (t n) -> p t n", t=NT)
        sq = view(2 * 1024).rearrange("p (b n) -> p b n", b=2)
        rot = view(2 * 1024).rearrange("p (b n) -> p b n", b=2)
        prob = [qk[:, i, :] for i in range(3)]
        PT = [qk[:, 3, :], rot[:, 0, :]]
        oT = sq.rearrange("p b n -> p (b n)").rearrange("p (c n) -> p c n", c=4)
        AT = rot.rearrange("p b n -> p (b n)")[:, 0:1024].rearrange("p (b n) -> p b n", b=2)
        o_sb = rot.rearrange("p b n -> p (b n)")[:, 1024:2048].rearrange("p (b n) -> p b n", b=2)
        osq = prob[0].rearrange("p (b n) -> p b n", b=2)
        roT = gs.rearrange("p t n -> p (t n)").rearrange("p (c n) -> p c n", c=4)
        rst = sb("rst", [P, NT, 2, RDV])
        hT = qkT.rearrange("p c n -> p (c n)")[:, 0:NHC * T].rearrange("p (c n) -> p c n", c=NHC)
        gl = v_tm.rearrange("p t n -> p (t n)")[:, 0:2 * T].rearrange("p (b n) -> p b n", b=2)
        at[0] = 0
        Kpad = view(2 * 4 * T).rearrange("p (b h n) -> p b h n", b=2, h=4)
        QT = view(LG * T).rearrange("p (g n) -> p g n", g=LG)
        KT = view(LG * T).rearrange("p (g n) -> p g n", g=LG)
        Pl = view(2 * 4 * 1280).rearrange("p (b h n) -> p b h n", b=2, h=4)
        behind = at[0]
        at[0] -= 4 * 1280
        KrT = view(T)
        rm1 = view(2 * T).rearrange("p (b n) -> p b n", b=2)
        rm2 = view(2 * T).rearrange("p (b n) -> p b n", b=2)
        latT = view(2 * T).rearrange("p (b n) -> p b n", b=2)
        at[0] = behind
        aT = view(LG * T).rearrange("p (g n) -> p g n", g=LG)
        if l:
            Vaug = sb("Vaug", [P, NT, LH, 32])
            iota8 = sb("iota8", [P, NT, E])
            region = sb("region", [P, NT, E])
            before = sb("before", [P, P])
            ones = sb("ones", [P, P])
            zrows = sb("zrows", [P, D])
            counts = sb("counts", [P, NT + 1, E])
            counts_i = sb("counts_i", [P, E], I32)
            route = sb("route", [P, 4, NT])
            rows_i = sb("rows_i", [P, 2 * NT], I32)
            zero_in = sem("zero_in")
        attn = z
        attnT = zT
        s2 = s_tm
        ssq = sb("ssq", [P, NT, 16])
        rinv = sb("rinv", [P, NT, 16])
        mx = sb("mx", [P, 2 * NT, 4])
        rsum = sb("rsum", [P, 2 * NT, 4])
        rrec = sb("rrec", [P, 2 * NT, 4])
        rss = sb("rss", [P, NT, 4])
        rrs = sb("rrs", [P, NT, 4])
        rd = sb("rd", [P, NT, LH])
        rt = sb("rt", [P, 8, NT, E])
        rt1 = sb("rt1", [P, 8, NT])

        pA = ctx.enter_context(nc.psum_tensor(f"L{l}_pA", [P, BANKS * 512], F32))
        pD = ctx.enter_context(nc.psum_tensor(f"L{l}_pD", [P, BANKS * 512], F32))

        loaded = sem("loaded")
        loaded_rest = sem("loaded_rest")
        const_p = sem("const_p")
        const_v = sem("const_v")
        per_batch = []

        def bsem(name):
            s = sem(name)
            per_batch.append(s)
            return s

        x_in = bsem("x_in")
        next_in = bsem("next_in")
        mmA = bsem("mmA")
        outA = bsem("outA")
        mmD = bsem("mmD")
        outD = bsem("outD")
        v_step = bsem("v_step")
        a_step = bsem("a_step")
        var_rdy = bsem("var_rdy")
        rstd = bsem("rstd")
        norm = bsem("norm")
        squares = bsem("squares")
        ssq_rdy = bsem("ssq_rdy")
        rinv_rdy = bsem("rinv_rdy")
        qk_rdy = bsem("qk_rdy")
        mx_rdy = bsem("mx_rdy")
        rrec_rdy = bsem("rrec_rdy")
        p_rdy = bsem("p_rdy")
        shifted = [bsem(f"shifted{t}") for t in range(NT)]
        stores = bsem("stores")
        arrive = bsem("arrive")
        p_const = sem("p_const")
        go = {e: sem("go_" + e) for e in ("pe", "act", "dve", "pool")}
        if l == 0:
            var_first = sem("var_first")
            rstd_first = sem("rstd_first")
            rqk_rdy = bsem("rqk_rdy")
            osq_rdy = bsem("osq_rdy")
            rss_rdy = bsem("rss_rdy")
            rrs_rdy = bsem("rrs_rdy")
            og_rdy = bsem("og_rdy")
        else:
            fin_silu = bsem("fin_silu")
            x1_rdy = bsem("x1_rdy")
            lq_rdy = bsem("lq_rdy")
            kpad = bsem("kpad")
            lexp = bsem("lexp")
            masked = bsem("masked")
            chosen = bsem("chosen")
            rows_rdy = bsem("rows_rdy")
            scattered = sem("scattered")
        block = ctx.enter_context(nc.Block())

        names = [n for n in W if n in ("wqkv", "fC", "fS", "qks", "rWo", "rgn")]
        others = [n for n in W if n not in names]

        @block.sync
        def _(sp):
            for n in names:
                sp.dma_start(W[n][:], source[n]).then_inc(loaded, 16)
            if l:
                sp.dma_start(cin[:], S["cur"][0]).then_inc(loaded, 16)
            else:
                sp.dma_start(x_tm[:], x_d[0]).then_inc(loaded, 16)
            for n in others:
                sp.dma_start(W[n][:], source[n]).then_inc(loaded_rest, 16)
            sp.wait_ge(const_v, 1)
            if l:
                sp.dma_start(S["rows"][E * REG:E * REG + P, :], zrows[:]).then_inc(zero_in, 16)
            def batch(b, following):
                if l:
                    sp.dma_start(x_tm[:], x_d[b]).then_inc(x_in, 16)
                    sp.dma_start(s_tm[:], S["s"][b]).then_inc(x_in, 16)
                else:
                    sp.wait_ge(norm, NT)
                    sp.dma_start(x_tm[:], x_d[following]).then_inc(next_in, 16)
                for t in range(NT):
                    sp.wait_ge(outD, DJ["wo", t] + 1)
                    sp.dma_start(hB[1:P, t, :], cur[0:P - 1, t, P:D]).then_inc(shifted[t], 16)
                    if t == 0:
                        sp.dma_start(hB[0:1, 0, :], I["zrow"]).then_inc(shifted[t], 16)
                    else:
                        sp.dma_start(hB[0:1, t, :], cur[P - 1:P, t - 1, P:D]).then_inc(shifted[t], 16)
                if l == 0:
                    sp.wait_ge(outD, DJ["w2", NT - 1] + 1)
                    sp.dma_start(S["cur"][b], cur[:]).then_inc(stores, 16)
                    sp.wait_ge(outD, DJ["rout", NT - 1] + 1)
                    sp.dma_start(S["s"][b], s_tm[:]).then_inc(stores, 16)
                    sp.wait_ge(stores, 32)
                else:
                    sp.dma_start(cin[:], S["cur"][following]).then_inc(next_in, 16)
                    sp.wait_ge(x1_rdy, NT)
                    sp.dma_start(S["x1"][b], x_tm[:]).then_inc(stores, 16)
                    sp.wait_ge(rows_rdy, 1)
                    sp.dma_start(S["route"][b], route[:]).then_inc(stores, 16)
                    sp.wait_ge(outD, DJ["lo", NT - 1] + 1)
                    sp.dma_start(S["s2"][b], s2[:]).then_inc(stores, 16)
                    sp.wait_ge(stores, 16 * 3)
                sp.wait_ge(next_in, 16)
                if l:
                    sp.wait_ge(x_in, 32)
                sp.wait_ge(arrive, 4)
                for s in per_batch:
                    sp.sem_clear(s)
                for g in go.values():
                    sp.sem_inc(g, 1)
            with sp.Fori(0, B - 1) as b:
                batch(b, b + 1)
            batch(B - 1, B - 1)
            if l:
                sp.dma_start(S["count"], counts[:, 0, :]).then_inc(zero_in, 16)
                for e in range(E):
                    end = sp.value_load(counts_i[0:1, e:e + 1], min_val=0, max_val=B * T)
                    sp.dma_start(S["rows"][bass.ds(end + e * REG, P), :], zrows[:]).then_inc(zero_in, 16)
                sp.wait_ge(zero_in, 16 * (E + 2))

        @block.tensor
        def _(pe):
            na, nd = [0], [0]

            def slotA(name):
                k = AJ[name]
                assert k == na[0], (name, k, na[0])
                na[0] += 1
                if beforeA[k] > 0:
                    pe.wait_ge(outA, beforeA[k])
                return pA[:, colsA[k]]

            def slotD(name):
                k = DJ[name]
                assert k == nd[0], (name, k, nd[0])
                nd[0] += 1
                if beforeD[k] > 0:
                    pe.wait_ge(outD, beforeD[k])
                return pD[:, colsD[k]]

            def transposes(name, src, chunks):
                ps = slotA(name)
                for c in range(chunks):
                    last = nc.tensor.transpose(ps[:, c * P:(c + 1) * P], src(c), ident[:])
                last.then_inc(mmA, 1)

            def project(out, lhs, rhs, n):
                for c in range(n):
                    last = nc.tensor.matmul(out, lhs(c), rhs(c), start=(c == 0), stop=(c == n - 1))
                return last

            def tile_cols(t):
                return slice(t * P, (t + 1) * P)

            def shifted_lhs(t):
                return lambda c: curT[:, c, t * P + (1 - c):(t + 1) * P + (1 - c)]

            def latent_attention():
                for t in range(NT):
                    pe.wait_ge(norm, NT + t + 1)
                    transposes(("x1T", t), lambda c: xn[:, t, c * P:(c + 1) * P], DC)
                xT = lambda c: curT[:, c, 1:T + 1]
                pe.wait_ge(outA, AJ["x1T", NT - 1] + 1)
                ps = slotD(("lat",))
                for i in range(2):
                    last = project(ps[0:LAT, i * T:(i + 1) * T], lambda c: W["lWd"][:, i, c, :], xT, DC)
                last.then_inc(mmD, 1)
                ps = slotD(("kr",))
                for i in range(2):
                    last = project(ps[:, i * T:(i + 1) * T], lambda c: W["lWkr"][:, i, c, :], xT, DC)
                last.then_inc(mmD, 1)
                ps = slotD(("rt",))
                for t in range(NT):
                    last = project(ps[:, t * E:(t + 1) * E], lambda c: curT[:, c, 1 + t * P:1 + (t + 1) * P], lambda c: W["gw"][:, c, :], DC)
                last.then_inc(mmD, 1)
                pe.wait_ge(outD, DJ["lat",] + 1)
                for t in range(NT):
                    ps = slotA(("lv", t))
                    nc.tensor.matmul(ps[:, 0:D], latT[0:LAT, 1, tile_cols(t)], W["lWv"][:], start=True, stop=True).then_inc(mmA, 1)
                for g in range(LG):
                    ps = slotD(("kc", g))
                    nc.tensor.matmul(ps[:, 0:T], W["lWk"][:, g, :], latT[0:LAT, 1, :], start=True, stop=True).then_inc(mmD, 1)
                for g in range(LG):
                    ps = slotD(("lq", g))
                    for i in range(2):
                        last = nc.tensor.matmul(ps[:, i * T:(i + 1) * T], W["lWq"][:, i, g, :], latT[0:LAT, 0, :], start=True, stop=True)
                    last.then_inc(mmD, 1)

                def values(g):
                    pe.wait_ge(masked, 4 * g + 4)
                    pe.wait_ge(outA, AJ["lv", NT - 1] + 1)
                    ps = slotA(("av", g))
                    for kt, off in enumerate(KEYS):
                        for i in range(4):
                            last = nc.tensor.matmul(ps[32 * i:32 * i + 32, kt * P:T], Vaug[:, kt, 4 * g + i, :],
                                                    Pl[:, g % 2, i, off:off + T - kt * P], start=(kt == 0), stop=(kt == NT - 1))
                    last.then_inc(mmA, 1)

                def by_token(g):
                    pe.wait_ge(outA, AJ["av", g] + 1)
                    ps = slotD(("aTM", g))
                    for t in range(NT):
                        last = nc.tensor.transpose(ps[:, t * P:(t + 1) * P], aT[:, g, tile_cols(t)], ident[:])
                    last.then_inc(mmD, 1)

                for g in range(LG):
                    pe.wait_ge(lq_rdy, g + 1)
                    for i in range(4):
                        def score(out, kt):
                            return nc.tensor.matmul(out, Kpad[:, g % 2, i, tile_cols(kt)], QT[:, g, kt * P:T], start=True, stop=True)
                        pe.wait_ge(kpad, 4 * g + i + 1)
                        ps = slotD(("sa", 4 * g + i))
                        score(ps[:, 0:512], 0).then_inc(mmD, 1)
                        ps = slotD(("sb", 4 * g + i))
                        score(ps[:, 0:384], 1)
                        score(ps[:, 384:512], 3).then_inc(mmD, 1)
                        ps = slotD(("sc", 4 * g + i))
                        score(ps[:, 0:256], 2).then_inc(mmD, 1)
                    if g == 1:
                        pe.wait_ge(chosen, 1)
                        ps = slotD(("rank",))
                        for i, m in enumerate((before, ones)):
                            last = nc.tensor.matmul(ps[:, i * NT * E:(i + 1) * NT * E], m[:], rt[:, 3].rearrange("p t e -> p (t e)"), start=True, stop=True)
                        last.then_inc(mmD, 1)
                    if g > 0:
                        values(g - 1)
                    if g > 1:
                        by_token(g - 2)
                by_token(LG - 2)
                values(LG - 1)
                by_token(LG - 1)
                pe.wait_ge(outD, DJ["aTM", LG - 1] + 1)
                for t in range(NT):
                    transposes(("attnT", t), lambda c: attn[:, t, c * P:(c + 1) * P], DC)
                for t in range(NT):
                    pe.wait_ge(outA, AJ["attnT", t] + 1)
                    ps = slotD(("lo", t))
                    project(ps[:, 0:D], lambda c: attnT[:, c, tile_cols(t)], lambda c: W["lWo"][:, c, :], DC).then_inc(mmD, 1)

            def v_product(t):
                ps = slotA(("v", t))
                project(ps[:, 0:512], shifted_lhs(t), lambda c: W["wqkv"][:, c, 1024:1536], DC).then_inc(mmA, 1)

            pe.wait_ge(loaded, 16 * len(names) + 16)
            pe.wait_ge(const_v, 1)
            with pe.Fori(0, B):
                def stream_transposes(t):
                    if l == 0:
                        pe.wait_ge(norm, t + 1)
                    transposes(("curT" if l else "xT", t), lambda c: (cin if l else xn)[:, t, c * P:(c + 1) * P], DC)
                stream_transposes(0)
                for t in range(NT):
                    if t + 1 < NT:
                        stream_transposes(t + 1)
                    pe.wait_ge(outA, AJ["curT" if l else "xT", t] + 1)
                    ps = slotD(("qk", t))
                    project(ps[:, 0:512], shifted_lhs(t), lambda c: W["wqkv"][:, c, 0:512], DC)
                    project(ps[:, 512:1024], shifted_lhs(t), lambda c: W["wqkv"][:, c, 512:1024], DC).then_inc(mmD, 1)
                    if l == 0:
                        v_product(t)
                pe.wait_ge(loaded_rest, 16 * len(others))
                for t in range(0 if l else NT):
                    pe.wait_ge(norm, NT + t + 1)
                    transposes(("zaT", t), lambda c: z[:, t, c * P:(c + 1) * P], DC)
                for t in range(NT):
                    if l == 0:
                        zl = lambda c: zT[:, c, tile_cols(t)]
                        pe.wait_ge(outA, AJ["zaT", t] + 1)
                        ps = slotD(("rqk", t))
                        project(ps[:, 0:512], zl, lambda c: W["rWqk"][:, c, :], DC).then_inc(mmD, 1)
                        ps = slotA(("rv", t))
                        project(ps[:, 0:RV], zl, lambda c: W["rWv"][:, c, :], DC).then_inc(mmA, 1)
                    else:
                        v_product(t)
                    pe.wait_ge(qk_rdy, t + 1)
                    transposes(("qkT", t), lambda c: qk[:, t, c * P:(c + 1) * P], 8)

                for u in range(2 * NT + 3):
                    if u < 2 * NT:
                        t, hh = u // 2, u % 2
                        pe.wait_ge(outA, AJ["qkT", t] + 1)
                        ps = slotA(("S", u))
                        lo = 0 if t else 1
                        for bank in range(2):
                            nc.tensor.matmul(ps[:, bank * 512:(bank + 1) * 512].rearrange("p (h k q) -> p h k q", h=2, k=2)[:, :, lo:2, :],
                                             identb[:], maskw[:, lo:2, :].unsqueeze(1).broadcast_to((P, 2, 2 - lo, P)), start=True, stop=False)
                        for i in range(4):
                            h = 4 * hh + i
                            r = slice(64 * (h % 2), 64 * (h % 2) + 64)
                            last = nc.tensor.matmul(ps[:, place(i) * 256 + lo * P:(place(i) + 1) * 256], qkT[r, h // 2, tile_cols(t)],
                                                    qkT[r, 4 + h // 2, (t - 1 + lo) * P:(t + 1) * P], start=False, stop=(i >= 2))
                        last.then_inc(mmA, 1)
                    if 2 <= u < 2 * NT + 2:
                        w = u - 2
                        pe.wait_ge(p_rdy, w + 1)
                        ps = slotD(("PT", w))
                        for i in range(4):
                            for k in range(0 if w // 2 else 1, 2):
                                last = nc.tensor.transpose(ps[:, (2 * i + k) * P:(2 * i + k + 1) * P],
                                                           prob[w % 3][:, i * 256 + k * P:i * 256 + (k + 1) * P], ident[:])
                        last.then_inc(mmD, 1)
                    if u >= 3:
                        w = u - 3
                        t, hh = w // 2, w % 2
                        pe.wait_ge(outD, DJ["PT", w] + 1)
                        ps = slotD(("O", w))
                        lo = 0 if t else 1
                        for pr in range(2):
                            for k in range(lo, 2):
                                for i in (2 * pr, 2 * pr + 1):
                                    h = 4 * hh + i
                                    last = nc.tensor.matmul(ps[64 * (i % 2):64 * (i % 2) + 64, pr * P:(pr + 1) * P],
                                                            v_tm[:, t - 1 + k, h * DH:(h + 1) * DH],
                                                            PT[w % 2][:, (2 * place(i) + k) * P:(2 * place(i) + k + 1) * P],
                                                            start=(k == lo), stop=(k == 1))
                        last.then_inc(mmD, 1)

                for t in range(0 if l else NT):
                    pe.wait_ge(rqk_rdy, t + 1)
                    transposes(("rT", t), lambda c: rqk[:, t, c * P:(c + 1) * P], 4)
                for t in range(NT):
                    pe.wait_ge(outD, DJ["O", 2 * t + 1] + 1)
                    ps = slotD(("wo", t))
                    project(ps[:, 0:D], lambda c: oT[:, c, tile_cols(t)], lambda c: W["wo"][:, c, :], 4).then_inc(mmD, 1)
                if l == 0:
                    for t in range(NT):
                        pe.wait_ge(outA, AJ["rT", t] + 1)
                        ps = slotD(("AT", t))
                        for h in range(RH):
                            r = slice(64 * (h % 2), 64 * (h % 2) + 64)
                            last = nc.tensor.matmul(ps[:, (h % 2) * 512 + (h // 2) * P:(h % 2) * 512 + (h // 2 + 1) * P], rqkT[r, 2 + h // 2, tile_cols(t)],
                                                    rqkT[r, h // 2, tile_cols(t)], start=True, stop=True)
                        last.then_inc(mmD, 1)
                        if t < NT - 1:
                            ps = slotD(("st", t))
                            for h in range(RH):
                                last = nc.tensor.matmul(ps[64 * (h % 2):64 * (h % 2) + 64, (h // 2) * RDV:(h // 2 + 1) * RDV],
                                                        rqk[:, t, 256 + h * RDK:256 + (h + 1) * RDK],
                                                        rv[:, t, h * RDV:(h + 1) * RDV], start=True, stop=True)
                            last.then_inc(mmD, 1)
                        ps = slotA(("rg", t))
                        project(ps[:, 0:RV], lambda c: zT[:, c, tile_cols(t)], lambda c: W["rWg"][:, c, :], DC).then_inc(mmA, 1)
                        pe.wait_ge(outD, DJ["AT", t] + 1)
                        ps = slotD(("ro", t))
                        for h in range(RH):
                            r = slice(64 * (h % 2), 64 * (h % 2) + 64)
                            out = ps[:, (h % 2) * 512 + (h // 2) * RDV:(h % 2) * 512 + (h // 2 + 1) * RDV]
                            last = nc.tensor.matmul(out, AT[:, t % 2, place(h) * P:(place(h) + 1) * P], rv[:, t, h * RDV:(h + 1) * RDV],
                                                    start=True, stop=(t == 0))
                            if t:
                                last = nc.tensor.matmul(out, rqkT[r, h // 2, tile_cols(t)], rst[r, t, h // 2, :],
                                                        start=False, stop=True)
                        last.then_inc(mmD, 1)
                for t in range(NT):
                    pe.wait_ge(norm, (0 if l else 2 * NT) + t + 1)
                    transposes(("zT", t), lambda c: z[:, t, c * P:(c + 1) * P], DC)
                for c in range(NHC):
                    n = HSZ[c]
                    if c == 0:
                        pe.wait_ge(outA, AJ["zT", NT - 1] + 1)
                    ps = slotA(("g", c))
                    project(ps[0:n, 0:T], lambda k: W["w1"][:, k, HID + c * HCH:HID + c * HCH + n], lambda k: zT[:, k, :], DC).then_inc(mmA, 1)
                    ps = slotD(("a", c))
                    project(ps[0:n, 0:T], lambda k: W["w1"][:, k, c * HCH:c * HCH + n], lambda k: zT[:, k, :], DC).then_inc(mmD, 1)
                for t in range(0 if l else NT):
                    pe.wait_ge(og_rdy, t + 1)
                    transposes(("roT", t), lambda c: rqk[:, t, c * P:(c + 1) * P], 4)
                for t in range(NT):
                    if t == 0:
                        pe.wait_ge(outD, DJ["a", NHC - 1] + 1)
                    ps = slotD(("w2", t))
                    rows = [min(HCH, HSZ[c] + (c == NHC - 1)) for c in range(NHC)]
                    project(ps[:, 0:D], lambda c: hT[0:rows[c], c, tile_cols(t)], lambda c: W["w2"][0:rows[c], c, :], NHC).then_inc(mmD, 1)
                if l == 0:
                    for t in range(NT):
                        pe.wait_ge(outA, AJ["roT", t] + 1)
                        ps = slotD(("rout", t))
                        project(ps[:, 0:D], lambda c: roT[:, c, tile_cols(t)], lambda c: W["rWo"][:, c, :], RH).then_inc(mmD, 1)
                if l:
                    latent_attention()
                pe.sem_inc(arrive, 1)
                pe.wait_ge(go["pe"], 1)
                pe.sem_clear(go["pe"])

        @block.scalar
        def _(act):
            na = [0]

            def take(name):
                k = AJ[name]
                assert k == na[0], (name, k, na[0])
                na[0] += 1
                act.wait_ge(mmA, k + 1)
                return pA[:, colsA[k]]

            def scaled(name, t, w):
                ps = take(name)
                for c in range(DC):
                    last = nc.scalar.activation(zT[:, c, t * P:(t + 1) * P], ps[:, c * P:(c + 1) * P], ACT.Identity,
                                                bias=w[:, 1, c:c + 1], scale=w[:, 0, c:c + 1])
                last.then_inc(outA, 1)

            def by_channel(name, t):
                ps = take(name)
                nc.scalar.copy(curT[:, :, 1 + t * P:1 + (t + 1) * P], ps[:, 0:D].rearrange("p (c n) -> p c n", c=DC)).then_inc(outA, 1)

            def latent_attention():
                for t in range(NT):
                    act.wait_ge(outD, DJ["w2", t] + 1)
                    nc.scalar.activation(z[:, t, :], cur[:, t, :], ACT.Silu).then_inc(fin_silu, 1)
                for t in range(NT):
                    by_channel(("x1T", t), t)
                for t in range(NT):
                    ps = take(("lv", t))
                    nc.scalar.copy(Vaug[:, t, :, 0:LDH], ps[:, 0:D].rearrange("p (h d) -> p h d", h=LH)).then_inc(outA, 1)

                def av(g):
                    ps = take(("av", g))
                    nc.scalar.copy(aT[:, g, :], ps[:, 0:T]).then_inc(outA, 1)

                def pad_keys(g, i):
                    r = slice(32 * i, 32 * i + 32)
                    nc.scalar.copy(Kpad[r, g % 2, i, :], KT[r, g, :]).then_inc(kpad, 1)

                act.wait_ge(outD, DJ["kc", 0] + 1)
                for i in range(4):
                    pad_keys(0, i)
                act.wait_ge(outD, DJ["rt",] + 1)
                nc.scalar.activation(rt[:, 1], rt[:, 0], ACT.Exp).then_inc(a_step, 1)
                for g in range(LG):
                    for i in range(4):
                        act.wait_ge(outD, DJ["sc", 4 * g + i] + 1)
                        ph = Pl[:, g % 2, i, :]
                        nc.scalar.activation(ph, ph, ACT.Exp, scale=1.0 / SQ24).then_inc(lexp, 1)
                        if g < LG - 1:
                            pad_keys(g + 1, i)
                    if g > 0:
                        av(g - 1)
                av(LG - 1)
                for t in range(NT):
                    ps = take(("attnT", t))
                    nc.scalar.copy(attnT[:, :, t * P:(t + 1) * P], ps[:, 0:D].rearrange("p (c n) -> p c n", c=DC)).then_inc(outA, 1)

            def v_copy(t):
                ps = take(("v", t))
                nc.scalar.copy(v_tm[:, t, :], ps[:, 0:512]).then_inc(outA, 1)

            def output_squares(t):
                act.wait_ge(outD, DJ["ro", t] + 1)
                if t >= 2:
                    act.wait_ge(rss_rdy, t - 1)
                nc.scalar.activation(osq[:, t % 2, :], o_sb[:, t % 2, :], ACT.Square).then_inc(osq_rdy, 1)

            act.wait_ge(loaded, 16 * len(names) + 16)
            act.wait_ge(const_p, 1)
            with act.Fori(0, B):
                by_channel(("curT" if l else "xT", 0), 0)
                for t in range(NT):
                    if t + 1 < NT:
                        by_channel(("curT" if l else "xT", t + 1), t + 1)
                    act.wait_ge(mmD, DJ["qk", t] + 1)
                    if t >= 2:
                        act.wait_ge(outD, DJ["qk", t - 2] + 1)
                    nc.scalar.activation(sq[:, t % 2, :], pD[:, colsD[DJ["qk", t]]], ACT.Square).then_inc(squares, 1)
                    if l == 0:
                        v_copy(t)
                act.wait_ge(loaded_rest, 16 * len(others))
                for t in range(0 if l else NT):
                    scaled(("zaT", t), t, W["rln"])
                for t in range(NT):
                    if l == 0:
                        ps = take(("rv", t))
                        nc.scalar.copy(rv[:, t, :], ps[:, 0:512]).then_inc(outA, 1)
                    else:
                        v_copy(t)
                    ps = take(("qkT", t))
                    nc.scalar.copy(qkT[:, :, t * P:(t + 1) * P], ps[:].rearrange("p (c n) -> p c n", c=8)).then_inc(outA, 1)
                for u in range(2 * NT):
                    act.wait_ge(mx_rdy, u + 1)
                    if u >= 3:
                        act.wait_ge(mmD, DJ["PT", u - 3] + 1)
                    ps = take(("S", u))
                    lo = 0 if u // 2 else P
                    for i in range(4):
                        last = nc.scalar.activation(prob[u % 3][:, i * 256 + lo:(i + 1) * 256], ps[:, i * 256 + lo:(i + 1) * 256], ACT.Exp,
                                                    bias=mx[:, u, i:i + 1], accum_out=rsum[:, u, i:i + 1])
                    last.then_inc(outA, 1)
                    act.wait_ge(rrec_rdy, u + 1)
                    for i in range(4):
                        pi = prob[u % 3][:, i * 256 + lo:(i + 1) * 256]
                        last = nc.scalar.activation(pi, pi, ACT.Copy, scale=rrec[:, u, i:i + 1])
                    last.then_inc(p_rdy, 1)
                if l == 0:
                    for t in range(NT):
                        ps = take(("rT", t))
                        nc.scalar.copy(rqkT[:, :, t * P:(t + 1) * P], ps[:, 0:512].rearrange("p (c n) -> p c n", c=4)).then_inc(outA, 1)
                    for t in range(NT):
                        ps = take(("rg", t))
                        nc.scalar.activation(gs[:, t, :], ps[:, 0:512], ACT.Silu).then_inc(outA, 1)
                        if t < NT - 1:
                            output_squares(t)
                for t in range(NT):
                    scaled(("zT", t), t, W["ln"])
                for c in range(NHC):
                    n = HSZ[c]
                    if c >= 2:
                        act.wait_ge(outD, DJ["a", c - 2] + 1)
                    ps = take(("g", c))
                    nc.scalar.activation(gl[0:n, c % 2, :], ps[0:n, 0:T], ACT.Gelu, bias=W["b1"][0:n, 1, c:c + 1]).then_inc(outA, 1)
                    if l == 0 and c == 0:
                        output_squares(NT - 1)
                for t in range(0 if l else NT):
                    ps = take(("roT", t))
                    act.wait_ge(og_rdy, NT)
                    nc.scalar.copy(roT[:, :, t * P:(t + 1) * P], ps[:, 0:512].rearrange("p (c n) -> p c n", c=4)).then_inc(outA, 1)
                if l:
                    latent_attention()
                act.sem_inc(arrive, 1)
                act.wait_ge(go["act"], 1)
                act.sem_clear(go["act"])

        @block.gpsimd
        def _(pool):
            n = [0]

            def step(ins):
                n[0] += 1
                ins.then_inc(p_const, 1)
                pool.wait_ge(p_const, n[0])

            step(nc.gpsimd.memset(ident[:], 0.0))
            step(nc.gpsimd.affine_select(out=ident[:], in_=ident[:], compare_op=ALU.not_equal, fill=1.0, base=0,
                                         pattern=[[-1, P]], channel_multiplier=1))
            step(nc.gpsimd.tensor_copy(identb[:], ident[:]))
            step(nc.gpsimd.memset(tri[:], 1.0))
            step(nc.gpsimd.affine_select(out=tri[:], in_=tri[:], compare_op=ALU.is_ge, fill=0.0, base=0,
                                         pattern=[[1, P]], channel_multiplier=-1))
            step(nc.gpsimd.memset(maskw[:], 0.0))
            step(nc.gpsimd.affine_select(out=maskw[:, 0, :], in_=maskw[:, 0, :], compare_op=ALU.is_ge, fill=-1e30, base=0,
                                         pattern=[[1, P]], channel_multiplier=-1))
            step(nc.gpsimd.affine_select(out=maskw[:, 1, :], in_=maskw[:, 1, :], compare_op=ALU.is_ge, fill=-1e30, base=0,
                                         pattern=[[-1, P]], channel_multiplier=1))
            step(nc.gpsimd.memset(half[:], -0.5))
            if l:
                for e in range(E):
                    step(nc.gpsimd.memset(iota8[:, :, e:e + 1], float(E - e)))
                    step(nc.gpsimd.memset(region[:, :, e:e + 1], float(e * REG)))
                step(nc.gpsimd.memset(Kpad, 0.0))
                step(nc.gpsimd.memset(ones[:], 1.0))
                step(nc.gpsimd.memset(zrows[:], 0.0))
                step(nc.gpsimd.memset(counts[:], 0.0))
                step(nc.gpsimd.affine_select(out=before[:], in_=ones[:], compare_op=ALU.is_ge, fill=0.0, base=-1,
                                             pattern=[[1, P]], channel_multiplier=-1))
                step(nc.gpsimd.memset(Vaug[:], 0.0))
                step(nc.gpsimd.memset(Vaug[:, :, :, LDH:LDH + 1], 1.0))
            nc.gpsimd.memset(curT[:, :, 0:1], 0.0).then_inc(const_p, 1)

            def reciprocal_roots():
                return nc.gpsimd.tensor_tensor(rs[:], ve[:], half[:, 0:NT], ALU.pow)

            def norm_scale(k):
                pool.wait_ge(var_rdy, k + 1)
                reciprocal_roots().then_inc(rstd, 1)

            if l == 0:
                pool.wait_ge(var_first, 2 * NT + 1)
                reciprocal_roots().then_inc(rstd_first, 1)
            with pool.Fori(0, B) as b:
                for t in range(NT):
                    if l == 0 and t == 1:
                        norm_scale(0)
                    pool.wait_ge(ssq_rdy, t + 1)
                    nc.gpsimd.tensor_tensor(rinv[:, t, :], ssq[:, t, :], half[:], ALU.pow)
                    nc.gpsimd.tensor_tensor(qk[:, t, :], qk[:, t, :], rot[:, t % 2, :], ALU.add).then_inc(rinv_rdy, 1)
                if l == 0:
                    for t in range(NT):
                        pool.wait_ge(outD, DJ["rqk", t] + 1)
                        nc.gpsimd.tensor_tensor(rqk[:, t, :], rqk[:, t, :], rot[:, t % 2, 0:512], ALU.add).then_inc(rqk_rdy, 1)
                    for t in range(NT):
                        pool.wait_ge(rss_rdy, t + 1)
                        nc.gpsimd.tensor_tensor(rrs[:, t, :], rss[:, t, :], half[:, 0:4], ALU.pow).then_inc(rrs_rdy, 1)
                        if t == 0:
                            norm_scale(1)
                    norm_scale(2)
                if l:
                    norm_scale(0)
                    norm_scale(1)
                    for g in range(LG):
                        pool.wait_ge(outD, DJ["lq", g] + 1)
                        nc.gpsimd.tensor_tensor(QT[:, g, :], rm1[:, g % 2, :], rm2[:, g % 2, :], ALU.add).then_inc(lq_rdy, 1)
                    for h in range(LH):
                        pool.wait_ge(lexp, h + 1)
                        ph = Pl[:, (h // 4) % 2, h % 4, :]
                        nc.gpsimd.tensor_tensor(ph[:, 0:P], ph[:, 0:P], tri[:], ALU.mult)
                        nc.gpsimd.tensor_tensor(ph[:, 512:640], ph[:, 512:640], tri[:], ALU.mult)
                        pair = ph[:, 896:1152].rearrange("p (a n) -> p a n", a=2)
                        nc.gpsimd.tensor_tensor(pair, pair, tri[:].unsqueeze(1).broadcast_to((P, 2, P)), ALU.mult).then_inc(masked, 1)
                        if h % 4 == 3 and h // 4 >= 2:
                            pool.wait_ge(rows_rdy, 1)
                            k = h // 4 - 2
                            for t in range(NT):
                                nc.gpsimd.indirect_dma_start(out=S["rows"], out_offset=bass.IndirectOffsetOnAxis(ap=rows_i[:, k * NT + t:k * NT + t + 1], axis=0),
                                                             in_=xn[:, t, :], in_offset=None).then_inc(scattered, 16)
                    pool.wait_ge(masked, LH)
                    pool.wait_ge(scattered, b * (16 * TOPK * NT) + 16 * TOPK * NT)
                else:
                    pool.wait_ge(rstd, 3)
                pool.sem_inc(arrive, 1)
                pool.wait_ge(go["pool"], 1)
                pool.sem_clear(go["pool"])

        @block.vector
        def _(dve):
            nd, ns, nln = [0], [0], [0]

            def take(name):
                k = DJ[name]
                assert k == nd[0], (name, k, nd[0])
                nd[0] += 1
                dve.wait_ge(mmD, k + 1)
                return pD[:, colsD[k]]

            def step(ins):
                ns[0] += 1
                ins.then_inc(v_step, 1)
                dve.wait_ge(v_step, ns[0])

            def heads(ap, h):
                return ap.rearrange("p (h d) -> p h d", h=h)

            def per_head(ap, n):
                return ap.unsqueeze(2).broadcast_to((P, ap.shape[1], n))

            def ln_stats(t, parts):
                for i, ap in enumerate(parts):
                    last = nc.vector.bn_stats(stat[:, t, i, :], ap)
                step(last)
                step(nc.vector.bn_aggr(mv[:, t, :], stat[:, t, 0:len(parts), :]))

            def ln_variances():
                nc.vector.tensor_scalar(ve[:], mv[:, :, 1], EPS, None, ALU.add).then_inc(var_rdy, 1)

            def ln_apply(t, parts, out):
                for i, ap in enumerate(parts):
                    n = D // len(parts)
                    last = nc.vector.tensor_scalar(out[:, t, i * n:(i + 1) * n], ap, mv[:, t, 0:1], rs[:, t:t + 1], ALU.subtract, ALU.mult)
                last.then_inc(norm, 1)

            wide = lambda ap: ap.unsqueeze(2).broadcast_to((P, NT, E))

            def router_logits():
                ps = take(("rt",))
                lg = ps[:, 0:NT * E].rearrange("p (t e) -> p t e", t=NT)
                step(nc.vector.tensor_reduce(rt1[:, 0], lg, AX.X, ALU.max))
                nc.vector.tensor_tensor(rt[:, 0], lg, wide(rt1[:, 0]), ALU.subtract).then_inc(outD, 1)

            def router_probabilities():
                dve.wait_ge(a_step, 1)
                step(nc.vector.tensor_reduce(rt1[:, 1], rt[:, 1], AX.X, ALU.add))
                step(nc.vector.reciprocal(rt1[:, 2], rt1[:, 1]))
                step(nc.vector.tensor_tensor(rt[:, 2], rt[:, 1], wide(rt1[:, 2]), ALU.mult))

            def router_pick(k):
                best = rt1[:, 3 + k]
                step(nc.vector.tensor_reduce(best, rt[:, 2], AX.X, ALU.max))
                step(nc.vector.tensor_tensor(rt[:, 3], rt[:, 2], wide(best), ALU.is_equal))
                step(nc.vector.tensor_tensor(rt[:, 4], rt[:, 3], iota8[:], ALU.mult))
                step(nc.vector.tensor_reduce(rt1[:, 5], rt[:, 4], AX.X, ALU.max))
                step(nc.vector.tensor_tensor(rt[:, 5 + k], iota8[:], wide(rt1[:, 5]), ALU.is_equal))
                if k == 0:
                    step(nc.vector.scalar_tensor_tensor(out=rt[:, 2], in0=rt[:, 5], scalar=-4.0, in1=rt[:, 2], op0=ALU.mult, op1=ALU.add))
                else:
                    nc.vector.tensor_tensor(rt[:, 3], rt[:, 5], rt[:, 6], ALU.add).then_inc(chosen, 1)

            def router_weights():
                step(nc.vector.tensor_tensor(rt1[:, 6], rt1[:, 3], rt1[:, 4], ALU.add))
                step(nc.vector.reciprocal(rt1[:, 7], rt1[:, 6]))
                step(nc.vector.tensor_tensor(route[:, 2:4, :], rt1[:, 3:5], rt1[:, 7:8].broadcast_to((P, 2, NT)), ALU.mult))

            def router_ranks():
                ps = take(("rank",))
                rank = ps[:, 0:NT * E].rearrange("p (t e) -> p t e", t=NT)
                total = ps[:, NT * E:2 * NT * E].rearrange("p (t e) -> p t e", t=NT)
                for t in range(NT):
                    step(nc.vector.tensor_tensor(counts[:, t + 1], total[:, t], counts[:, t], ALU.add))
                nc.vector.tensor_tensor(rt[:, 1], rank, counts[:, 0:NT], ALU.add).then_inc(outD, 1)
                dve.wait_ge(outD, DJ["rank",] + 1)

            def router_rows():
                step(nc.vector.tensor_tensor(rt[:, 2], rt[:, 1], region[:], ALU.add))
                for k in range(TOPK):
                    step(nc.vector.tensor_tensor(rt[:, 4], rt[:, 2], rt[:, 5 + k], ALU.mult))
                    step(nc.vector.tensor_reduce(route[:, k, :], rt[:, 4], AX.X, ALU.add))
                nc.vector.tensor_copy(rows_i[:], route[:, 0:2, :].rearrange("p k t -> p (k t)")).then_inc(rows_rdy, 1)
                step(nc.vector.tensor_copy(counts[:, 0], counts[:, NT]))
                step(nc.vector.tensor_copy(counts_i[:], counts[:, 0]))

            def gated_sum(t):
                if t == 0:
                    dve.wait_ge(x_in, 32)
                dve.wait_ge(fin_silu, t + 1)
                step(nc.vector.tensor_tensor(z[:, t, :], z[:, t, :], s_tm[:, t, :], ALU.mult))
                nc.vector.tensor_tensor(x_tm[:, t, :], x_tm[:, t, :], z[:, t, :], ALU.add).then_inc(x1_rdy, 1)
                dve.wait_ge(x1_rdy, t + 1)
                ln_stats(t, [x_tm[:, t, :]])

            def latent_attention():
                gated_sum(NT - 1)
                ln_variances()
                dve.wait_ge(rstd, 2)
                for t in range(NT):
                    ln_apply(t, [x_tm[:, t, :]], xn)

                ps = take(("lat",))
                nc.vector.tensor_copy(latT[0:LAT], ps[0:LAT, :].rearrange("p (a n) -> p a n", a=2)).then_inc(outD, 1)
                ps = take(("kr",))
                nc.vector.tensor_tensor(rm1[:, 0, :], ps[:, 0:T], W["lcos"][:], ALU.mult)
                nc.vector.tensor_tensor(rm2[:, 0, :], ps[:, T:2 * T], W["lsin"][:], ALU.mult).then_inc(outD, 1)
                dve.wait_ge(outD, DJ["kr",] + 1)
                step(nc.vector.tensor_tensor(KrT, rm1[:, 0, :], rm2[:, 0, :], ALU.add))
                router_logits()
                for g in range(LG):
                    ps = take(("kc", g))
                    nc.vector.tensor_tensor(KT[:, g, :], ps[:, 0:T], KrT, ALU.add).then_inc(outD, 1)
                for g in range(LG):
                    ps = take(("lq", g))
                    if g >= 2:
                        dve.wait_ge(lq_rdy, g - 1)
                    nc.vector.tensor_tensor(rm1[:, g % 2, :], ps[:, 0:T], W["lcos"][:], ALU.mult)
                    nc.vector.tensor_tensor(rm2[:, g % 2, :], ps[:, T:2 * T], W["lsin"][:], ALU.mult).then_inc(outD, 1)
                for h in range(LH):
                    g, i = h // 4, h % 4
                    if g >= 2 and i == 0:
                        dve.wait_ge(mmA, AJ["av", g - 2] + 1)
                    if h == 4:
                        dve.wait_ge(lq_rdy, LG)
                    ph = Pl[:, g % 2]
                    ps = take(("sa", h))
                    nc.vector.tensor_scalar(ph[:, i, 0:512], ps, 80.0, -80.0, ALU.min, ALU.max).then_inc(outD, 1)
                    ps = take(("sb", h))
                    nc.vector.tensor_scalar(ph[:, i, 512:1024], ps, 80.0, -80.0, ALU.min, ALU.max).then_inc(outD, 1)
                    ps = take(("sc", h))
                    nc.vector.tensor_scalar(ph[:, i, 1024:1280], ps[:, 0:256], 80.0, -80.0, ALU.min, ALU.max).then_inc(outD, 1)
                    if h == 1:
                        router_probabilities()
                    elif h in (2, 4):
                        router_pick((h - 2) // 2)
                    elif h == 6:
                        router_weights()
                    elif h == 7:
                        router_ranks()
                    elif h == 9:
                        router_rows()
                    if i == 3 and g >= 2:
                        by_token(g - 2)
                by_token(LG - 2)
                by_token(LG - 1)
                for t in range(NT):
                    ps = take(("lo", t))
                    nc.vector.tensor_copy(s2[:, t, :], ps[:, 0:D]).then_inc(outD, 1)

            def by_token(g):
                ps = take(("aTM", g))
                pv = ps.rearrange("p (t h d) -> p t h d", t=NT, h=4)
                rg = rd[:, :, 4 * g:4 * g + 4]
                step(nc.vector.reciprocal(rg, pv[:, :, :, LDH]))
                nc.vector.tensor_tensor(attn[:, :, 4 * g * LDH:4 * (g + 1) * LDH].rearrange("p t (h d) -> p t h d", h=4), pv[:, :, :, 0:LDH],
                                        rg.unsqueeze(3).broadcast_to((P, NT, 4, LDH)), ALU.mult).then_inc(outD, 1)

            dve.wait_ge(loaded, 16 * len(names) + 16)
            dve.wait_ge(const_p, 1)
            for t in range(NT):
                nc.vector.tensor_tensor(Ct[:, t], W["fC"][:, t], W["qks"][:, 0], ALU.mult)
                last = nc.vector.tensor_tensor(St[:, t], W["fS"][:, t], W["qks"][:, 1], ALU.mult)
            if l == 0:
                last = nc.vector.tensor_scalar(W["rWo"][:], W["rWo"][:], W["rgn"][:, 0:1], None, ALU.mult)
            last.then_inc(const_v, 1)
            dve.wait_ge(const_v, 1)

            stream = cin if l else xn
            if l == 0:
                for t in range(NT):
                    nc.vector.bn_stats(stat[:, t, 0, :], x_tm[:, t, :]).then_inc(var_first, 1)
                    dve.wait_ge(var_first, 2 * t + 1)
                    nc.vector.bn_aggr(mv[:, t, :], stat[:, t, 0:1, :]).then_inc(var_first, 1)
                    dve.wait_ge(var_first, 2 * t + 2)
                nc.vector.tensor_scalar(ve[:], mv[:, :, 1], EPS, None, ALU.add).then_inc(var_first, 1)
                dve.wait_ge(rstd_first, 1)

            with dve.Fori(0, B):
                for t in range(0 if l else NT):
                    ln_apply(t, [x_tm[:, t, :]], xn)

                def scale_qk(t):
                    dve.wait_ge(rinv_rdy, t + 1)
                    nc.vector.tensor_tensor(heads(qk[:, t, :], 16), heads(qk[:, t, :], 16), per_head(rinv[:, t, :], DH), ALU.mult).then_inc(qk_rdy, 1)

                for t in range(NT):
                    ps = take(("qk", t))
                    pv = ps[:].rearrange("p (a h d) -> p a h d", a=2, h=8)
                    o1 = qk[:, t, :].rearrange("p (a h d) -> p a h d", a=2, h=8)
                    o2 = rot[:, t % 2, :].rearrange("p (a h d) -> p a h d", a=2, h=8)
                    if t >= 2:
                        dve.wait_ge(rinv_rdy, t - 1)
                    dve.wait_ge(squares, t + 1)
                    nc.vector.tensor_tensor(o1, pv, Ct[:, t].unsqueeze(2).broadcast_to((P, 2, 8, DH)), ALU.mult)
                    for s in range(2):
                        a, b = slice(32 * s, 32 * s + 32), slice(32 * (1 - s), 32 * (1 - s) + 32)
                        nc.vector.tensor_tensor(o2[:, :, :, a], pv[:, :, :, b], St[:, t, :, a].unsqueeze(2).broadcast_to((P, 2, 8, 32)), ALU.mult)
                    nc.vector.tensor_reduce(ssq[:, t, :], heads(sq[:, t % 2, :], 16), AX.X, ALU.add).then_inc(outD, 1)
                    dve.wait_ge(outD, DJ["qk", t] + 1)
                    nc.vector.tensor_scalar(ssq[:, t, :], ssq[:, t, :], 1e-24, None, ALU.max).then_inc(ssq_rdy, 1)
                    if t:
                        scale_qk(t - 1)
                    if l == 0 and t == 0:
                        dve.wait_ge(norm, NT)
                        for i in range(NT):
                            ln_stats(i, [xn[:, i, :]])
                        ln_variances()
                    if l == 0 and t == 1:
                        dve.wait_ge(rstd, 1)
                        for i in range(NT):
                            ln_apply(i, [xn[:, i, :]], z)
                scale_qk(NT - 1)
                dve.wait_ge(loaded_rest, 16 * len(others))
                if l == 0:
                    for t in range(NT):
                        ps = take(("rqk", t))
                        pv = ps[:, 0:512].rearrange("p (h a d) -> p h a d", h=8, a=2)
                        o1 = rqk[:, t, :].rearrange("p (h a d) -> p h a d", h=8, a=2)
                        o2 = rot[:, t % 2, 0:512].rearrange("p (h a d) -> p h a d", h=8, a=2)
                        if t >= 2:
                            dve.wait_ge(rqk_rdy, t - 1)
                        elif t == 0:
                            dve.wait_ge(rinv_rdy, NT)
                        nc.vector.tensor_tensor(o1, pv, W["rC"][:, t].unsqueeze(2).broadcast_to((P, 8, 2, 32)), ALU.mult)
                        nc.vector.tensor_tensor(o2[:, :, 0, :], pv[:, :, 1, :], W["rS"][:, t, :, 0, :], ALU.mult)
                        nc.vector.tensor_tensor(o2[:, :, 1, :], pv[:, :, 0, :], W["rS"][:, t, :, 1, :], ALU.mult).then_inc(outD, 1)

                for u in range(2 * NT + 3):
                    if u < 2 * NT:
                        dve.wait_ge(mmA, AJ["S", u] + 1)
                        lo = 0 if u // 2 else P
                        nc.vector.tensor_reduce(mx[:, u, :], heads(pA[:, colsA[AJ["S", u]]], 4)[:, :, lo:256], AX.X, ALU.max, negate=True).then_inc(mx_rdy, 1)
                    if 2 <= u < 2 * NT + 2:
                        w = u - 2
                        k = 0 if w // 2 else 1
                        ps = take(("PT", w))
                        if l == 0 and w == 1:
                            dve.wait_ge(rqk_rdy, NT)
                        if w >= 2:
                            dve.wait_ge(mmD, DJ["O", w - 2] + 1)
                        nc.vector.tensor_copy(PT[w % 2].rearrange("p (h k q) -> p h k q", h=4, k=2)[:, :, k:2, :],
                                              ps.rearrange("p (h k q) -> p h k q", h=4, k=2)[:, :, k:2, :]).then_inc(outD, 1)
                    if u < 2 * NT:
                        dve.wait_ge(outA, AJ["S", u] + 1)
                        nc.vector.reciprocal(rrec[:, u, :], rsum[:, u, :]).then_inc(rrec_rdy, 1)
                    if u >= 3:
                        w = u - 3
                        t, hh = w // 2, w % 2
                        ps = take(("O", w))
                        nc.vector.tensor_copy(oT[:, 2 * hh:2 * hh + 2, t * P:(t + 1) * P], ps[:, 0:256].rearrange("p (c n) -> p c n", c=2)).then_inc(outD, 1)

                parts = lambda t: [cur[:, t, 0:P], hB[:, t, :]]

                def layer_norm_stats(first=0):
                    for t in range(first, NT):
                        dve.wait_ge(shifted[t], 32)
                        ln_stats(t, parts(t))
                    ln_variances()

                def layer_norm_apply():
                    dve.wait_ge(rstd, 1 if l else 2)
                    for t in range(NT):
                        ln_apply(t, parts(t), z)
                for t in range(NT):
                    ps = take(("wo", t))
                    nc.vector.tensor_tensor(cur[:, t, :], ps[:, 0:D], stream[:, t, :], ALU.add).then_inc(outD, 1)
                    if l and t >= 2:
                        dve.wait_ge(shifted[t - 2], 32)
                        ln_stats(t - 2, parts(t - 2))
                if l:
                    layer_norm_stats(2)
                    layer_norm_apply()
                if l == 0:
                    def mean_squares(t):
                        dve.wait_ge(osq_rdy, t + 1)
                        step(nc.vector.tensor_reduce(rss[:, t, :], heads(osq[:, t % 2, :], 4), AX.X, ALU.add))
                        nc.vector.tensor_scalar(rss[:, t, :], rss[:, t, :], 1.0 / RDV, EPS, ALU.mult, ALU.add).then_inc(rss_rdy, 1)

                    def gate(t):
                        dve.wait_ge(rrs_rdy, t + 1)
                        dve.wait_ge(outA, AJ["rg", t] + 1)
                        o = heads(rqk[:, t, :], 4)
                        step(nc.vector.tensor_tensor(o, heads(o_sb[:, t % 2, :], 4), per_head(rrs[:, t, :], RDV), ALU.mult))
                        nc.vector.tensor_tensor(rqk[:, t, :], rqk[:, t, :], gs[:, t, :], ALU.mult).then_inc(og_rdy, 1)
                    for t in range(NT):
                        ps = take(("AT", t))
                        nc.vector.tensor_tensor(AT[:, t % 2, :].rearrange("p (b a n) -> p b a n", b=2, a=2),
                                                ps[:].rearrange("p (b n) -> p b n", b=2)[:, :, 0:2 * P].rearrange("p b (a n) -> p b a n", a=2),
                                                tri[:].unsqueeze(1).unsqueeze(1).broadcast_to((P, 2, 2, P)), ALU.mult).then_inc(outD, 1)
                        if t < NT - 1:
                            ps = take(("st", t))
                            pv = ps[:, 0:256].rearrange("p (a n) -> p a n", a=2)
                            if t == 0:
                                nc.vector.tensor_copy(rst[:, 1], pv).then_inc(outD, 1)
                            else:
                                nc.vector.tensor_tensor(rst[:, t + 1], pv, rst[:, t], ALU.add).then_inc(outD, 1)
                        if t == 2:
                            layer_norm_stats()
                        if t == 3:
                            layer_norm_apply()
                        if t >= 1:
                            mean_squares(t - 1)
                        if t >= 2:
                            gate(t - 2)
                        ps = take(("ro", t))
                        if t >= 2:
                            dve.wait_ge(og_rdy, t - 1)
                        nc.vector.tensor_copy(o_sb[:, t % 2, :].rearrange("p (a b n) -> p b a n", a=2, b=2),
                                              ps[:].rearrange("p (b n) -> p b n", b=2)[:, :, 0:2 * P].rearrange("p b (a n) -> p b a n", a=2)).then_inc(outD, 1)

                step(nc.vector.memset(hT[64:HCH, NHC - 1, :], 1.0))
                for c in range(NHC):
                    n = HSZ[c]
                    ps = take(("a", c))
                    dve.wait_ge(outA, AJ["g", c] + 1)
                    nc.vector.scalar_tensor_tensor(out=hT[0:n, c, :], in0=ps[0:n, 0:T], scalar=W["b1"][0:n, 0, c:c + 1], in1=gl[0:n, c % 2, :],
                                                   op0=ALU.add, op1=ALU.mult).then_inc(outD, 1)
                    if l == 0 and c == 0:
                        gate(NT - 2)
                    if l == 0 and c == 1:
                        mean_squares(NT - 1)
                    if l == 0 and c == 3:
                        gate(NT - 1)
                for t in range(NT):
                    ps = take(("w2", t))
                    nc.vector.tensor_tensor(cur[:, t, :], ps[:, 0:D], cur[:, t, :], ALU.add).then_inc(outD, 1)
                    if l and t:
                        gated_sum(t - 1)
                    if l == 0 and t == 1:
                        dve.wait_ge(next_in, 16)
                        for i in range(NT):
                            ln_stats(i, [x_tm[:, i, :]])
                        ln_variances()
                if l == 0:
                    for t in range(NT):
                        ps = take(("rout", t))
                        nc.vector.tensor_tensor(s_tm[:, t, :], ps[:, 0:D], xn[:, t, :], ALU.add).then_inc(outD, 1)
                if l:
                    latent_attention()
                dve.sem_inc(arrive, 1)
                dve.wait_ge(go["dve"], 1)
                dve.sem_clear(go["dve"])


def block_moe(nc, I, S):
    ctx = ExitStack()
    with ctx:
        def sb(name, shape, dt=F32):
            return ctx.enter_context(nc.sbuf_tensor("m_" + name, shape, dt))

        def sem(name):
            return ctx.enter_context(nc.semaphore("m_" + name))
        w1 = sb("w1", [P, E, DC, F])
        w2 = sb("w2", [P, E, FC, D])
        ident = sb("ident", [P, P])
        xin = sb("xin", [P, UNROLL, D])
        xT = sb("xT", [P, 2, DC, P])
        h = sb("h", [P, 2, F])
        hT = sb("hT", [P, 2, F])
        y = sb("y", [P, 2, D])
        cnt = sb("cnt", [P, E])
        k128 = sb("k128", [P, B * T // P])
        full = sb("full", [P, E, B * T // P])
        tl = sb("tl", [P, E])
        end = sb("end", [P, E + 1])
        jot = sb("jot", [P, NTILES])
        past = sb("past", [P, NTILES, E])
        tmp = sb("tmp", [P, NTILES, E])
        ex = sb("ex", [P, NTILES])
        start = sb("start", [P, NTILES])
        row = sb("row", [P, 2, NTILES])
        ex_i = sb("ex_i", [P, NTILES], I32)
        row_i = sb("row_i", [P, NTILES], I32)
        shift = sb("shift", [P, 3, E])
        ph = [ctx.enter_context(nc.psum_tensor(f"m_ph{i}", [P, F], F32)) for i in range(2)]
        pt = ctx.enter_context(nc.psum_tensor("m_pt", [P, F], F32))
        px = ctx.enter_context(nc.psum_tensor("m_px", [P, 512], F32))
        py = ctx.enter_context(nc.psum_tensor("m_py", [P, 512], F32))
        wl = [sem(f"wl{e}") for e in range(E)]
        ready = sem("ready")
        cl = sem("cl")
        const = sem("const")
        p_const = sem("p_const")
        v_step = sem("v_step")
        table = sem("table")
        t_out = sem("t_out")
        per_loop = []

        def bsem(name):
            s = sem(name)
            per_loop.append(s)
            return s
        xl = [bsem(f"xl{u}") for u in range(UNROLL)]
        seen = bsem("seen")
        xt = bsem("xt")
        xtc = bsem("xtc")
        up = bsem("up")
        gel = bsem("gel")
        tr = bsem("tr")
        trc = bsem("trc")
        dn = bsem("dn")
        yc = bsem("yc")
        st = [bsem(f"st{i}") for i in range(2)]
        arrive = bsem("arrive")
        go = {e: sem("go_" + e) for e in ("pe", "act", "dve")}
        block = ctx.enter_context(nc.Block())
        NK = B * T // P

        @block.gpsimd
        def _(pool):
            n = [0]

            def step(ins):
                n[0] += 1
                ins.then_inc(p_const, 1)
                pool.wait_ge(p_const, n[0])
            step(nc.gpsimd.memset(ident[:], 0.0))
            step(nc.gpsimd.affine_select(out=ident[:], in_=ident[:], compare_op=ALU.not_equal, fill=1.0, base=0,
                                         pattern=[[-1, P]], channel_multiplier=1))
            step(nc.gpsimd.iota(k128[:], [[P, NK]], base=0, channel_multiplier=0, allow_small_or_imprecise_dtypes=True))
            step(nc.gpsimd.iota(shift[:, 1], [[REG, E]], base=0, channel_multiplier=0, allow_small_or_imprecise_dtypes=True))
            nc.gpsimd.iota(jot[:], [[1, NTILES]], base=0, channel_multiplier=0, allow_small_or_imprecise_dtypes=True).then_inc(const, 1)
            for e in range(E):
                pool.wait_ge(wl[e], 32)
                pool.sem_inc(ready, 1)

        @block.sync
        def _(sp):
            sp.dma_start(cnt[:], S["count"]).then_inc(cl, 16)
            sp.dma_start(w1[:, 0], I["m_w1"][0]).then_inc(wl[0], 16)
            sp.dma_start(w2[:, 0], I["m_w2"][0]).then_inc(wl[0], 16)
            sp.wait_ge(table, 1)
            sp.dma_start(S["tile"], shift[:]).then_inc(t_out, 16)
            with sp.Fori(0, NTILES // UNROLL) as it:
                for u in range(UNROLL):
                    r = sp.value_load(row_i[0:1, bass.ds(it * UNROLL + u, 1)], min_val=0, max_val=E * REG)
                    sp.dma_start(xin[:, u, :], S["rows"][bass.ds(r, P), :]).then_inc(xl[u], 16)
                for u in range(UNROLL):
                    sp.wait_ge(yc, u + 1)
                    sp.dma_start(S["y"][bass.ds((it * UNROLL + u) * P, P), :], y[:, u % 2, :]).then_inc(st[u % 2], 16)
                for i in range(2):
                    sp.wait_ge(st[i], 16 * UNROLL // 2)
                sp.wait_ge(arrive, 3)
                for s in per_loop:
                    sp.sem_clear(s)
                for g in go.values():
                    sp.sem_inc(g, 1)
            sp.wait_ge(t_out, 16)

        @block.tensor
        def _(pe):
            pe.wait_ge(const, 1)
            pe.wait_ge(table, 1)
            with pe.Fori(0, NTILES // UNROLL) as it:
                e = [None] * UNROLL

                def transpose_x(u):
                    pe.wait_ge(xl[u], 16)
                    if u >= 1:
                        pe.wait_ge(xtc, u)
                    for c in range(DC):
                        last = nc.tensor.transpose(px[:, c * P:(c + 1) * P], xin[:, u, c * P:(c + 1) * P], ident[:])
                    last.then_inc(xt, 1)
                transpose_x(0)
                for u in range(UNROLL + 2):
                    if u < UNROLL:
                        e[u] = pe.value_load(ex_i[0:1, bass.ds(it * UNROLL + u, 1)], min_val=0, max_val=E - 1)
                        pe.wait_ge(ready, e[u] + 1)
                        pe.sem_inc(seen, 1)
                        pe.wait_ge(xtc, u + 1)
                        if u >= 2:
                            pe.wait_ge(gel, u - 1)
                        for c in range(DC):
                            for n in range(2):
                                last = nc.tensor.matmul(ph[u % 2][:, n * 512:(n + 1) * 512], xT[:, u % 2, c, :],
                                                        w1[:, bass.ds(e[u], 1), c, n * 512:(n + 1) * 512],
                                                        start=(c == 0), stop=(c == DC - 1))
                        last.then_inc(up, 1)
                    if u + 1 < UNROLL:
                        transpose_x(u + 1)
                    if 1 <= u <= UNROLL:
                        w = u - 1
                        pe.wait_ge(gel, w + 1)
                        if w >= 1:
                            pe.wait_ge(trc, w)
                        for c in range(FC):
                            last = nc.tensor.transpose(pt[:, c * P:(c + 1) * P], h[:, w % 2, c * P:(c + 1) * P], ident[:])
                        last.then_inc(tr, 1)
                    if u >= 2:
                        w = u - 2
                        pe.wait_ge(trc, w + 1)
                        if w >= 1:
                            pe.wait_ge(yc, w)
                        for c in range(FC):
                            last = nc.tensor.matmul(py[:, 0:D], hT[:, w % 2, c * P:(c + 1) * P], w2[:, bass.ds(e[w], 1), c, :],
                                                    start=(c == 0), stop=(c == FC - 1))
                        last.then_inc(dn, 1)
                pe.sem_inc(arrive, 1)
                pe.wait_ge(go["pe"], 1)
                pe.sem_clear(go["pe"])

        @block.scalar
        def _(act):
            for u in range(UNROLL):
                act.wait_ge(xl[u], 16)
            for e in range(1, E):
                act.dma_start(w1[:, e], I["m_w1"][e]).then_inc(wl[e], 16)
                act.dma_start(w2[:, e], I["m_w2"][e]).then_inc(wl[e], 16)
            with act.Fori(0, NTILES // UNROLL):
                for u in range(UNROLL + 2):
                    if u < UNROLL:
                        act.wait_ge(up, u + 1)
                        if u >= 2:
                            act.wait_ge(tr, u - 1)
                        nc.scalar.activation(h[:, u % 2, :], ph[u % 2][:], ACT.Gelu).then_inc(gel, 1)
                    if u >= 2:
                        w = u - 2
                        act.wait_ge(dn, w + 1)
                        if w >= 2:
                            act.wait_ge(st[w % 2], 16 * (w // 2))
                        nc.scalar.copy(y[:, w % 2, :], py[:, 0:D]).then_inc(yc, 1)
                act.wait_ge(yc, UNROLL)
                act.sem_inc(arrive, 1)
                act.wait_ge(go["act"], 1)
                act.sem_clear(go["act"])

        @block.vector
        def _(dve):
            n = [0]

            def step(ins):
                n[0] += 1
                ins.then_inc(v_step, 1)
                dve.wait_ge(v_step, n[0])
            by_expert = lambda ap: ap.unsqueeze(1).broadcast_to((P, NTILES, E))
            dve.wait_ge(const, 1)
            dve.wait_ge(cl, 16)
            step(nc.vector.tensor_tensor(full[:], cnt[:].unsqueeze(2).broadcast_to((P, E, NK)), k128[:].unsqueeze(1).broadcast_to((P, E, NK)), ALU.is_gt))
            step(nc.vector.tensor_reduce(tl[:], full[:], AX.X, ALU.add))
            step(nc.vector.memset(end[:, 0:1], 0.0))
            for e in range(E):
                step(nc.vector.tensor_tensor(end[:, e + 1:e + 2], end[:, e:e + 1], tl[:, e:e + 1], ALU.add))
            step(nc.vector.tensor_tensor(past[:], jot[:].unsqueeze(2).broadcast_to((P, NTILES, E)), by_expert(end[:, 1:E + 1]), ALU.is_ge))
            step(nc.vector.tensor_reduce(ex[:], past[:], AX.X, ALU.add))
            step(nc.vector.tensor_tensor(tmp[:], past[:], by_expert(tl[:]), ALU.mult))
            step(nc.vector.tensor_reduce(start[:], tmp[:], AX.X, ALU.add))
            step(nc.vector.tensor_tensor(start[:], jot[:], start[:], ALU.subtract))
            step(nc.vector.tensor_scalar(row[:, 0], ex[:], float(REG), None, ALU.mult))
            step(nc.vector.scalar_tensor_tensor(out=row[:, 1], in0=start[:], scalar=float(P), in1=row[:, 0], op0=ALU.mult, op1=ALU.add))
            step(nc.vector.tensor_scalar(row_i[:], row[:, 1], float(E * REG), None, ALU.min))
            step(nc.vector.tensor_scalar(ex_i[:], ex[:], float(E - 1), None, ALU.min))
            step(nc.vector.tensor_scalar(shift[:, 2], end[:, 0:E], float(P), None, ALU.mult))
            nc.vector.tensor_tensor(shift[:, 0], shift[:, 2], shift[:, 1], ALU.subtract).then_inc(table, 1)
            with dve.Fori(0, NTILES // UNROLL):
                for u in range(UNROLL + 1):
                    if u < UNROLL:
                        dve.wait_ge(xt, u + 1)
                        if u >= 2:
                            dve.wait_ge(up, u - 1)
                        nc.vector.tensor_copy(xT[:, u % 2, :, :].rearrange("p c n -> p (c n)"), px[:, 0:D]).then_inc(xtc, 1)
                    if u >= 1:
                        w = u - 1
                        dve.wait_ge(tr, w + 1)
                        if w >= 2:
                            dve.wait_ge(dn, w - 1)
                        nc.vector.tensor_copy(hT[:, w % 2, :], pt[:]).then_inc(trc, 1)
                dve.wait_ge(trc, UNROLL)
                dve.sem_inc(arrive, 1)
                dve.wait_ge(go["dve"], 1)
                dve.sem_clear(go["dve"])


def block_out(nc, S, out_d):
    ctx = ExitStack()
    with ctx:
        def sb(name, shape, dt=F32):
            return ctx.enter_context(nc.sbuf_tensor("o_" + name, shape, dt))

        def sem(name):
            return ctx.enter_context(nc.semaphore("o_" + name))
        NB = 2
        yk = [sb(f"y{b}", [P, TOPK, NT, D]) for b in range(B)]
        s = [sb(f"s{i}", [P, NT, D]) for i in range(NB)]
        x = [sb(f"x{i}", [P, NT, D]) for i in range(NB)]
        gated = [sb(f"g{i}", [P, NT, D]) for i in range(NB)]
        shift = sb("shift", [P, 3, E])
        route = sb("route", [P, B, 4, NT])
        rows = sb("rows", [P, B, 2 * NT])
        over = sb("over", [P, B, 2 * NT])
        step_e = sb("step_e", [P, E])
        rows_i = sb("rows_i", [P, B, 2 * NT], I32)
        fetched = [sem(f"in{b}") for b in range(B)]
        gathered = [sem(f"gath{b}") for b in range(B)]
        tables_in = sem("tables_in")
        v_step = sem("v_step")
        rows_rdy = sem("rows_rdy")
        mixed = sem("mixed")
        gate = sem("gate")
        sums = sem("sum")
        stored = [sem(f"st{i}") for i in range(NB)]
        block = ctx.enter_context(nc.Block())
        out_v = out_d.rearrange("(b t) p c -> b p t c", t=NT)

        @block.sync
        def _(sp):
            sp.dma_start(shift[:], S["tile"]).then_inc(tables_in, 16)
            sp.dma_start(route[:], S["route"].rearrange("b p k t -> p b k t")).then_inc(tables_in, 16)
            for b in range(B + NB):
                if b >= NB:
                    sp.wait_ge(sums, b - NB + 1)
                    sp.dma_start(out_v[b - NB], x[b % NB][:]).then_inc(stored[b % NB], 16)
                if b < B:
                    if b >= NB:
                        sp.wait_ge(stored[b % NB], 16 * (b // NB))
                    sp.dma_start(s[b % NB][:], S["s2"][b]).then_inc(fetched[b], 16)
                    sp.dma_start(x[b % NB][:], S["x1"][b]).then_inc(fetched[b], 16)
            for i in range(NB):
                sp.wait_ge(stored[i], 16 * B // NB)

        @block.gpsimd
        def _(pool):
            pool.wait_ge(rows_rdy, 1)
            for b in range(B):
                for k in range(TOPK):
                    for t in range(NT):
                        nc.gpsimd.indirect_dma_start(out=yk[b][:, k, t, :], out_offset=None, in_=S["y"],
                                                     in_offset=bass.IndirectOffsetOnAxis(ap=rows_i[:, b, k * NT + t:k * NT + t + 1], axis=0))\
                            .then_inc(gathered[b], 16)

        @block.scalar
        def _(act):
            for b in range(B):
                act.wait_ge(mixed, b + 1)
                nc.scalar.activation(gated[b % NB][:], yk[b][:, 0], ACT.Silu).then_inc(gate, 1)

        @block.vector
        def _(dve):
            n = [0]

            def step(ins):
                n[0] += 1
                ins.then_inc(v_step, 1)
                dve.wait_ge(v_step, n[0])
            dve.wait_ge(tables_in, 32)
            step(nc.vector.tensor_tensor(step_e[:, 1:E], shift[:, 0, 1:E], shift[:, 0, 0:E - 1], ALU.subtract))
            step(nc.vector.tensor_scalar(rows[:], route[:, :, 0:2, :].rearrange("p b k t -> p b (k t)"), shift[:, 0, 0:1], None, ALU.add))
            for e in range(1, E):
                step(nc.vector.tensor_scalar(over[:], route[:, :, 0:2, :].rearrange("p b k t -> p b (k t)"), float(e * REG), step_e[:, e:e + 1], ALU.is_ge, ALU.mult))
                step(nc.vector.tensor_tensor(rows[:], rows[:], over[:], ALU.add))
            nc.vector.tensor_copy(rows_i[:], rows[:]).then_inc(rows_rdy, 1)

            def mix(b):
                dve.wait_ge(gathered[b], 16 * TOPK * NT)
                for t in range(NT):
                    step(nc.vector.tensor_scalar(yk[b][:, 0, t, :], yk[b][:, 0, t, :], route[:, b, 2, t:t + 1], None, ALU.mult))
                for t in range(NT):
                    last = nc.vector.scalar_tensor_tensor(out=yk[b][:, 0, t, :], in0=yk[b][:, 1, t, :], scalar=route[:, b, 3, t:t + 1], in1=yk[b][:, 0, t, :],
                                                          op0=ALU.mult, op1=ALU.add)
                last.then_inc(mixed, 1)
            mix(0)
            for b in range(B):
                if b + 1 < B:
                    mix(b + 1)
                dve.wait_ge(gate, b + 1)
                dve.wait_ge(fetched[b], 32)
                step(nc.vector.tensor_tensor(gated[b % NB][:], gated[b % NB][:], s[b % NB][:], ALU.mult))
                nc.vector.tensor_tensor(x[b % NB][:], x[b % NB][:], gated[b % NB][:], ALU.add).then_inc(sums, 1)


def tables():
    f = np.float32
    inv = 1.0 / 10000.0 ** (np.arange(0, RDK, 2, dtype=np.float64) / RDK)
    ang = (np.arange(T, dtype=f)[:, None] * inv.astype(f)).astype(np.float64)
    gamma = 1.0 - 2.0 ** (-5.0 - np.arange(RH))
    rC = np.zeros((T, 8, 32))
    rS = np.zeros((T, 8, 2, 32))
    for h in range(RH):
        dq = gamma[h] ** (np.arange(T) + 1.0)
        for u, fac in ((h, dq * RDK ** -0.5), (RH + h, 1.0 / dq)):
            rC[:, u] = np.cos(ang) * fac[:, None]
            rS[:, u, 0] = -np.sin(ang) * fac[:, None]
            rS[:, u, 1] = np.sin(ang) * fac[:, None]
    hi = np.arange(0, DH, 2, dtype=f)
    inv = (1.0 / 10000.0 ** (hi.astype(np.float64) / DH)).astype(f)
    fr = (np.arange(T, dtype=f)[:, None] * inv).astype(np.float64)
    base = (hi.astype(np.float64) + 0.4 * DH) / (1.4 * DH)
    power = (np.arange(T) - T // 2) / float(WINDOW // 2)
    sc = base[None, :] ** power[:, None]
    fC = np.zeros((T, 2, DH))
    fS = np.zeros((T, 2, DH))
    for i, s in ((0, sc * 8.0), (1, 1.0 / sc)):
        fC[:, i] = np.concatenate([np.cos(fr) * s] * 2, -1)
        fS[:, i] = np.concatenate([-np.sin(fr) * s, np.sin(fr) * s], -1)
    inv = (10000.0 ** (-np.arange(0, LDR, 2, dtype=np.float64) / LDR)).astype(f)
    an = (np.arange(T, dtype=f)[:, None] * inv).astype(np.float64)
    lc = np.zeros((32, T))
    ls = np.zeros((32, T))
    lc[0:LDH] = 1.0
    for j in range(LDR // 2):
        lc[LDH + 2 * j] = lc[LDH + 2 * j + 1] = np.cos(an[:, j])
        ls[LDH + 2 * j] = -np.sin(an[:, j])
        ls[LDH + 2 * j + 1] = np.sin(an[:, j])
    by_tile = lambda a: np.ascontiguousarray(a.reshape((NT, P) + a.shape[1:]).swapaxes(0, 1).astype(f))
    return {"w_rC": by_tile(rC), "w_rS": by_tile(rS), "w_fC": by_tile(fC), "w_fS": by_tile(fS),
            "w_lcos": np.tile(lc, (4, 1)).astype(f), "w_lsin": np.tile(ls, (4, 1)).astype(f),
            "zrow": np.zeros((1, P), f)}


def arrange(a):
    ch = lambda w: np.ascontiguousarray(w.reshape((-1, P) + w.shape[1:]).swapaxes(0, 1))
    per = lambda v: np.ascontiguousarray(v.reshape(-1, P).T)
    r = {"x": a["L0_attn_x"]}
    r["w_rWqk"] = ch(np.concatenate([a["L0_attn_Wq"], a["L0_attn_Wk"]], 1))
    r["w_rWv"] = ch(a["L0_attn_Wv"])
    r["w_rWg"] = ch(a["L0_attn_Wg"])
    r["w_rWo"] = ch(a["L0_attn_Wo"])
    r["w_rln"] = np.stack([per(a["L0_attn_ln_w"]), per(a["L0_attn_ln_b"])], 1)
    r["w_rgn"] = a["L0_attn_g_norm_w"].reshape(P, 1)
    r["w_wqkv"] = np.stack([ch(w) for w in a["L0_ffn_wqkv"]], 1)
    r["w_wo"] = np.stack([ch(w) for w in a["L0_ffn_wo"]], 1)
    r["w_ln"] = np.stack([np.stack([per(g), per(b)], 1) for g, b in zip(a["L0_ffn_ln_g"], a["L0_ffn_ln_b"])], 1)
    r["w_w1"] = np.stack([ch(w) for w in a["L0_ffn_w1"]], 1)
    b1 = np.zeros((HCH, DEPTH, 2, NHC), np.float32)
    w2 = np.zeros((HCH, DEPTH, NHC, D), np.float32)
    for l in range(DEPTH):
        for c in range(NHC):
            n = HSZ[c]
            for i in range(2):
                b1[0:n, l, i, c] = a["L0_ffn_b1"][l, i * HID + c * HCH:i * HID + c * HCH + n]
            w2[0:n, l, c] = a["L0_ffn_w2"][l, c * HCH:c * HCH + n]
        w2[HSZ[-1], l, NHC - 1] = a["L0_ffn_b2"][l]
    r["w_b1"], r["w_w2"] = b1, w2
    swap = np.concatenate([np.arange(32, 64), np.arange(0, 32)])
    qs = np.stack([np.stack([a["L0_ffn_q_scale"], a["L0_ffn_k_scale"]], 1),
                   np.stack([a["L0_ffn_q_scale"][:, swap], a["L0_ffn_k_scale"][:, swap]], 1)], 1)
    r["w_qks"] = np.broadcast_to(qs[None], (P,) + qs.shape)
    r["w_lWd"] = np.stack([ch(a["L1_attn_W_DQ"]), ch(a["L1_attn_W_DKV"])], 1)
    wq = np.zeros((LAT, 2, LG, 4, 32), np.float32)
    wk = np.zeros((LAT, LG, 4, 32), np.float32)
    wkr = np.zeros((D, 2, 4, 32), np.float32)
    partner = np.arange(LDR).reshape(-1, 2)[:, ::-1].reshape(-1)
    wq[:, 0, :, :, 0:LDH] = a["L1_attn_W_UQ"].reshape(LAT, LG, 4, LDH)
    qr = a["L1_attn_W_QR"].reshape(LAT, LG, 4, LDR)
    wq[:, 0, :, :, LDH:LDH + LDR] = qr
    wq[:, 1, :, :, LDH:LDH + LDR] = qr[..., partner]
    wk[..., 0:LDH] = a["L1_attn_W_UK"].reshape(LAT, LG, 4, LDH)
    kr = a["L1_attn_W_KR"]
    wkr[:, 0, :, LDH:LDH + LDR] = kr[:, None]
    wkr[:, 1, :, LDH:LDH + LDR] = kr[:, partner][:, None]
    r["w_lWq"] = wq.reshape(LAT, 2, LG, P)
    r["w_lWk"] = wk.reshape(LAT, LG, P)
    r["w_lWkr"] = wkr.reshape(DC, P, 2, P).transpose(1, 2, 0, 3)
    r["w_lWv"] = a["L1_attn_W_UV"]
    r["w_lWo"] = ch(a["L1_attn_W_O"])
    r["w_gw"] = ch(a["L1_ffn_gate_w"])
    r["m_w1"] = np.stack([ch(w) for w in a["L1_ffn_w1"]], 0)
    r["m_w2"] = np.stack([ch(w) for w in a["L1_ffn_w2"]], 0)
    return r


def kernel(**inputs):
    import numpy as _np
    import concourse.bacc as _bacc
    from concourse import mybir as _mybir
    from concourse.bass_utils import run_bass_kernel_spmd as _run

    nc = _bacc.Bacc("TRN2", target_bir_lowering=False, num_devices=1)
    arrays = {**arrange({k: _np.asarray(v) for k, v in inputs.items()}), **tables()}
    arrays = {k: _np.ascontiguousarray(v) for k, v in arrays.items()}
    ins = {k: nc.dram_tensor(f"in_{k}", v.shape, _mybir.dt.from_np(v.dtype), kind="ExternalInput").ap() for k, v in arrays.items()}
    out = nc.dram_tensor("out_0", (B, T, D), F32, kind="ExternalOutput").ap()
    build(nc, ins, out)
    r = _run(nc, [{f"in_{k}": v for k, v in arrays.items()}], core_ids=[0])
    return r.results[0]["out_0"]
```
